# Optimizing a Trainium2 kernel written in Bass

```python
import numpy as np
import jax
import jax.numpy as jnp

def _softmax(x, axis=-1):
    return jax.nn.softmax(x, axis=axis)

def _gelu(x):
    return jax.nn.gelu(x, approximate=True)

def _silu(x):
    return jax.nn.silu(x)

def _sigmoid(x):
    return jax.nn.sigmoid(x)

def _layernorm(x, axis=-1, eps=1e-05):
    m = jnp.mean(x, axis=axis, keepdims=True)
    v = jnp.var(x, axis=axis, keepdims=True)
    return (x - m) / jnp.sqrt(v + eps)

def _scatter_add(tgt, idx, src, axis=0):
    return tgt.at[idx].add(src)

def _segment_sum(src, seg, n):
    return jax.ops.segment_sum(src, seg, n)
kernel_name = 'mk_flamingo_gated_d2_seqx_r8_bd9925'

def setup_inputs(seed: int=0):
    np.random.seed(seed)
    _w = jnp.asarray

    def _rec_inputs():
        import jax
        import jax.numpy as jnp
        _rk = jax.random.key(seed)
        x = -0.000125 + 0.9999 * jax.random.normal(jax.random.fold_in(_rk, 1), (32, 56, 256), jnp.float32)
        _lenS = 56 - jax.random.randint(jax.random.fold_in(_rk, 7), (32,), 0, max(1, 56 // 4) + 1, jnp.int32)
        _lenS2 = 1500 - jax.random.randint(jax.random.fold_in(_rk, 8), (32,), 0, max(1, 1500 // 4) + 1, jnp.int32)
        _ctx_2048P = jax.random.normal(jax.random.fold_in(_rk, 11), (32, 16, 256), jnp.float32)
        _ctx_2048c = jax.random.dirichlet(jax.random.fold_in(_rk, 511), 0.3 * jnp.ones((16,), jnp.float32), (32, 1500))
        _ctx_2048t = jnp.einsum('bsk,bkd->bsd', _ctx_2048c, _ctx_2048P)
        _ctx_2048t = _ctx_2048t * jax.lax.rsqrt(jnp.mean(jnp.square(_ctx_2048t)) + 1e-12) * 0.953939
        ctx_2048 = -1.52775e-05 + 0.999936 * (_ctx_2048t + 0.3 * jax.random.normal(jax.random.fold_in(_rk, 611), (32, 1500, 256), jnp.float32))
        _g = jax.random.normal(jax.random.fold_in(_rk, 9001), (2, 2), jnp.float32)
        _g = jnp.sign(_g) * jnp.maximum(jnp.abs(_g), 1.0) + (_g == 0) * 1.0
        g_xattn = _g[0]
        g_ffn = _g[1]
        return (x, ctx_2048, g_xattn, g_ffn)
    x, ctx_2048, g_xattn, g_ffn = _rec_inputs()

    def _L0_xattn_setup():
        import jax, jax.numpy as jnp
        import numpy as np
        EPS = 1e-06
        NUM_HEADS = 16

        def _feature_map(x):
            return jnp.where(x > 0, x + 1.0, jnp.exp(x))
        key = jax.random.key(seed)
        ks = jax.random.split(key, 7)
        B, L, S, D = (4, 512, 512, 256)
        sc = 1.0 / np.sqrt(D)
        return {'query': jax.random.normal(ks[0], (B, L, D), jnp.float32), 'kv': jax.random.normal(ks[1], (B, S, D), jnp.float32), 'Wq': jax.random.normal(ks[2], (D, D), jnp.float32) * sc, 'Wg': jax.random.normal(ks[3], (D, D), jnp.float32) * sc, 'bg': jnp.ones((D,), jnp.float32), 'Wkv': jax.random.normal(ks[4], (2 * D, D), jnp.float32) * sc, 'Wo': jax.random.normal(ks[5], (D, D), jnp.float32) * sc}
    _L0_xattn_all = _L0_xattn_setup()
    _L0_xattn_in = {k: v for k, v in _L0_xattn_all.items() if k in ('Wq', 'Wg', 'bg', 'Wkv', 'Wo')}
    del _L0_xattn_all

    def _L0_ffn_setup():
        import jax, jax.numpy as jnp
        import numpy as np
        from jax import lax
        E = 8
        K = 2
        H = 256
        I = 512
        B, S = (2, 256)
        SCALE = 0.02

        def _silu_and_mul(gu):
            g, u = jnp.split(gu, 2, axis=-1)
            return jax.nn.silu(g) * u
        key = jax.random.key(seed)
        ks = jax.random.split(key, 6)
        return {'hidden_states': jax.random.normal(ks[0], (B, S, H), dtype=jnp.float32), 'gate_w': jax.random.normal(ks[1], (H, E), dtype=jnp.float32) * SCALE, 'w_gate_up': jax.random.normal(ks[2], (E, H, 2 * I), dtype=jnp.float32) * SCALE, 'w_down': jax.random.normal(ks[3], (E, I, H), dtype=jnp.float32) * SCALE, 'shared_gate_up': jax.random.normal(ks[4], (H, 2 * I), dtype=jnp.float32) * SCALE, 'shared_down': jax.random.normal(ks[5], (I, H), dtype=jnp.float32) * SCALE}
    _L0_ffn_all = _L0_ffn_setup()
    _L0_ffn_in = {k: v for k, v in _L0_ffn_all.items() if k in ('gate_w', 'w_gate_up', 'w_down', 'shared_gate_up', 'shared_down')}
    del _L0_ffn_all

    def _L1_xattn_setup():
        import jax, jax.numpy as jnp
        import numpy as np
        NUM_HEADS = 16

        def _qdq(x):
            s = jnp.maximum(jnp.max(jnp.abs(x), axis=-1, keepdims=True) / 127.0, 1e-08)
            return jnp.clip(jnp.round(x / s), -127.0, 127.0) * s
        key = jax.random.key(seed)
        ks = jax.random.split(key, 8)
        B, N, M, D = (2, 512, 64, 256)
        w_std = 0.02
        return {'x': jax.random.normal(ks[0], (B, N, D), jnp.float32), 'cond': jax.random.normal(ks[1], (B, M, D), jnp.float32), 'wq': jax.random.normal(ks[2], (D, D), jnp.float32) * w_std, 'bq': jax.random.normal(ks[3], (D,), jnp.float32) * w_std, 'wkv': jax.random.normal(ks[4], (2 * D, D), jnp.float32) * w_std, 'bkv': jax.random.normal(ks[5], (2 * D,), jnp.float32) * w_std, 'wp': jax.random.normal(ks[6], (D, D), jnp.float32) * w_std, 'bp': jax.random.normal(ks[7], (D,), jnp.float32) * w_std}
    _L1_xattn_all = _L1_xattn_setup()
    _L1_xattn_in = {k: v for k, v in _L1_xattn_all.items() if k in ('wq', 'bq', 'wkv', 'bkv', 'wp', 'bp')}
    del _L1_xattn_all

    def _L1_ffn_setup():
        import jax, jax.numpy as jnp
        import numpy as np
        BLOCK_SIZE = 32
        HIDDEN_SIZE = 256
        MLP_DIM = 2048
        NVFP4_LUT = jnp.array([0.0, 0.5, 1.0, 1.5, 2.0, 3.0, 4.0, 6.0, 0.0, -0.5, -1.0, -1.5, -2.0, -3.0, -4.0, -6.0], dtype=jnp.float32)

        def dequant_nvfp4(W_packed, scales, block=BLOCK_SIZE):
            N = W_packed.shape[0]
            low = W_packed & 15
            high = W_packed >> 4 & 15
            idx = jnp.stack([low, high], axis=-1).reshape(N, -1)
            vals = NVFP4_LUT[idx]
            K = vals.shape[1]
            vals = vals.reshape(N, K // block, block) * scales[:, :, None]
            return vals.reshape(N, K)
        key = jax.random.key(seed)
        ks = jax.random.split(key, 7)
        x = jax.random.normal(ks[0], (4, 32, HIDDEN_SIZE), dtype=jnp.float32)
        gate_W_packed = jax.random.randint(ks[1], (MLP_DIM, HIDDEN_SIZE // 2), 0, 32, dtype=jnp.int32)
        gate_scales = jax.random.uniform(ks[2], (MLP_DIM, HIDDEN_SIZE // BLOCK_SIZE), dtype=jnp.float32) * 0.1 + 0.001
        up_W_packed = jax.random.randint(ks[3], (MLP_DIM, HIDDEN_SIZE // 2), 0, 32, dtype=jnp.int32)
        up_scales = jax.random.uniform(ks[4], (MLP_DIM, HIDDEN_SIZE // BLOCK_SIZE), dtype=jnp.float32) * 0.1 + 0.001
        down_W_packed = jax.random.randint(ks[5], (HIDDEN_SIZE, MLP_DIM // 2), 0, 32, dtype=jnp.int32)
        down_scales = jax.random.uniform(ks[6], (HIDDEN_SIZE, MLP_DIM // BLOCK_SIZE), dtype=jnp.float32) * 0.1 + 0.001
        return {'x': x, 'gate_W_packed': gate_W_packed, 'gate_scales': gate_scales, 'up_W_packed': up_W_packed, 'up_scales': up_scales, 'down_W_packed': down_W_packed, 'down_scales': down_scales}
    _L1_ffn_all = _L1_ffn_setup()
    _L1_ffn_in = {k: v for k, v in _L1_ffn_all.items() if k in ('gate_W_packed', 'gate_scales', 'up_W_packed', 'up_scales', 'down_W_packed', 'down_scales')}
    del _L1_ffn_all
    return {'x': x, 'ctx_2048': ctx_2048, 'g_xattn': g_xattn, 'g_ffn': g_ffn, 'L0_xattn_Wq': _L0_xattn_in['Wq'], 'L0_xattn_Wg': _L0_xattn_in['Wg'], 'L0_xattn_bg': _L0_xattn_in['bg'], 'L0_xattn_Wkv': _L0_xattn_in['Wkv'], 'L0_xattn_Wo': _L0_xattn_in['Wo'], 'L0_ffn_gate_w': _L0_ffn_in['gate_w'], 'L0_ffn_w_gate_up': _L0_ffn_in['w_gate_up'], 'L0_ffn_w_down': _L0_ffn_in['w_down'], 'L0_ffn_shared_gate_up': _L0_ffn_in['shared_gate_up'], 'L0_ffn_shared_down': _L0_ffn_in['shared_down'], 'L1_xattn_wq': _L1_xattn_in['wq'], 'L1_xattn_bq': _L1_xattn_in['bq'], 'L1_xattn_wkv': _L1_xattn_in['wkv'], 'L1_xattn_bkv': _L1_xattn_in['bkv'], 'L1_xattn_wp': _L1_xattn_in['wp'], 'L1_xattn_bp': _L1_xattn_in['bp'], 'L1_ffn_gate_W_packed': _L1_ffn_in['gate_W_packed'], 'L1_ffn_gate_scales': _L1_ffn_in['gate_scales'], 'L1_ffn_up_W_packed': _L1_ffn_in['up_W_packed'], 'L1_ffn_up_scales': _L1_ffn_in['up_scales'], 'L1_ffn_down_W_packed': _L1_ffn_in['down_W_packed'], 'L1_ffn_down_scales': _L1_ffn_in['down_scales']}

def reference(x, ctx_2048, g_xattn, g_ffn, L0_xattn_Wq, L0_xattn_Wg, L0_xattn_bg, L0_xattn_Wkv, L0_xattn_Wo, L0_ffn_gate_w, L0_ffn_w_gate_up, L0_ffn_w_down, L0_ffn_shared_gate_up, L0_ffn_shared_down, L1_xattn_wq, L1_xattn_bq, L1_xattn_wkv, L1_xattn_bkv, L1_xattn_wp, L1_xattn_bp, L1_ffn_gate_W_packed, L1_ffn_gate_scales, L1_ffn_up_W_packed, L1_ffn_up_scales, L1_ffn_down_W_packed, L1_ffn_down_scales):
    import jax
    import jax.numpy as jnp

    def _L0_xattn_ref(query, kv, Wq, Wg, bg, Wkv, Wo):
        import jax, jax.numpy as jnp
        import numpy as np
        EPS = 1e-06
        NUM_HEADS = 16

        def _feature_map(x):
            return jnp.where(x > 0, x + 1.0, jnp.exp(x))
        B, L, D = query.shape
        S = kv.shape[1]
        H = NUM_HEADS
        hd = D // H
        q = query @ Wq.T
        gate = jax.nn.sigmoid(query @ Wg.T + bg)
        kvp = kv @ Wkv.T
        k, v = jnp.split(kvp, 2, axis=-1)
        q = _feature_map(q.reshape(B, L, H, hd).transpose(0, 2, 1, 3))
        k = _feature_map(k.reshape(B, S, H, hd).transpose(0, 2, 1, 3))
        v = v.reshape(B, S, H, hd).transpose(0, 2, 1, 3)
        kv_summary = jnp.einsum('bhsd,bhse->bhde', k, v)
        k_sum = k.sum(axis=-2)
        z = 1.0 / (jnp.einsum('bhld,bhd->bhl', q, k_sum)[..., None] + EPS)
        attn = jnp.einsum('bhld,bhde->bhle', q, kv_summary) * z
        attn = attn.transpose(0, 2, 1, 3).reshape(B, L, D)
        out = attn * gate @ Wo.T
        return out

    def _L0_ffn_ref(hidden_states, gate_w, w_gate_up, w_down, shared_gate_up, shared_down):
        import jax, jax.numpy as jnp
        import numpy as np
        from jax import lax
        E = 8
        K = 2
        H = 256
        I = 512
        B, S = (2, 256)
        SCALE = 0.02

        def _silu_and_mul(gu):
            g, u = jnp.split(gu, 2, axis=-1)
            return jax.nn.silu(g) * u
        orig_shape = hidden_states.shape
        x = hidden_states.reshape(-1, orig_shape[-1])
        shared_out = _silu_and_mul(x @ shared_gate_up) @ shared_down
        router_logits = x @ gate_w
        probs = jax.nn.softmax(router_logits, axis=-1)
        topk_w, topk_i = lax.top_k(probs, K)
        topk_w = topk_w / jnp.sum(topk_w, axis=-1, keepdims=True)
        combine = jnp.sum(jax.nn.one_hot(topk_i, E, dtype=x.dtype) * topk_w[..., None], axis=1)

        def body(acc, we):
            wg, wd, cw = we
            h = _silu_and_mul(x @ wg) @ wd
            return (acc + cw[:, None] * h, None)
        moe_out, _ = lax.scan(body, jnp.zeros_like(x), (w_gate_up, w_down, combine.T))
        return (moe_out + shared_out).reshape(orig_shape)

    def _L1_xattn_ref(x, cond, wq, bq, wkv, bkv, wp, bp):
        import jax, jax.numpy as jnp
        import numpy as np
        NUM_HEADS = 16

        def _qdq(x):
            s = jnp.maximum(jnp.max(jnp.abs(x), axis=-1, keepdims=True) / 127.0, 1e-08)
            return jnp.clip(jnp.round(x / s), -127.0, 127.0) * s
        B, N, C = x.shape
        M = cond.shape[1]
        H = NUM_HEADS
        Dh = C // H
        q = _qdq(x) @ _qdq(wq).T + bq
        kv = cond @ wkv.T + bkv
        k, v = jnp.split(kv, 2, axis=-1)
        q = q.reshape(B, N, H, Dh)
        k = k.reshape(B, M, H, Dh)
        v = v.reshape(B, M, H, Dh)
        scale = 1.0 / np.sqrt(Dh)
        attn = jax.nn.softmax(jnp.einsum('bnhd,bmhd->bhnm', q, k) * scale, axis=-1)
        o = jnp.einsum('bhnm,bmhd->bnhd', attn, v).reshape(B, N, C)
        out = _qdq(o) @ _qdq(wp).T + bp
        return out

    def _L1_ffn_ref(x, gate_W_packed, gate_scales, up_W_packed, up_scales, down_W_packed, down_scales):
        import jax, jax.numpy as jnp
        import numpy as np
        BLOCK_SIZE = 32
        HIDDEN_SIZE = 256
        MLP_DIM = 2048
        NVFP4_LUT = jnp.array([0.0, 0.5, 1.0, 1.5, 2.0, 3.0, 4.0, 6.0, 0.0, -0.5, -1.0, -1.5, -2.0, -3.0, -4.0, -6.0], dtype=jnp.float32)

        def dequant_nvfp4(W_packed, scales, block=BLOCK_SIZE):
            N = W_packed.shape[0]
            low = W_packed & 15
            high = W_packed >> 4 & 15
            idx = jnp.stack([low, high], axis=-1).reshape(N, -1)
            vals = NVFP4_LUT[idx]
            K = vals.shape[1]
            vals = vals.reshape(N, K // block, block) * scales[:, :, None]
            return vals.reshape(N, K)
        B, S, H = x.shape
        xt = x.reshape(B * S, H)
        Wg = dequant_nvfp4(gate_W_packed, gate_scales)
        Wu = dequant_nvfp4(up_W_packed, up_scales)
        Wd = dequant_nvfp4(down_W_packed, down_scales)
        gate = jnp.einsum('th,nh->tn', xt, Wg)
        up = jnp.einsum('th,nh->tn', xt, Wu)
        gelu = jnp.tanh(0.7978845608028654 * (gate + 0.044715 * gate ** 3)) * gate * 0.5 + gate * 0.5
        inter = gelu * up
        out = jnp.einsum('tn,hn->th', inter, Wd)
        return out.reshape(B, S, H)
    x = x + jnp.tanh(g_xattn[0]) * _L0_xattn_ref(_layernorm(x, axis=-1), ctx_2048, L0_xattn_Wq, L0_xattn_Wg, L0_xattn_bg, L0_xattn_Wkv, L0_xattn_Wo)
    x = x + jnp.tanh(g_ffn[0]) * _L0_ffn_ref(_layernorm(x, axis=-1), L0_ffn_gate_w, L0_ffn_w_gate_up, L0_ffn_w_down, L0_ffn_shared_gate_up, L0_ffn_shared_down)
    x = x + jnp.tanh(g_xattn[1]) * _L1_xattn_ref(_layernorm(x, axis=-1), ctx_2048, L1_xattn_wq, L1_xattn_bq, L1_xattn_wkv, L1_xattn_bkv, L1_xattn_wp, L1_xattn_bp)
    x = x + jnp.tanh(g_ffn[1]) * _L1_ffn_ref(_layernorm(x, axis=-1), L1_ffn_gate_W_packed, L1_ffn_gate_scales, L1_ffn_up_W_packed, L1_ffn_up_scales, L1_ffn_down_W_packed, L1_ffn_down_scales)
    return x

_drawn_inputs = setup_inputs


def setup_inputs(seed=0):
    import zlib

    import numpy as np

    out = dict(_drawn_inputs(seed))
    spreads = {'g_ffn': (-1.0, 0.2), 'L0_xattn_bg': (1.0, 0.6)}
    factors = {'L0_xattn_Wq': 3.792,
     'L0_ffn_gate_w': 3.69,
     'L0_ffn_w_gate_up': 3.186,
     'L0_ffn_w_down': 3.188,
     'L1_xattn_wq': 23.975,
     'L1_xattn_bq': 200.0,
     'L1_xattn_bkv': 6.687}
    for name, (base, spread) in spreads.items():
        noise = np.random.default_rng([zlib.crc32(name.encode()), seed]).standard_normal(out[name].shape)
        drawn = base * np.exp(spread * noise) if base else spread * noise
        out[name] = jnp.asarray(drawn.astype(out[name].dtype))
    for name, factor in factors.items():
        out[name] = (out[name] * factor).astype(out[name].dtype)
    return out
```

```python
from contextlib import ExitStack

import numpy as np

import concourse.bass as bass
from concourse import mybir

F32 = mybir.dt.float32
I32 = mybir.dt.int32
ALU = mybir.AluOpType
ACT = mybir.ActivationFunctionType
AX = mybir.AxisListType

B, L, D, S = 32, 56, 256, 1500
H, HD = 16, 16
P = 128
KC = D // P
HC = P // HD
T = B * L
TT = 2 * L
NT = T // TT
TG = 4 * TT
NG = T // TG
CH = 125
NC = S // CH
CP = 2
NP = NC // CP
CW = D + 4
E, I = 8, 512
IC = I // P
M, MC = 2048, 2048 // P
BLK = 32
MAGIC = 12582912.0
PAIRS = H // 2


class Core:

    def __init__(self, nc, ctx):
        self.nc, self.ctx = nc, ctx

    def sb(self, name, shape, dt=F32):
        return self.ctx.enter_context(self.nc.sbuf_tensor(name, shape, dt))

    def ps(self, name, shape):
        return self.ctx.enter_context(self.nc.psum_tensor(name, shape, F32))

    def sem(self, name):
        return self.ctx.enter_context(self.nc.semaphore(name))


def in_order(eng, sem):
    count = [0]

    def step(ins):
        count[0] += 1
        ins.then_inc(sem, 1)
        eng.wait_ge(sem, count[0])

    return step


def norm_buffers(c, tag):
    return {
        "stats": c.sb(f"{tag}_stats", [TT, NT, 6]), "mv": c.sb(f"{tag}_mv", [TT, NT, 2]),
        "var": c.sb(f"{tag}_var", [TT, NT]), "rstd": c.sb(f"{tag}_rstd", [TT, NT]),
        "half": c.sb(f"{tag}_half", [TT, NT]),
        "stats_done": c.sem(f"{tag}_stats_done"), "mv_done": c.sem(f"{tag}_mv_done"),
        "var_done": c.sem(f"{tag}_var_done"), "half_set": c.sem(f"{tag}_half_set"),
        "rstd_done": c.sem(f"{tag}_rstd_done"), "xn_done": c.sem(f"{tag}_xn_done"),
    }


def norm_vector(dve, n, x, xn):
    for t in range(NT):
        dve.bn_stats(out=n["stats"][:, t, :], in_=x[:, t, :]).then_inc(n["stats_done"], 1)
    for t in range(NT):
        dve.wait_ge(n["stats_done"], t + 1)
        dve.bn_aggr(out=n["mv"][:, t, :], in_=n["stats"][:, t, :]).then_inc(n["mv_done"], 1)
    dve.wait_ge(n["mv_done"], NT)
    dve.tensor_scalar(n["var"][:, :], n["mv"][:, :, 1], 1e-5, None, ALU.add).then_inc(n["var_done"], 1)
    dve.wait_ge(n["rstd_done"], 1)
    for t in range(NT):
        dve.tensor_scalar(xn[:, t, :], x[:, t, :], n["mv"][:, t, 0:1], n["rstd"][:, t:t + 1],
                          ALU.subtract, ALU.mult).then_inc(n["xn_done"], 1)


def norm_pool(pool, n):
    pool.memset(n["half"][:, :], -0.5).then_inc(n["half_set"], 1)
    pool.wait_ge(n["half_set"], 1)
    pool.wait_ge(n["var_done"], 1)
    pool.tensor_tensor(n["rstd"][:, :], n["var"][:, :], n["half"][:, :], ALU.pow).then_inc(n["rstd_done"], 1)


def fake_quant(dve, step, src, out, absmax, scale, inverse, n):
    step(dve.tensor_reduce(absmax, src, AX.X, ALU.max, apply_absolute_value=True))
    step(dve.tensor_scalar(scale, absmax, 1.0 / 127.0, 1e-8, ALU.mult, ALU.max))
    step(dve.reciprocal(inverse, scale))
    for k in range(n):
        step(dve.tensor_scalar(out[:, k, :], src[:, k, :], inverse[:, k:k + 1], MAGIC, ALU.mult, ALU.add))
        step(dve.tensor_scalar(out[:, k, :], out[:, k, :], MAGIC, 127.0, ALU.subtract, ALU.min))
        step(dve.tensor_scalar(out[:, k, :], out[:, k, :], -127.0, scale[:, k:k + 1], ALU.max, ALU.mult))


def transpose_tiles(pe, bank, src, g, ident):
    for k in range(KC):
        for h in range(2):
            at = k * 2 * TT + h * TT
            mm = pe.transpose(bank[:, at:at + TT], src[:, 2 * g + h, k * P:(k + 1) * P], ident[0:TT, 0:TT])
    return mm


def setup(nc, a, K):
    with ExitStack() as ctx:
        c = Core(nc, ctx)
        names = ["Wq", "Wg", "Wk", "Wv", "Wo", "wq", "wk", "wv", "wp"]
        raw = {n: c.sb(f"raw_{n}", [P, KC, D]) for n in names}
        xn = c.sb("s_xn", [TT, NT, D])
        xnT = c.sb("s_xnT", [P, KC, T])
        expq = c.sb("s_expq", [P, 8, TG])
        am, sc, iv = (c.sb(f"s_{n}", [P, 2, KC]) for n in ("am", "sc", "iv"))
        banks = [c.ps(f"s_bank{i}", [P, 512]) for i in range(8)]
        n = norm_buffers(c, "n0")
        x_in, w_in, v_in = c.sem("x_in"), [c.sem(f"w_in_{m}") for m in names], c.sem("v_in")
        zeroed, ones_set, masks_set = c.sem("zeroed"), c.sem("ones_set"), c.sem("masks_set")
        full, emptied, quant = c.sem("s_full"), c.sem("s_emptied"), c.sem("s_quant")
        exp_done, min_done, phi_done = c.sem("s_exp"), c.sem("s_min"), c.sem("s_phi")
        gate_done, quant_done, tanh_done = c.sem("s_gate"), c.sem("s_quantised"), c.sem("s_tanh")
        src = {
            "Wq": a["L0_xattn_Wq"], "Wg": a["L0_xattn_Wg"], "Wk": a["L0_xattn_Wkv"][0:D, :],
            "Wv": a["L0_xattn_Wkv"][D:2 * D, :], "Wo": a["L0_xattn_Wo"], "wq": a["L1_xattn_wq"],
            "wk": a["L1_xattn_wkv"][0:D, :], "wv": a["L1_xattn_wkv"][D:2 * D, :], "wp": a["L1_xattn_wp"],
        }
        NW, NX = len(names), NT // 2
        order = ["Wq", "Wg", "Wk", "Wv", "Wo", "wk", "wv", "wq", "wp"]
        block = ctx.enter_context(nc.Block())

        @block.sync
        def _(sp):
            sp.dma_start(K["x"][:, :, :], a["x"].rearrange("b l d -> (b l) d").rearrange("(t p) d -> p t d", p=TT)).then_inc(x_in, 16)
            for m, s in zip(names, w_in):
                sp.dma_start(raw[m][:, :, :], src[m].rearrange("(o p) i -> p o i", p=P)).then_inc(s, 16)
            sp.wait_ge(v_in, 16 * 8)

        @block.scalar
        def _(act):
            with nc.allow_non_contiguous_dma(reason="biases, one value to a partition"):
                for t, v in (("bg", a["L0_xattn_bg"]), ("bq", a["L1_xattn_bq"]),
                             ("bk", a["L1_xattn_bkv"][0:D]), ("bv", a["L1_xattn_bkv"][D:2 * D])):
                    act.dma_start(K[t][:, :], v.rearrange("(o p) -> p o", p=P)).then_inc(v_in, 16)
                act.dma_start(K["bp"][:, :], a["L1_xattn_bp"].partition_broadcast(TT)).then_inc(v_in, 16)
                act.dma_start(K["gates"][:, 0:2], a["g_xattn"].partition_broadcast(TT)).then_inc(v_in, 16)
                act.dma_start(K["gates"][:, 2:4], a["g_ffn"].partition_broadcast(TT)).then_inc(v_in, 16)
                act.dma_start(K["gates"][:, 4:5], a["g_ffn"][0:1].partition_broadcast(TT)).then_inc(v_in, 16)
            act.wait_ge(v_in, 16 * 8)
            act.activation(K["gate_tanh"][:, :], K["gates"][:, 0:4], ACT.Tanh).then_inc(tanh_done, 1)
            for q in range(8):
                act.wait_ge(full, NW + NX + q + 1)
                act.activation(expq[:, q, :], banks[(NW + NX + q) % 8][:, 0:TG], ACT.Exp).then_inc(exp_done, 1)
            for q in range(8):
                k, g = divmod(q, NG)
                act.wait_ge(full, NW + NX + 8 + q + 1)
                act.activation(K["gateT"][:, k, g * TG:(g + 1) * TG], banks[(NW + NX + 8 + q) % 8][:, 0:TG],
                               ACT.Sigmoid, bias=K["bg"][:, k:k + 1]).then_inc(gate_done, 1)

        @block.gpsimd
        def _(pool):
            pool.memset(K["ident"][:, :], 0.0).then_inc(zeroed, 1)
            pool.memset(K["headmask"][:, :], 1.0).then_inc(ones_set, 1)
            pool.memset(K["pairmask"][:, :], 1.0).then_inc(ones_set, 1)
            pool.memset(K["fold"][:, :], 0.0).then_inc(zeroed, 1)
            pool.wait_ge(zeroed, 2)
            pool.affine_select(out=K["ident"][:, :], in_=K["ident"][:, :], compare_op=ALU.not_equal, fill=1.0,
                               base=0, pattern=[[-1, P]], channel_multiplier=1).then_inc(masks_set, 1)
            pool.wait_ge(ones_set, 2)
            hm = K["headmask"][:, :].rearrange("p (h n) -> p h n", h=HC)
            pool.affine_select(out=hm, in_=hm, compare_op=ALU.is_ge, fill=0.0, base=0,
                               pattern=[[-HD, HC], [0, L]], channel_multiplier=1).then_inc(masks_set, 1)
            pool.wait_ge(masks_set, 2)
            pool.affine_select(out=hm, in_=hm, compare_op=ALU.is_ge, fill=0.0, base=HD - 1,
                               pattern=[[HD, HC], [0, L]], channel_multiplier=-1).then_inc(masks_set, 1)
            pool.wait_ge(masks_set, 3)
            pool.tensor_copy(K["blockmask"][:, :].rearrange("p (h e) -> p h e", h=HC), hm[:, :, 0:HD]).then_inc(masks_set, 1)
            pm = K["pairmask"][:, :].rearrange("p (j h e) -> p j h e", j=4, h=2)
            pool.affine_select(out=pm[:, :, 0, :], in_=pm[:, :, 0, :], compare_op=ALU.is_ge, fill=0.0, base=L - 1,
                               pattern=[[0, 4], [0, HD]], channel_multiplier=-1).then_inc(masks_set, 1)
            pool.affine_select(out=pm[:, :, 1, :], in_=pm[:, :, 1, :], compare_op=ALU.is_ge, fill=0.0, base=-L,
                               pattern=[[0, 4], [0, HD]], channel_multiplier=1).then_inc(masks_set, 1)
            pool.affine_select(out=K["fold"][:, :], in_=K["fold"][:, :], compare_op=ALU.not_equal, fill=1.0,
                               base=0, pattern=[[-1, L]], channel_multiplier=1).then_inc(masks_set, 1)
            pool.wait_ge(masks_set, 7)
            pool.affine_select(out=K["fold"][:, :], in_=K["fold"][:, :], compare_op=ALU.not_equal, fill=1.0,
                               base=-L, pattern=[[-1, L]], channel_multiplier=1).then_inc(masks_set, 1)
            norm_pool(pool, n)
            for q in range(8):
                pool.wait_ge(exp_done, q + 1)
                pool.tensor_scalar(expq[:, q, :], expq[:, q, :], 1.0, 0.0, ALU.min, ALU.max).then_inc(min_done, 1)

        @block.vector
        def _(dve):
            step = in_order(dve, quant)
            dve.wait_ge(x_in, 16)
            norm_vector(dve, n, K["x"], xn)
            for i, m in enumerate(("wq", "wp")):
                dve.wait_ge(w_in[names.index(m)], 16)
                fake_quant(dve, step, raw[m][:, :, :], raw[m], am[:, i, :], sc[:, i, :], iv[:, i, :], KC)
            for i, m in enumerate(order):
                dve.wait_ge(full, i + 1)
                dve.tensor_copy(K["T_" + m][:, :, :].rearrange("p k o -> p (k o)"), banks[i % 8][:, :]).then_inc(emptied, 1)
            for g in range(NX):
                dve.wait_ge(full, NW + g + 1)
                dve.tensor_copy(xnT[:, :, g * 2 * TT:(g + 1) * 2 * TT],
                                banks[(NW + g) % 8][:, 0:TG].rearrange("p (k n) -> p k n", k=KC)).then_inc(emptied, 1)
            for q in range(8):
                k, g = divmod(q, NG)
                dve.wait_ge(min_done, q + 1)
                dve.scalar_tensor_tensor(out=K["phiqT"][:, k, g * TG:(g + 1) * TG], in0=banks[(NW + NX + q) % 8][:, 0:TG],
                                         scalar=0.0, in1=expq[:, q, :], op0=ALU.max, op1=ALU.add).then_inc(phi_done, 1)

        @block.tensor
        def _(pe):
            pe.wait_ge(masks_set, 1)
            for i, m in enumerate(order):
                pe.wait_ge(w_in[names.index(m)], 16)
                if m in ("wq", "wp"):
                    pe.wait_ge(quant, (3 + 3 * KC) * (1 + ("wq", "wp").index(m)))
                if i >= 8:
                    pe.wait_ge(emptied, i - 7)
                for k in range(KC):
                    for o in range(KC):
                        mm = pe.transpose(banks[i % 8][:, (k * KC + o) * P:(k * KC + o + 1) * P],
                                          raw[m][:, o, k * P:(k + 1) * P], K["ident"][:, :])
                mm.then_inc(full, 1)
            for g in range(NX):
                pe.wait_ge(n["xn_done"], 2 * g + 2)
                pe.wait_ge(emptied, NW + g - 7)
                transpose_tiles(pe, banks[(NW + g) % 8], xn, g, K["ident"]).then_inc(full, 1)
            pe.wait_ge(emptied, NW + NX)
            for which, w in enumerate(("T_Wq", "T_Wg")):
                for q in range(8):
                    k, g = divmod(q, NG)
                    if which:
                        pe.wait_ge(phi_done, q + 1)
                    for i in range(KC):
                        mm = pe.matmul(banks[(NW + NX + 8 * which + q) % 8][:, 0:TG], K[w][:, i, k * P:(k + 1) * P],
                                       xnT[:, i, g * TG:(g + 1) * TG], start=(i == 0), stop=(i == KC - 1))
                    mm.then_inc(full, 1)


def linear_attention(nc, a, K):
    with ExitStack() as ctx:
        c = Core(nc, ctx)
        ctx_sb = [c.sb(f"l_ctx{u}", [CH, NC, CW]) for u in range(2)]
        ctxT = c.sb("l_ctxT", [P, KC, S])
        phik = [c.sb(f"l_phik{u}", [CH, NC, D]) for u in range(2)]
        expk = c.sb("l_expk", [CH, 2, CP * D])
        G = c.sb("l_G", [P, KC, D + 1])
        GT = c.sb("l_GT", [P, KC, D])
        KV = c.sb("l_KV", [P, KC, P])
        KS = c.sb("l_KS", [P, KC, P])
        den = c.sb("l_den", [P, KC, L])
        rden = c.sb("l_rden", [P, KC, L])
        t_bank = [c.ps(f"l_t{i}", [P, 512]) for i in range(2)]
        k_bank = [c.ps(f"l_k{i}", [P, 512]) for i in range(2)]
        g_bank = [c.ps(f"l_g{i}", [P, 512]) for i in range(KC)]
        gt_bank, s_bank = c.ps("l_gt", [P, 512]), c.ps("l_s", [P, 512])
        nd = s_bank[:, 256:256 + 4 * L].rearrange("p (k w n) -> p k w n", k=KC, w=2)
        ones_set = c.sem("l_ones")
        ctx_in = [c.sem(f"l_ctx_in{u}") for u in range(2)]
        t_full, t_read = c.sem("l_t_full"), c.sem("l_t_read")
        k_full, exp_done, min_done, phi_done = c.sem("l_k_full"), c.sem("l_exp"), c.sem("l_min"), c.sem("l_phi")
        g_full, g_read = c.sem("l_g_full"), c.sem("l_g_read")
        gt_full, gt_read = c.sem("l_gt_full"), c.sem("l_gt_read")
        kv_full, kv_read = c.sem("l_kv_full"), c.sem("l_kv_read")
        nd_full, den_eps, den_inv, nd_read = c.sem("l_nd_full"), c.sem("l_den_eps"), c.sem("l_den_inv"), c.sem("l_nd_read")
        block = ctx.enter_context(nc.Block())
        rows = a["ctx_2048"]

        def load(sp, b, u):
            v = rows[bass.ds(b, 1), :, :].rearrange("b (p c) d -> p (b c) d", p=CH)
            sp.dma_start(ctx_sb[u][0:112, :, 0:D], v[0:112, :, :]).then_inc(ctx_in[u], 16)
            sp.dma_start(ctx_sb[u][112:CH, :, 0:D], v[112:CH, :, :]).then_inc(ctx_in[u], 16)

        @block.sync
        def _(sp):
            load(sp, 0, 0)
            load(sp, 1, 1)
            with sp.Fori(0, B // 2 - 1) as i:
                for u in range(2):
                    sp.wait_ge(g_full, 2 * i + u + 1)
                    load(sp, 2 * i + 2 + u, u)

        @block.gpsimd
        def _(pool):
            for u in range(2):
                pool.memset(ctx_sb[u][:, :, D:CW], 1.0).then_inc(ones_set, 1)

        @block.scalar
        def _(act):
            def batch(b, first):
                def t_copy(g):
                    act.wait_ge(t_full, NP * b + g + 1)
                    if not first:
                        act.wait_ge(k_full, NP * b - NP + g + 1)
                    act.copy(ctxT[:, :, g * CP * CH:(g + 1) * CP * CH],
                             t_bank[g % 2][:, 0:KC * CP * CH].rearrange("p (k n) -> p k n", k=KC)).then_inc(t_read, 1)

                def exp(g):
                    act.wait_ge(min_done, NP * b + g + 1)
                    act.activation(expk[:, g % 2, :], expk[:, g % 2, :], ACT.Exp).then_inc(exp_done, 1)

                t_copy(0)
                t_copy(1)
                if not first:
                    act.wait_ge(gt_full, b)
                    act.copy(GT[:, :, :].rearrange("p k d -> p (k d)"), gt_bank[:, :]).then_inc(gt_read, 1)
                exp(0)
                for g in range(2, NP):
                    t_copy(g)
                    exp(g - 1)
                exp(NP - 1)

            batch(0, True)
            with act.Fori(1, B) as b:
                batch(b, False)
            act.wait_ge(gt_full, B)
            act.copy(GT[:, :, :].rearrange("p k d -> p (k d)"), gt_bank[:, :]).then_inc(gt_read, 1)

        @block.vector
        def _(dve):
            def g_copy(b):
                dve.wait_ge(g_full, b + 1)
                for k in range(KC):
                    ins = dve.tensor_copy(G[:, k, :], g_bank[k][:, 0:D + 1])
                    ins.then_inc(g_read, 1)

            def kv_copy(b):
                dve.wait_ge(kv_full, b + 1)
                dve.tensor_tensor(KV[:, :, :], s_bank[:, 0:D].rearrange("p (k e) -> p k e", k=KC),
                                  K["blockmask"][:, :].unsqueeze(1).to_broadcast([P, KC, P]), ALU.mult).then_inc(kv_read, 1)
                for k in range(KC):
                    dve.tensor_scalar(KS[:, k, :], K["blockmask"][:, :], G[:, k, D:D + 1], None, ALU.mult).then_inc(kv_read, 1)

            def nd_use(b):
                dve.wait_ge(nd_full, b + 1)
                dve.tensor_scalar(den[:, :, :], nd[:, :, 1, :], 1e-6, None, ALU.add).then_inc(den_eps, 1)
                dve.wait_ge(den_eps, b + 1)
                dve.reciprocal(rden[:, :, :], den[:, :, :]).then_inc(den_inv, 1)
                dve.wait_ge(den_inv, b + 1)
                dve.tensor_tensor(K["attT"][:, :, bass.ds(b * L, L)], nd[:, :, 0, :], rden[:, :, :], ALU.mult).then_inc(nd_read, 1)

            def batch(b, u, early):
                def low(g):
                    dve.wait_ge(k_full, NP * b + g + 1)
                    if early or g >= 2:
                        dve.wait_ge(phi_done, NP * b + g - 1)
                    dve.tensor_scalar(expk[:, g % 2, :], k_bank[g % 2][0:CH, :], 0.0, None, ALU.min).then_inc(min_done, 1)

                def phi(g):
                    dve.wait_ge(exp_done, NP * b + g + 1)
                    if early >= 2:
                        dve.wait_ge(g_full, b - 1)
                    dve.scalar_tensor_tensor(out=phik[u][:, g * CP:(g + 1) * CP, :].rearrange("p c d -> p (c d)"),
                                             in0=k_bank[g % 2][0:CH, :], scalar=0.0, in1=expk[:, g % 2, :],
                                             op0=ALU.max, op1=ALU.add).then_inc(phi_done, 1)
                if early:
                    g_copy(b - 1)
                low(0)
                low(1)
                phi(0)
                if early:
                    kv_copy(b - 1)
                low(2)
                phi(1)
                low(3)
                phi(2)
                if early:
                    nd_use(b - 1)
                low(4)
                phi(3)
                low(5)
                phi(4)
                phi(5)

            batch(0, 0, 0)
            batch(1, 1, 1)
            with dve.Fori(1, B // 2) as i:
                batch(2 * i, 0, 2)
                batch(2 * i + 1, 1, 2)
            g_copy(B - 1)
            kv_copy(B - 1)
            nd_use(B - 1)
            dve.wait_ge(nd_read, B)
            dve.tensor_tensor(K["attT"][:, :, :], K["attT"][:, :, :], K["gateT"][:, :, :], ALU.mult)

        @block.tensor
        def _(pe):
            def t_group(b, n, u, g, early):
                if g == 0:
                    pe.wait_ge(ctx_in[u], 32 * (n + 1))
                if early or g >= 2:
                    pe.wait_ge(t_read, NP * b + g - 1)
                for k in range(KC):
                    for h in range(CP):
                        at = (k * CP + h) * CH
                        mm = pe.transpose(t_bank[g % 2][:, at:at + CH], ctx_sb[u][:, g * CP + h, k * P:(k + 1) * P],
                                          K["ident"][0:CH, 0:CH])
                mm.then_inc(t_full, 1)

            def k_group(b, g, early):
                pe.wait_ge(t_read, NP * b + g + 1)
                if early or g >= 2:
                    pe.wait_ge(phi_done, NP * b + g - 1)
                for h in range(CP):
                    for i in range(KC):
                        at = (g * CP + h) * CH
                        mm = pe.matmul(k_bank[g % 2][0:CH, h * D:(h + 1) * D], ctxT[:, i, at:at + CH], K["T_Wk"][:, i, :],
                                       start=(i == 0), stop=(i == KC - 1))
                mm.then_inc(k_full, 1)

            def g_group(b, u, g, early):
                pe.wait_ge(phi_done, NP * b + g + 1)
                if g == 0 and early:
                    pe.wait_ge(g_read, KC * b)
                if g == 0 and not early:
                    pe.wait_ge(ones_set, 2)
                for ch in range(g * CP, (g + 1) * CP):
                    for k in range(KC):
                        mm = pe.matmul(g_bank[k][:, 0:D + 1], phik[u][:, ch, k * P:(k + 1) * P], ctx_sb[u][:, ch, 0:D + 1],
                                       start=(ch == 0), stop=(ch == NC - 1))
                if g == NP - 1:
                    mm.then_inc(g_full, 1)

            def gt(b):
                pe.wait_ge(g_read, KC * (b + 1))
                for i in range(KC):
                    for k in range(KC):
                        at = (i * KC + k) * P
                        mm = pe.transpose(gt_bank[:, at:at + P], G[:, k, i * P:(i + 1) * P], K["ident"][:, :])
                mm.then_inc(gt_full, 1)

            def kv(b, again):
                pe.wait_ge(gt_read, b + 1)
                if again:
                    pe.wait_ge(nd_read, b)
                for k in range(KC):
                    for i in range(KC):
                        mm = pe.matmul(s_bank[:, k * P:(k + 1) * P], GT[:, i, k * P:(k + 1) * P],
                                       K["T_Wv"][:, i, k * P:(k + 1) * P], start=(i == 0), stop=(i == KC - 1))
                mm.then_inc(kv_full, 1)

            def numden(b):
                pe.wait_ge(kv_read, (1 + KC) * (b + 1))
                for k in range(KC):
                    for w, lhs in enumerate((KV, KS)):
                        mm = pe.matmul(nd[:, k, w, :], lhs[:, k, :], K["phiqT"][:, k, bass.ds(b * L, L)],
                                       start=True, stop=True)
                mm.then_inc(nd_full, 1)

            def batch(b, n, u, early):
                t_group(b, n, u, 0, early)
                t_group(b, n, u, 1, early)
                if early:
                    gt(b - 1)
                k_group(b, 0, early)
                t_group(b, n, u, 2, early)
                k_group(b, 1, early)
                if early:
                    kv(b - 1, early > 1)
                t_group(b, n, u, 3, early)
                k_group(b, 2, early)
                g_group(b, u, 0, early)
                t_group(b, n, u, 4, early)
                k_group(b, 3, early)
                if early:
                    numden(b - 1)
                g_group(b, u, 1, early)
                t_group(b, n, u, 5, early)
                k_group(b, 4, early)
                g_group(b, u, 2, early)
                k_group(b, 5, early)
                for g in range(3, NP):
                    g_group(b, u, g, early)

            batch(0, 0, 0, 0)
            batch(1, 0, 1, 1)
            with pe.Fori(1, B // 2) as i:
                batch(2 * i, i, 0, 2)
                batch(2 * i + 1, i, 1, 2)
            gt(B - 1)
            kv(B - 1, True)
            numden(B - 1)


def experts(nc, a, K):
    with ExitStack() as ctx:
        c = Core(nc, ctx)
        xn = c.sb("e_xn", [TT, NT, D])
        acc = c.sb("e_acc", [TT, NT, D])
        xnT = c.sb("e_xnT", [P, KC, T])
        wr = c.sb("e_wr", [P, KC, E])
        wgu = [c.sb(f"e_wgu{u}", [P, KC, 2 * I]) for u in range(2)]
        wd = [c.sb(f"e_wd{u}", [P, IC, D]) for u in range(2)]
        hT = [c.sb(f"e_hT{u}", [P, IC, TG]) for u in range(2)]
        sil = c.sb("e_sil", [P, 2, TG])
        comb = c.sb("e_comb", [TT, NT, 1 + E])
        pr, key, pick, rest, ranks = (c.sb(f"e_{m}", [TT, NT, E]) for m in ("pr", "key", "pick", "rest", "ranks"))
        irank = c.sb("e_irank", [TT, E], I32)
        mx, tot = c.sb("e_mx", [TT, NT]), c.sb("e_tot", [TT, NT])
        g_bank = [c.ps(f"e_g{i}", [P, 512]) for i in range(2)]
        u_bank = [c.ps(f"e_u{i}", [P, 512]) for i in range(2)]
        d_bank = [c.ps(f"e_d{i}", [P, 512]) for i in range(4)]
        n = norm_buffers(c, "n1")
        w_in, wr_in = [c.sem(f"e_w_in{u}") for u in range(2)], c.sem("e_wr_in")
        o_full, o_read, small = c.sem("e_o_full"), c.sem("e_o_read"), c.sem("e_small")
        t_full, t_read, r_full = c.sem("e_t_full"), c.sem("e_t_read"), c.sem("e_r_full")
        exp_go, exp_done, iota_done, rank_done = c.sem("e_exp_go"), c.sem("e_exp"), c.sem("e_iota"), c.sem("e_rank")
        g_full, u_full, sil_done, h_done = c.sem("e_g_full"), c.sem("e_u_full"), c.sem("e_sil_done"), c.sem("e_h")
        d_full, d_read, comb_done, zeroed = c.sem("e_d_full"), c.sem("e_d_read"), c.sem("e_comb_done"), c.sem("e_zero")
        block = ctx.enter_context(nc.Block())
        STEPS = NG
        gu_of = lambda e: a["L0_ffn_w_gate_up"][bass.ds(e, 1), :, :].rearrange("e (k p) n -> p (e k) n", p=P)
        wd_of = lambda e: a["L0_ffn_w_down"][bass.ds(e, 1), :, :].rearrange("e (k p) n -> p (e k) n", p=P)

        @block.sync
        def _(sp):
            def load(u, gu, down):
                sp.dma_start(wgu[u][:, :, :], gu).then_inc(w_in[u], 16)
                sp.dma_start(wd[u][:, :, :], down).then_inc(w_in[u], 16)

            with nc.allow_non_contiguous_dma(reason="router weights, 8 to a row"):
                sp.dma_start(wr[:, :, :], a["L0_ffn_gate_w"].rearrange("(k p) e -> p k e", p=P)).then_inc(wr_in, 16)
            load(0, a["L0_ffn_shared_gate_up"].rearrange("(k p) n -> p k n", p=P),
                 a["L0_ffn_shared_down"].rearrange("(k p) n -> p k n", p=P))
            load(1, gu_of(0), wd_of(0))
            with sp.Fori(1, E // 2) as i:
                sp.wait_ge(d_full, NG * (2 * i - 1))
                load(0, gu_of(2 * i - 1), wd_of(2 * i - 1))
                sp.wait_ge(d_full, NG * 2 * i)
                load(1, gu_of(2 * i), wd_of(2 * i))
            sp.wait_ge(d_full, NG * (E - 1))
            load(0, gu_of(E - 1), wd_of(E - 1))

        @block.gpsimd
        def _(pool):
            pool.memset(comb[:, :, 0:1], 1.0).then_inc(zeroed, 1)
            pool.memset(acc[:, :, :], 0.0).then_inc(zeroed, 1)
            pool.iota(irank[:, :], [[-1, E]], base=E, channel_multiplier=0).then_inc(iota_done, 1)
            pool.wait_ge(iota_done, 1)
            pool.tensor_copy(ranks[:, :, :], irank[:, :].unsqueeze(1).to_broadcast([TT, NT, E])).then_inc(rank_done, 1)
            norm_pool(pool, n)

        @block.scalar
        def _(act):
            act.wait_ge(exp_go, 1)
            act.activation(pr[:, :, :], key[:, :, :], ACT.Exp).then_inc(exp_done, 1)

            def expert(m):
                for g in range(STEPS):
                    for j in range(IC):
                        k = (m * STEPS + g) * IC + j
                        act.wait_ge(g_full, k + 1)
                        if not isinstance(m, int) or m or g or j >= 2:
                            act.wait_ge(h_done, k - 1)
                        act.activation(sil[:, j % 2, :], g_bank[j % 2][:, 0:TG], ACT.Silu).then_inc(sil_done, 1)

            expert(0)
            with act.Fori(1, 1 + E) as m:
                expert(m)

        @block.vector
        def _(dve):
            step = in_order(dve, small)
            for t in range(NT):
                dve.wait_ge(o_full, t + 1)
                dve.scalar_tensor_tensor(out=K["x"][:, t, :], in0=d_bank[t % 4][0:TT, 0:D], scalar=K["gate_tanh"][:, 0:1],
                                         in1=K["x"][:, t, :], op0=ALU.mult, op1=ALU.add).then_inc(o_read, 1)
            dve.wait_ge(o_read, NT)
            norm_vector(dve, n, K["x"], xn)
            for g in range(NT // 2):
                dve.wait_ge(t_full, g + 1)
                dve.tensor_copy(xnT[:, :, g * 2 * TT:(g + 1) * 2 * TT],
                                g_bank[g % 2][:, 0:TG].rearrange("p (k n) -> p k n", k=KC)).then_inc(t_read, 1)
            dve.wait_ge(r_full, 1)
            logits = d_bank[0][0:TT, 0:NT * E].rearrange("p (t e) -> p t e", e=E)
            wide = lambda v: v.unsqueeze(2).to_broadcast([TT, NT, E])
            step(dve.tensor_reduce(mx[:, :], logits, AX.X, ALU.max))
            dve.tensor_tensor(key[:, :, :], logits, wide(mx[:, :]), ALU.subtract).then_inc(exp_go, 1)
            dve.wait_ge(exp_done, 1)
            step(dve.tensor_reduce(tot[:, :], pr[:, :, :], AX.X, ALU.add))
            step(dve.reciprocal(tot[:, :], tot[:, :]))
            step(dve.tensor_tensor(pr[:, :, :], pr[:, :, :], wide(tot[:, :]), ALU.mult))
            step(dve.tensor_copy(rest[:, :, :], pr[:, :, :]))
            dve.wait_ge(rank_done, 1)
            dve.wait_ge(zeroed, 2)
            chosen = comb[:, :, 1:1 + E]
            for r in range(2):
                step(dve.tensor_reduce(mx[:, :], rest[:, :, :], AX.X, ALU.max))
                step(dve.tensor_tensor(key[:, :, :], rest[:, :, :], wide(mx[:, :]), ALU.is_equal))
                step(dve.tensor_tensor(key[:, :, :], key[:, :, :], ranks[:, :, :], ALU.mult))
                step(dve.tensor_reduce(mx[:, :], key[:, :, :], AX.X, ALU.max))
                step(dve.tensor_tensor(pick[:, :, :], key[:, :, :], wide(mx[:, :]), ALU.is_equal))
                if r == 0:
                    step(dve.tensor_copy(chosen, pick[:, :, :]))
                    step(dve.scalar_tensor_tensor(out=rest[:, :, :].rearrange("p t e -> p (t e)"),
                                                  in0=pick[:, :, :].rearrange("p t e -> p (t e)"), scalar=-2.0,
                                                  in1=rest[:, :, :].rearrange("p t e -> p (t e)"), op0=ALU.mult, op1=ALU.add))
                else:
                    step(dve.tensor_tensor(chosen, chosen, pick[:, :, :], ALU.add))
            step(dve.tensor_tensor(pr[:, :, :], pr[:, :, :], chosen, ALU.mult))
            step(dve.tensor_reduce(tot[:, :], pr[:, :, :], AX.X, ALU.add))
            step(dve.reciprocal(tot[:, :], tot[:, :]))
            step(dve.tensor_tensor(chosen, pr[:, :, :], wide(tot[:, :]), ALU.mult))

            def up(m, g, known):
                for j in range(IC):
                    k = (m * STEPS + g) * IC + j
                    dve.wait_ge(sil_done, k + 1)
                    dve.wait_ge(u_full, k + 1)
                    if not known or m * STEPS + g >= 2:
                        dve.wait_ge(d_full, m * STEPS + g - 1)
                    dve.tensor_tensor(hT[g % 2][:, j, :], sil[:, j % 2, :], u_bank[j % 2][:, 0:TG], ALU.mult).then_inc(h_done, 1)

            def down(m, g, known):
                dve.wait_ge(d_full, m * STEPS + g + 1)
                if not known or m * STEPS + g:
                    dve.wait_ge(d_read, 4 * (m * STEPS + g))
                for q in range(4):
                    t = 4 * g + q
                    dve.scalar_tensor_tensor(out=acc[:, t, :], in0=d_bank[q][0:TT, 0:D], scalar=comb[:, t, bass.ds(m, 1)],
                                             in1=acc[:, t, :], op0=ALU.mult, op1=ALU.add).then_inc(d_read, 1)

            def expert(m, known):
                for g in range(STEPS):
                    up(m, g, known)
                    if g:
                        down(m, g - 1, known)
                    elif not known:
                        down(m - 1, STEPS - 1, False)

            expert(0, True)
            with dve.Fori(1, 1 + E) as m:
                expert(m, False)
            down(E, STEPS - 1, True)
            dve.wait_ge(d_read, 4 * STEPS * (1 + E))
            dve.scalar_tensor_tensor(out=K["x"][:, :, :].rearrange("p t d -> p (t d)"), in0=acc[:, :, :].rearrange("p t d -> p (t d)"),
                                     scalar=K["gate_tanh"][:, 2:3], in1=K["x"][:, :, :].rearrange("p t d -> p (t d)"),
                                     op0=ALU.mult, op1=ALU.add)

        @block.tensor
        def _(pe):
            for t in range(NT):
                if t >= 4:
                    pe.wait_ge(o_read, t - 3)
                for i in range(KC):
                    mm = pe.matmul(d_bank[t % 4][0:TT, 0:D], K["attT"][:, i, t * TT:(t + 1) * TT], K["T_Wo"][:, i, :],
                                   start=(i == 0), stop=(i == KC - 1))
                mm.then_inc(o_full, 1)
            for g in range(NT // 2):
                pe.wait_ge(n["xn_done"], 2 * g + 2)
                if g >= 2:
                    pe.wait_ge(t_read, g - 1)
                transpose_tiles(pe, g_bank[g % 2], xn, g, K["ident"]).then_inc(t_full, 1)
            pe.wait_ge(t_read, NT // 2)
            pe.wait_ge(wr_in, 16)
            for t in range(NT):
                for i in range(KC):
                    mm = pe.matmul(d_bank[0][0:TT, t * E:(t + 1) * E], xnT[:, i, t * TT:(t + 1) * TT], wr[:, i, :],
                                   start=(i == 0), stop=(i == KC - 1))
            mm.then_inc(r_full, 1)
            pe.wait_ge(exp_go, 1)

            def up(m, g, u, known):
                for j in range(IC):
                    k = (m * STEPS + g) * IC + j
                    if not known or k >= 2:
                        pe.wait_ge(h_done, k - 1)
                    for bank, col, done in ((g_bank, j, g_full), (u_bank, IC + j, u_full)):
                        for i in range(KC):
                            mm = pe.matmul(bank[j % 2][:, 0:TG], wgu[u][:, i, col * P:(col + 1) * P],
                                           xnT[:, i, g * TG:(g + 1) * TG], start=(i == 0), stop=(i == KC - 1))
                        mm.then_inc(done, 1)

            def down(m, g, u, known):
                pe.wait_ge(h_done, IC * (m * STEPS + g + 1))
                if not known or m * STEPS + g:
                    pe.wait_ge(d_read, 4 * (m * STEPS + g))
                for q in range(4):
                    for j in range(IC):
                        mm = pe.matmul(d_bank[q][0:TT, 0:D], hT[g % 2][:, j, q * TT:(q + 1) * TT], wd[u][:, j, :],
                                       start=(j == 0), stop=(j == IC - 1))
                mm.then_inc(d_full, 1)

            def expert(m, n, u, known):
                pe.wait_ge(w_in[u], 32 * (n + 1))
                for g in range(STEPS):
                    up(m, g, u, known)
                    if g:
                        down(m, g - 1, u, known)
                    elif not known:
                        down(m - 1, STEPS - 1, 1 - u, False)

            expert(0, 0, 0, True)
            with pe.Fori(0, E // 2) as i:
                expert(2 * i + 1, i, 1, False)
                expert(2 * i + 2, i + 1, 0, False)
            down(E, STEPS - 1, 0, True)


A_PLAN = [["T0", "T1"], ["K00", "V0"], ["V1", "T2", "T3"], ["K10", "V2"], ["K01", "T4", "T5"], ["K11", "V3"],
          ["K02", "V4"], ["K12", "V5"]]
A_ORDER = [w for slot in A_PLAN for w in slot]
KG = 3
GW = S // KG


def queries(nc, a, K):
    with ExitStack() as ctx:
        c = Core(nc, ctx)
        xn = c.sb("q_xn", [TT, NT, D])
        xnT = c.sb("q_xnT", [P, KC, T])
        am, sc, iv = (c.sb(f"q_{m}", [TT, NT]) for m in ("am", "sc", "iv"))
        t_bank = [c.ps(f"q_t{i}", [P, 512]) for i in range(4)]
        q_bank = [c.ps(f"q_q{i}", [P, 512]) for i in range(4)]
        n = norm_buffers(c, "n2")
        small, t_full, t_read, q_full, q_read = (c.sem(f"q_{m}") for m in ("small", "t_full", "t_read", "q_full", "q_read"))
        STEPS_ALL = 3 + 3 * NT
        block = ctx.enter_context(nc.Block())

        @block.gpsimd
        def _(pool):
            norm_pool(pool, n)

        @block.vector
        def _(dve):
            step = in_order(dve, small)
            norm_vector(dve, n, K["x"], xn)
            dve.wait_ge(n["xn_done"], NT)
            fake_quant(dve, step, xn[:, :, :], xn, am[:, :], sc[:, :], iv[:, :], NT)
            for g in range(NT // 2):
                dve.wait_ge(t_full, g + 1)
                dve.tensor_copy(xnT[:, :, g * 2 * TT:(g + 1) * 2 * TT],
                                t_bank[g % 4][:, 0:TG].rearrange("p (k n) -> p k n", k=KC)).then_inc(t_read, 1)

        @block.scalar
        def _(act):
            for q in range(KC * NG):
                k, g = divmod(q, NG)
                act.wait_ge(q_full, q + 1)
                act.activation(K["phiqT"][:, k, g * TG:(g + 1) * TG], q_bank[q % 4][:, 0:TG], ACT.Identity,
                               bias=K["bq"][:, k:k + 1]).then_inc(q_read, 1)

        @block.tensor
        def _(pe):
            for g in range(NT // 2):
                pe.wait_ge(small, 3 + 3 * (2 * g + 2))
                if g >= 4:
                    pe.wait_ge(t_read, g - 3)
                transpose_tiles(pe, t_bank[g % 4], xn, g, K["ident"]).then_inc(t_full, 1)
            pe.wait_ge(t_read, NT // 2)
            for q in range(KC * NG):
                k, g = divmod(q, NG)
                if q >= 4:
                    pe.wait_ge(q_read, q - 3)
                for i in range(KC):
                    mm = pe.matmul(q_bank[q % 4][:, 0:TG], K["T_wq"][:, i, k * P:(k + 1) * P], xnT[:, i, g * TG:(g + 1) * TG],
                                   start=(i == 0), stop=(i == KC - 1))
                mm.then_inc(q_full, 1)


def softmax_attention(nc, a, K):
    with ExitStack() as ctx:
        c = Core(nc, ctx)
        ctx_sb = [c.sb(f"a_ctx{u}", [CH, NC, D]) for u in range(2)]
        ctxT = c.sb("a_ctxT", [P, KC, S])
        keyT = [c.sb(f"a_keyT{u}", [P, KC, S]) for u in range(2)]
        val = [c.sb(f"a_val{u}", [CH, NC, D]) for u in range(2)]
        qbd = [c.sb(f"a_qbd{u}", [P, KC, HC, L]) for u in range(2)]
        prob = [c.sb(f"a_prob{u}", [TT, S]) for u in range(2)]
        probT = c.sb("a_probT", [CH, NC, TG])
        mxs = c.sb("a_mxs", [TT, PAIRS])
        lsum = c.sb("a_lsum", [TT, PAIRS])
        linv = c.sb("a_linv", [TT, PAIRS])
        lsel = c.sb("a_lsel", [TT, 4, 2, HD])
        lT = c.sb("a_lT", [P, L])
        picked = c.sb("a_picked", [P, HC, L])
        osum = c.sb("a_osum", [P, L])
        mraw = c.sb("a_mraw", [TT, PAIRS])
        s_bank = c.ps("a_s", [P, 3, 512])
        a_bank = [c.ps(f"a_a{i}", [P, 512]) for i in range(2)]
        p_bank = [c.ps(f"a_p{i}", [P, 512]) for i in range(2)]
        o_bank = c.ps("a_o", [P, 512])
        ctx_in = [c.sem(f"a_ctx_in{u}") for u in range(2)]
        q_made = c.sem("a_q_made")
        a_full = [c.sem(f"a_a_full{i}") for i in range(2)]
        a_read = [c.sem(f"a_a_read{i}") for i in range(2)]
        s_full, max_done, exp_done = c.sem("a_s_full"), c.sem("a_max"), c.sem("a_exp")
        p_full = [c.sem(f"a_p_full{i}") for i in range(2)]
        p_read = [c.sem(f"a_p_read{i}") for i in range(2)]
        linv_done, lsel_done = c.sem("a_linv_done"), c.sem("a_lsel_done")
        mraw_done = c.sem("a_mraw_done")
        o_full, lt_done, pick_done, sum_done, o_done = (c.sem(f"a_o_{m}") for m in ("full", "lt", "pick", "sum", "done"))
        block = ctx.enter_context(nc.Block())
        AN = len(A_ORDER) // 2

        def load(sp, b, u):
            v = a["ctx_2048"][bass.ds(b, 1), :, :].rearrange("b (p c) d -> p (b c) d", p=CH)
            sp.dma_start(ctx_sb[u][0:112, :, :], v[0:112, :, :]).then_inc(ctx_in[u], 16)
            sp.dma_start(ctx_sb[u][112:CH, :, :], v[112:CH, :, :]).then_inc(ctx_in[u], 16)

        @block.sync
        def _(sp):
            load(sp, 0, 0)
            load(sp, 1, 1)
            with sp.Fori(0, B // 2 - 1) as i:
                for u in range(2):
                    last_t = A_ORDER.index("T5")
                    sp.wait_ge(a_read[last_t % 2], AN * (2 * i + u) + last_t // 2 + 1)
                    load(sp, 2 * i + 2 + u, u)

        @block.gpsimd
        def _(pool):
            def spread(b, u, known):
                if not known or b >= 2:
                    pool.wait_ge(s_full, PAIRS * (b - 1))
                for k in range(KC):
                    q = K["phiqT"][:, k, bass.ds(b * L, L)]
                    pool.tensor_tensor(qbd[u][:, k, :, :], K["headmask"][:, :].rearrange("p (h n) -> p h n", h=HC),
                                       q.unsqueeze(1).to_broadcast([P, HC, L]), ALU.mult).then_inc(q_made, 1)

            spread(0, 0, True)
            spread(1, 1, True)
            with pool.Fori(1, B // 2) as i:
                spread(2 * i, 0, False)
                spread(2 * i + 1, 1, False)

        def evacuate(eng, b, u, w):
            at = A_ORDER.index(w)
            bank, nth = a_bank[at % 2], AN * b + at // 2 + 1
            eng.wait_ge(a_full[at % 2], nth)
            if w[0] == "T":
                g = int(w[1])
                ins = eng.copy(ctxT[:, :, g * CP * CH:(g + 1) * CP * CH],
                               bank[:, 0:KC * CP * CH].rearrange("p (k n) -> p k n", k=KC))
            elif w[0] == "K":
                k, g = int(w[1]), int(w[2])
                ins = eng.activation(keyT[u][:, k, g * GW:(g + 1) * GW], bank[:, 0:GW], ACT.Identity, bias=K["bk"][:, k:k + 1])
            else:
                g = int(w[1])
                ins = eng.tensor_copy(val[u][:, g * CP:(g + 1) * CP, :].rearrange("p c d -> p (c d)"), bank[0:CH, :])
            ins.then_inc(a_read[at % 2], 1)

        def p_evacuate(eng, copy, b, j, f):
            at = 3 * j + f
            eng.wait_ge(p_full[at % 2], 12 * b + at // 2 + 1)
            q = j % 4
            copy(probT[:, 4 * f:4 * f + 4, q * TT:(q + 1) * TT],
                 p_bank[at % 2][0:CH, 0:TG].rearrange("p (c n) -> p c n", c=4)).then_inc(p_read[at % 2], 1)

        @block.scalar
        def _(act):
            def pieces(b, u, slot):
                for w in A_PLAN[slot]:
                    if w[0] in "TK":
                        evacuate(act, b, u, w)

            def exp(b, j):
                act.wait_ge(max_done, PAIRS * b + j + 1)
                act.activation(prob[j % 2][:, :].rearrange("p (g n) -> p g n", g=KG), s_bank[0:TT, :, 0:GW], ACT.Exp,
                               bias=mxs[:, j:j + 1], scale=HD ** -0.5, accum_out=lsum[:, j:j + 1]).then_inc(exp_done, 1)

            def batch(b, u, first=False, last=False):
                for j in range(PAIRS):
                    if not last:
                        pieces(b + 1, 1 - u, j)
                    exp(b, j)
                    if j or not first:
                        p_evacuate(act, act.copy, b if j else b - 1, (j - 1) % PAIRS, 1)

            for slot in range(PAIRS):
                pieces(0, 0, slot)
            batch(0, 0, first=True)
            with act.Fori(0, B // 2 - 1) as i:
                batch(2 * i + 1, 1)
                batch(2 * i + 2, 0)
            batch(B - 1, 1, last=True)
            p_evacuate(act, act.copy, B - 1, PAIRS - 1, 1)

        @block.vector
        def _(dve):
            def pieces(b, u, slot):
                for w in A_PLAN[slot]:
                    if w[0] == "V":
                        evacuate(dve, b, u, w)

            def maximum(b, j):
                dve.wait_ge(s_full, PAIRS * b + j + 1)
                dve.tensor_reduce(mraw[:, j:j + 1], s_bank[0:TT, :, 0:GW], AX.XY, ALU.max, negate=True).then_inc(mraw_done, 1)
                dve.wait_ge(mraw_done, PAIRS * b + j + 1)
                dve.tensor_scalar(mxs[:, j:j + 1], mraw[:, j:j + 1], HD ** -0.5, None, ALU.mult).then_inc(max_done, 1)

            def select(b, g):
                dve.wait_ge(exp_done, PAIRS * b + 4 * g + 4)
                dve.reciprocal(linv[:, 4 * g:4 * g + 4], lsum[:, 4 * g:4 * g + 4]).then_inc(linv_done, 1)
                dve.wait_ge(linv_done, 2 * b + g + 1)
                dve.tensor_tensor(lsel[:, :, :, :], K["pairmask"][:, :].rearrange("p (j h e) -> p j h e", j=4, h=2),
                                  linv[:, 4 * g:4 * g + 4].unsqueeze(2).unsqueeze(3).to_broadcast([TT, 4, 2, HD]),
                                  ALU.mult).then_inc(lsel_done, 1)

            def outputs(b, g):
                nth = 2 * b + g + 1
                dve.wait_ge(o_full, nth)
                dve.tensor_copy(lT[:, :], o_bank[:, TG:TG + L]).then_inc(lt_done, 1)
                dve.tensor_tensor(picked[:, :, :].rearrange("p h n -> p (h n)"), o_bank[:, 0:TG], K["headmask"][:, :],
                                  ALU.mult).then_inc(pick_done, 1)
                dve.wait_ge(pick_done, nth)
                dve.tensor_reduce(osum[:, :], picked[:, :, :].rearrange("p h n -> p n h"), AX.X, ALU.add).then_inc(sum_done, 1)
                dve.wait_ge(sum_done, nth)
                dve.wait_ge(lt_done, nth)
                dve.tensor_tensor(K["attT"][:, g, bass.ds(b * L, L)], osum[:, :], lT[:, :], ALU.mult).then_inc(o_done, 1)

            def batch(b, u, first=False, last=False):
                for j in range(PAIRS):
                    if j == 4:
                        select(b, 0)
                    if j == 0 and not first:
                        select(b - 1, 1)
                    maximum(b, j)
                    if not last:
                        pieces(b + 1, 1 - u, j)
                    if j or not first:
                        for f in (0, 2):
                            p_evacuate(dve, dve.tensor_copy, b if j else b - 1, (j - 1) % PAIRS, f)
                    if j == 4:
                        outputs(b, 0)
                    if j == 0 and not first:
                        outputs(b - 1, 1)

            for slot in range(PAIRS):
                pieces(0, 0, slot)
            batch(0, 0, first=True)
            with dve.Fori(0, B // 2 - 1) as i:
                batch(2 * i + 1, 1)
                batch(2 * i + 2, 0)
            batch(B - 1, 1, last=True)
            select(B - 1, 1)
            for f in (0, 2):
                p_evacuate(dve, dve.tensor_copy, B - 1, PAIRS - 1, f)
            outputs(B - 1, 1)
            dve.wait_ge(o_done, 2 * B)
            for k in range(KC):
                dve.tensor_scalar(K["attT"][:, k, :], K["attT"][:, k, :], K["bv"][:, k:k + 1], None, ALU.add)

        @block.tensor
        def _(pe):
            def piece(b, n, u, w, known):
                at = A_ORDER.index(w)
                bank = a_bank[at % 2]
                if not known or at >= 2:
                    pe.wait_ge(a_read[at % 2], AN * b + at // 2)
                if w[0] == "T":
                    g = int(w[1])
                    if g == 0:
                        pe.wait_ge(ctx_in[u], 32 * (n + 1))
                    for k in range(KC):
                        for h in range(CP):
                            o = (k * CP + h) * CH
                            mm = pe.transpose(bank[:, o:o + CH], ctx_sb[u][:, g * CP + h, k * P:(k + 1) * P], K["ident"][0:CH, 0:CH])
                elif w[0] == "K":
                    k, g = int(w[1]), int(w[2])
                    need = A_ORDER.index(f"T{2 * g + 1}")
                    pe.wait_ge(a_read[need % 2], AN * b + need // 2 + 1)
                    pe.wait_ge(a_read[(need - 1) % 2], AN * b + (need - 1) // 2 + 1)
                    for i in range(KC):
                        mm = pe.matmul(bank[:, 0:GW], K["T_wk"][:, i, k * P:(k + 1) * P], ctxT[:, i, g * GW:(g + 1) * GW],
                                       start=(i == 0), stop=(i == KC - 1))
                else:
                    g = int(w[1])
                    need = A_ORDER.index(f"T{g}")
                    pe.wait_ge(a_read[need % 2], AN * b + need // 2 + 1)
                    for h in range(CP):
                        for i in range(KC):
                            o = (g * CP + h) * CH
                            mm = pe.matmul(bank[0:CH, h * D:(h + 1) * D], ctxT[:, i, o:o + CH], K["T_wv"][:, i, :],
                                           start=(i == 0), stop=(i == KC - 1))
                mm.then_inc(a_full[at % 2], 1)

            def scores(b, u, j, known):
                if j == 0:
                    pe.wait_ge(q_made, KC * (b + 1))
                    pe.wait_ge(a_read[0], AN * (b + 1))
                    pe.wait_ge(a_read[1], AN * (b + 1))
                if not known or PAIRS * b + j:
                    pe.wait_ge(exp_done, PAIRS * b + j)
                k, q = divmod(j, 4)
                for g in range(KG):
                    mm = pe.matmul(s_bank[0:TT, g, 0:GW], qbd[u][:, k, 2 * q:2 * q + 2, :].rearrange("p h n -> p (h n)"),
                                   keyT[u][:, k, g * GW:(g + 1) * GW], start=True, stop=True)
                mm.then_inc(s_full, 1)

            def turn(b, j, known):
                pe.wait_ge(exp_done, PAIRS * b + j + 1)
                for f in range(3):
                    at = 3 * j + f
                    if not known or 12 * b + at // 2:
                        pe.wait_ge(p_read[at % 2], 12 * b + at // 2)
                    for q in range(4):
                        ch = 4 * f + q
                        mm = pe.transpose(p_bank[at % 2][0:CH, q * TT:(q + 1) * TT], prob[j % 2][:, ch * CH:(ch + 1) * CH],
                                          K["ident"][0:TT, 0:TT])
                    mm.then_inc(p_full[at % 2], 1)

            def values(b, u, g, known):
                pe.wait_ge(p_read[0], 12 * b + 6 * (g + 1))
                pe.wait_ge(p_read[1], 12 * b + 6 * (g + 1))
                if not known or 2 * b + g:
                    pe.wait_ge(o_done, 2 * b + g)
                for ch in range(NC):
                    pe.matmul(o_bank[:, 0:TG], val[u][:, ch, g * P:(g + 1) * P], probT[:, ch, :],
                              start=(ch == 0), stop=(ch == NC - 1))
                pe.wait_ge(lsel_done, 2 * b + g + 1)
                pe.matmul(o_bank[:, TG:TG + L], lsel[:, :, :, :].rearrange("p j h e -> p (j h e)"), K["fold"][:, :],
                          start=True, stop=True).then_inc(o_full, 1)

            def batch(b, n, u, first=False, last=False):
                for j in range(PAIRS):
                    scores(b, u, j, first)
                    if not last:
                        for w in A_PLAN[j]:
                            piece(b + 1, n, 1 - u, w, False)
                    if j:
                        turn(b, j - 1, first)
                    elif not first:
                        turn(b - 1, PAIRS - 1, False)
                    if j == 4:
                        values(b, u, 0, first)
                    if j == 0 and not first:
                        values(b - 1, 1 - u, 1, False)

            for w in A_ORDER:
                piece(0, 0, 0, w, True)
            batch(0, 0, 0, first=True)
            with pe.Fori(0, B // 2 - 1) as i:
                batch(2 * i + 1, i + 1, 1)
                batch(2 * i + 2, i + 1, 0)
            batch(B - 1, 0, 1, last=True)
            turn(B - 1, PAIRS - 1, False)
            values(B - 1, 1, 1, False)


def attention_output(nc, a, K):
    with ExitStack() as ctx:
        c = Core(nc, ctx)
        o = c.sb("p_o", [TT, NT, D])
        oT = c.sb("p_oT", [P, KC, T])
        am, sc, iv = (c.sb(f"p_{m}", [TT, NT]) for m in ("am", "sc", "iv"))
        t_bank = [c.ps(f"p_t{i}", [P, 512]) for i in range(4)]
        q_bank = [c.ps(f"p_q{i}", [P, 512]) for i in range(4)]
        small, r_full, r_read, t_full, t_read, q_full, q_read = (
            c.sem(f"p_{m}") for m in ("small", "r_full", "r_read", "t_full", "t_read", "q_full", "q_read"))
        block = ctx.enter_context(nc.Block())

        @block.vector
        def _(dve):
            step = in_order(dve, small)
            for t in range(NT):
                dve.wait_ge(r_full, t + 1)
                dve.tensor_copy(o[:, t, :], q_bank[t % 4][0:TT, 0:D]).then_inc(r_read, 1)
            dve.wait_ge(r_read, NT)
            fake_quant(dve, step, o[:, :, :], o, am[:, :], sc[:, :], iv[:, :], NT)
            for g in range(NT // 2):
                dve.wait_ge(t_full, g + 1)
                dve.tensor_copy(oT[:, :, g * 2 * TT:(g + 1) * 2 * TT],
                                t_bank[g % 4][:, 0:TG].rearrange("p (k n) -> p k n", k=KC)).then_inc(t_read, 1)
            for t in range(NT):
                dve.wait_ge(q_full, t + 1)
                step(dve.tensor_tensor(o[:, t, :], q_bank[t % 4][0:TT, 0:D], K["bp"][:, :], ALU.add))
                dve.scalar_tensor_tensor(out=K["x"][:, t, :], in0=o[:, t, :], scalar=K["gate_tanh"][:, 1:2],
                                         in1=K["x"][:, t, :], op0=ALU.mult, op1=ALU.add).then_inc(q_read, 1)

        @block.tensor
        def _(pe):
            for t in range(NT):
                if t >= 4:
                    pe.wait_ge(r_read, t - 3)
                for k in range(KC):
                    mm = pe.transpose(q_bank[t % 4][0:TT, k * P:(k + 1) * P], K["attT"][:, k, t * TT:(t + 1) * TT], K["ident"][:, :])
                mm.then_inc(r_full, 1)
            for g in range(NT // 2):
                pe.wait_ge(small, 3 + 3 * (2 * g + 2))
                if g >= 4:
                    pe.wait_ge(t_read, g - 3)
                transpose_tiles(pe, t_bank[g % 4], o, g, K["ident"]).then_inc(t_full, 1)
            for t in range(NT):
                pe.wait_ge(t_read, t // 2 + 1)
                if t < 4:
                    pe.wait_ge(r_read, NT)
                else:
                    pe.wait_ge(q_read, t - 3)
                for i in range(KC):
                    mm = pe.matmul(q_bank[t % 4][0:TT, 0:D], oT[:, i, t * TT:(t + 1) * TT], K["T_wp"][:, i, :],
                                   start=(i == 0), stop=(i == KC - 1))
                mm.then_inc(q_full, 1)


def dequantise(nc, a, K):
    with ExitStack() as ctx:
        c = Core(nc, ctx)
        pk = [c.sb(f"w_pk{u}", [P, 8 * P], I32) for u in range(2)]
        scl = [c.sb(f"w_scl{u}", [P, 64]) for u in range(2)]
        nib = c.sb("w_nib", [P, 8 * P, 2], I32)
        mag = c.sb("w_mag", [P, 8 * P, 2], I32)
        v0, v1 = c.sb("w_v0", [P, 8 * P, 2]), c.sb("w_v1", [P, 8 * P, 2])
        W = [c.sb(f"w_W{u}", [P, 2 * 8 * P]) for u in range(2)]
        banks = [c.ps(f"w_b{i}", [P, 512]) for i in range(8)]
        w_in = [c.sem(f"w_in{u}") for u in range(2)]
        small, turned, full, emptied = c.sem("w_small"), c.sem("w_turned"), c.sem("w_full"), c.sem("w_emptied")
        jobs = []
        for name, dst in (("gate", "WgT"), ("up", "WuT")):
            for h in range(2):
                wv = a[f"L1_ffn_{name}_W_packed"].rearrange("(m p) k -> p m k", p=P)[:, 8 * h:8 * h + 8, :]
                sv = a[f"L1_ffn_{name}_scales"].rearrange("(m p) k -> p m k", p=P)[:, 8 * h:8 * h + 8, :]
                jobs.append((dst, h, wv, sv, 8))
        for h in range(2):
            wv = a["L1_ffn_down_W_packed"][h * P:(h + 1) * P, :].unsqueeze(1)
            sv = a["L1_ffn_down_scales"][h * P:(h + 1) * P, :].unsqueeze(1)
            jobs.append(("WdT", h, wv, sv, 1))
        NS = 11
        block = ctx.enter_context(nc.Block())

        @block.sync
        def _(sp):
            for n, (_, _, wv, sv, m) in enumerate(jobs):
                if n >= 2:
                    sp.wait_ge(small, NS * (n - 1))
                with nc.allow_non_contiguous_dma(reason="block scales, 8 to a row"):
                    sp.dma_start(pk[n % 2][:, :].rearrange("p (m k) -> p m k", m=m), wv).then_inc(w_in[n % 2], 16)
                    sp.dma_start(scl[n % 2][:, :].rearrange("p (m k) -> p m k", m=m), sv).then_inc(w_in[n % 2], 16)

        @block.vector
        def _(dve):
            step = in_order(dve, small)
            flat = lambda t: t[:, :, :].rearrange("p k e -> p (k e)")
            for n in range(len(jobs)):
                u = n % 2
                dve.wait_ge(w_in[u], 32 * (n // 2 + 1))
                step(dve.tensor_scalar(nib[:, :, 0], pk[u][:, :], 15, None, ALU.bitwise_and))
                step(dve.tensor_scalar(nib[:, :, 1], pk[u][:, :], 4, 15, ALU.logical_shift_right, ALU.bitwise_and))
                step(dve.tensor_scalar(flat(mag), flat(nib), 7, None, ALU.bitwise_and))
                step(dve.tensor_scalar(flat(v0), flat(mag), 2.0, -8.0, ALU.mult, ALU.add))
                step(dve.scalar_tensor_tensor(out=flat(v0), in0=flat(mag), scalar=-2.0, in1=flat(v0), op0=ALU.add, op1=ALU.max))
                step(dve.scalar_tensor_tensor(out=flat(v0), in0=flat(mag), scalar=0.5, in1=flat(v0), op0=ALU.mult, op1=ALU.max))
                step(dve.tensor_scalar(flat(v1), flat(nib), 8.0, -2.0, ALU.is_ge, ALU.mult))
                step(dve.tensor_scalar(flat(v1), flat(v1), 1.0, None, ALU.add))
                step(dve.tensor_tensor(flat(v0), flat(v0), flat(v1), ALU.mult))
                if n >= 2:
                    dve.wait_ge(full, 4 * (n - 1))
                step(dve.tensor_tensor(W[u][:, :].rearrange("p (s k) -> p s k", k=BLK),
                                       v0[:, :, :].rearrange("p k e -> p (k e)").rearrange("p (s k) -> p s k", k=BLK),
                                       scl[u][:, :].unsqueeze(2).to_broadcast([P, 64, BLK]), ALU.mult))
                step(dve.tensor_copy(v1[:, 0:1, 0:1], v0[:, 0:1, 0:1]))

        @block.scalar
        def _(act):
            for n, (dst, h, _, _, m) in enumerate(jobs):
                for f in range(4):
                    act.wait_ge(full, 4 * n + f + 1)
                    bank = banks[(4 * n + f) % 8]
                    if m == 8:
                        out = K[dst][:, :, (8 * h + 2 * f) * P:(8 * h + 2 * f + 2) * P]
                        act.copy(out, bank[:, :].rearrange("p (k n) -> p k n", k=KC)).then_inc(emptied, 1)
                    else:
                        out = K[dst][:, 4 * f:4 * f + 4, h * P:(h + 1) * P]
                        act.copy(out, bank[:, :].rearrange("p (m n) -> p m n", m=4)).then_inc(emptied, 1)

        @block.tensor
        def _(pe):
            for n, (dst, h, _, _, m) in enumerate(jobs):
                pe.wait_ge(small, NS * (n + 1))
                for f in range(4):
                    if 4 * n + f >= 8:
                        pe.wait_ge(emptied, 4 * n + f - 7)
                    bank = banks[(4 * n + f) % 8]
                    for q in range(4):
                        if m == 8:
                            k, r = divmod(q, 2)
                            src = W[n % 2][:, (2 * f + r) * D + k * P:(2 * f + r) * D + (k + 1) * P]
                        else:
                            src = W[n % 2][:, (4 * f + q) * P:(4 * f + q + 1) * P]
                        mm = pe.transpose(bank[:, q * P:(q + 1) * P], src, K["ident"][:, :])
                    mm.then_inc(full, 1)


def feed_forward(nc, a, out, K):
    with ExitStack() as ctx:
        c = Core(nc, ctx)
        xn = c.sb("f_xn", [TT, NT, D])
        xnT = c.sb("f_xnT", [P, KC, T])
        sq, tn, h1 = (c.sb(f"f_{m}", [P, 2, TG]) for m in ("sq", "tn", "h1"))
        hT = c.sb("f_hT", [P, 2, TG])
        g_bank = [c.ps(f"f_g{i}", [P, 512]) for i in range(2)]
        u_bank = [c.ps(f"f_u{i}", [P, 512]) for i in range(2)]
        d_bank = [c.ps(f"f_d{i}", [P, 512]) for i in range(4)]
        n = norm_buffers(c, "n3")
        t_full, t_read, g_full, u_full = (c.sem(f"f_{m}") for m in ("t_full", "t_read", "g_full", "u_full"))
        sq_done, cube_done, inner_done, tanh_done, half_done, gelu_done, h_done = (
            c.sem(f"f_{m}") for m in ("sq_done", "cube_done", "inner_done", "tanh_done", "half_done", "gelu_done", "h_done"))
        d_full, x_done, stored = c.sem("f_d_full"), c.sem("f_x_done"), c.sem("f_stored")
        block = ctx.enter_context(nc.Block())
        NS = NG * MC

        @block.gpsimd
        def _(pool):
            norm_pool(pool, n)
            for s in range(NS):
                pool.wait_ge(sq_done, s + 1)
                pool.tensor_scalar(sq[:, s % 2, :], sq[:, s % 2, :], 0.044715, 1.0, ALU.mult, ALU.add).then_inc(cube_done, 1)
                if s:
                    pool.wait_ge(tanh_done, s)
                    pool.tensor_scalar(tn[:, (s - 1) % 2, :], tn[:, (s - 1) % 2, :], 1.0, 0.5, ALU.add, ALU.mult).then_inc(half_done, 1)
            pool.wait_ge(tanh_done, NS)
            pool.tensor_scalar(tn[:, (NS - 1) % 2, :], tn[:, (NS - 1) % 2, :], 1.0, 0.5, ALU.add, ALU.mult).then_inc(half_done, 1)

        @block.scalar
        def _(act):
            def square(s):
                act.wait_ge(g_full, s + 1)
                if s >= 2:
                    act.wait_ge(inner_done, s - 1)
                act.activation(sq[:, s % 2, :], g_bank[s % 2][:, 0:TG], ACT.Square).then_inc(sq_done, 1)

            def tanh(s):
                act.wait_ge(inner_done, s + 1)
                if s >= 2:
                    act.wait_ge(gelu_done, s - 1)
                act.activation(tn[:, s % 2, :], sq[:, s % 2, :], ACT.Tanh, scale=0.7978845608028654).then_inc(tanh_done, 1)

            square(0)
            for s in range(NS):
                tanh(s)
                if s + 1 < NS:
                    square(s + 1)

        @block.vector
        def _(dve):
            norm_vector(dve, n, K["x"], xn)
            for g in range(NT // 2):
                dve.wait_ge(t_full, g + 1)
                dve.tensor_copy(xnT[:, :, g * 2 * TT:(g + 1) * 2 * TT],
                                g_bank[g % 2][:, 0:TG].rearrange("p (k n) -> p k n", k=KC)).then_inc(t_read, 1)

            def inner(s):
                dve.wait_ge(cube_done, s + 1)
                dve.tensor_tensor(sq[:, s % 2, :], sq[:, s % 2, :], g_bank[s % 2][:, 0:TG], ALU.mult).then_inc(inner_done, 1)

            def product(s):
                dve.wait_ge(half_done, s + 1)
                dve.tensor_tensor(h1[:, s % 2, :], tn[:, s % 2, :], g_bank[s % 2][:, 0:TG], ALU.mult).then_inc(gelu_done, 1)
                dve.wait_ge(gelu_done, s + 1)
                dve.wait_ge(u_full, s + 1)
                if s >= 2:
                    dve.wait_ge(d_full, s - 1)
                dve.tensor_tensor(hT[:, s % 2, :], h1[:, s % 2, :], u_bank[s % 2][:, 0:TG], ALU.mult).then_inc(h_done, 1)

            def result(g):
                dve.wait_ge(d_full, MC * (g + 1))
                for q in range(4):
                    t = 4 * g + q
                    dve.scalar_tensor_tensor(out=K["x"][:, t, :], in0=d_bank[q][0:TT, 0:D], scalar=K["gate_tanh"][:, 3:4],
                                             in1=K["x"][:, t, :], op0=ALU.mult, op1=ALU.add).then_inc(x_done, 1)

            for s in range(NS):
                inner(s)
                product(s)
                if s and s % MC == 0:
                    result(s // MC - 1)
            result(NG - 1)

        @block.tensor
        def _(pe):
            for g in range(NT // 2):
                pe.wait_ge(n["xn_done"], 2 * g + 2)
                if g >= 2:
                    pe.wait_ge(t_read, g - 1)
                transpose_tiles(pe, g_bank[g % 2], xn, g, K["ident"]).then_inc(t_full, 1)
            pe.wait_ge(t_read, NT // 2)

            def up(s):
                g, m = divmod(s, MC)
                if s >= 2:
                    pe.wait_ge(h_done, s - 1)
                for bank, w, done in ((g_bank, "WgT", g_full), (u_bank, "WuT", u_full)):
                    for i in range(KC):
                        mm = pe.matmul(bank[s % 2][:, 0:TG], K[w][:, i, m * P:(m + 1) * P], xnT[:, i, g * TG:(g + 1) * TG],
                                       start=(i == 0), stop=(i == KC - 1))
                    mm.then_inc(done, 1)

            def down(s):
                g, m = divmod(s, MC)
                pe.wait_ge(h_done, s + 1)
                if m == 0 and g:
                    pe.wait_ge(x_done, 4 * g)
                for q in range(4):
                    mm = pe.matmul(d_bank[q][0:TT, 0:D], hT[:, s % 2, q * TT:(q + 1) * TT], K["WdT"][:, m, :],
                                   start=(m == 0), stop=(m == MC - 1))
                mm.then_inc(d_full, 1)

            up(0)
            for s in range(NS):
                if s + 1 < NS:
                    up(s + 1)
                down(s)

        @block.sync
        def _(sp):
            y = out.rearrange("b l d -> (b l) d").rearrange("(t p) d -> p t d", p=TT)
            for g in range(NG):
                sp.wait_ge(x_done, 4 * (g + 1))
                sp.dma_start(y[:, 4 * g:4 * g + 4, :], K["x"][:, 4 * g:4 * g + 4, :]).then_inc(stored, 16)
            sp.wait_ge(stored, 16 * NG)


def build(nc, a, out):
    with ExitStack() as ctx:
        c = Core(nc, ctx)
        K = {
            "x": c.sb("x", [TT, NT, D]), "attT": c.sb("attT", [P, KC, T]),
            "ident": c.sb("ident", [P, P]), "headmask": c.sb("headmask", [P, TG]), "blockmask": c.sb("blockmask", [P, P]),
            "pairmask": c.sb("pairmask", [TT, P]), "fold": c.sb("fold", [TT, L]),
            "gates": c.sb("gates", [TT, 5]), "gate_tanh": c.sb("gate_tanh", [TT, 4]), "bp": c.sb("bp", [TT, D]),
        }
        for m in ("bg", "bq", "bk", "bv"):
            K[m] = c.sb(m, [P, KC])
        for m in ("Wq", "Wg", "Wk", "Wv", "Wo", "wq", "wk", "wv", "wp"):
            K["T_" + m] = c.sb("T_" + m, [P, KC, D])
        with ExitStack() as scope:
            K["phiqT"] = scope.enter_context(nc.sbuf_tensor("phiqT", [P, KC, T], F32))
            with ExitStack() as inner:
                K["gateT"] = inner.enter_context(nc.sbuf_tensor("gateT", [P, KC, T], F32))
                setup(nc, a, K)
                linear_attention(nc, a, K)
            experts(nc, a, K)
            queries(nc, a, K)
            softmax_attention(nc, a, K)
        attention_output(nc, a, K)
        with ExitStack() as scope:
            K["WgT"] = scope.enter_context(nc.sbuf_tensor("WgT", [P, KC, M], F32))
            K["WuT"] = scope.enter_context(nc.sbuf_tensor("WuT", [P, KC, M], F32))
            K["WdT"] = scope.enter_context(nc.sbuf_tensor("WdT", [P, MC, D], F32))
            dequantise(nc, a, K)
            feed_forward(nc, a, out, K)


_INS = ["x", "ctx_2048", "g_xattn", "g_ffn", "L0_xattn_Wq", "L0_xattn_Wg", "L0_xattn_bg", "L0_xattn_Wkv", "L0_xattn_Wo",
        "L0_ffn_gate_w", "L0_ffn_w_gate_up", "L0_ffn_w_down", "L0_ffn_shared_gate_up", "L0_ffn_shared_down",
        "L1_xattn_wq", "L1_xattn_bq", "L1_xattn_wkv", "L1_xattn_bkv", "L1_xattn_wp", "L1_xattn_bp",
        "L1_ffn_gate_W_packed", "L1_ffn_gate_scales", "L1_ffn_up_W_packed", "L1_ffn_up_scales",
        "L1_ffn_down_W_packed", "L1_ffn_down_scales"]


def kernel(**inputs):
    import concourse.bacc as bacc
    from concourse.bass_utils import run_bass_kernel_spmd

    nc = bacc.Bacc("TRN2", target_bir_lowering=False, num_devices=1)
    arrays, a = {}, {}
    for name in _INS:
        v = np.ascontiguousarray(inputs[name])
        arrays[f"in_{name}"] = v
        a[name] = nc.dram_tensor(f"in_{name}", v.shape, mybir.dt.from_np(v.dtype), kind="ExternalInput").ap()
    out = nc.dram_tensor("out", (B, L, D), F32, kind="ExternalOutput").ap()
    build(nc, a, out)
    r = run_bass_kernel_spmd(nc, [arrays], core_ids=[0])
    return r.results[0]["out"]
```

```python
from contextlib import ExitStack

import numpy as np

import concourse.bass as bass
from concourse import mybir

F32 = mybir.dt.float32
F32R = mybir.dt.float32r
I32 = mybir.dt.int32
ALU = mybir.AluOpType
ACT = mybir.ActivationFunctionType
AX = mybir.AxisListType

B, L, D, S = 32, 56, 256, 1500
H, HD = 16, 16
P = 128
KC = D // P
HC = P // HD
T = B * L
TT = 2 * L
NT = T // TT
TG = 4 * TT
NG = T // TG
CH = 125
NC = S // CH
CP = 2
NP = NC // CP
CW = D + 4
E, I = 8, 512
IC = I // P
M, MC = 2048, 2048 // P
BLK = 32
MAGIC = 12582912.0
PAIRS = H // 2


class Parts:

    def __init__(self, hi, lo):
        self.hi, self.lo = hi, lo

    def at(self, *index):
        return Parts(self.hi[index], self.lo[index])


def matmul_parts(pe, out, pairs, start=True, stop=True):
    for n, (a, b) in enumerate(pairs):
        passes = ((a.hi, b.lo), (a.hi, b.hi), (a.lo, b.hi))
        for m, (lhs, rhs) in enumerate(passes):
            mm = pe.matmul(out, lhs, rhs, start=(start and n == 0 and m == 0),
                           stop=(stop and n == len(pairs) - 1 and m == 2))
    return mm


class Core:

    def __init__(self, nc, ctx):
        self.nc, self.ctx = nc, ctx

    def sb(self, name, shape, dt=F32):
        return self.ctx.enter_context(self.nc.sbuf_tensor(name, shape, dt))

    def parts(self, name, shape):
        return Parts(self.sb(name + "_hi", shape, F32R), self.sb(name + "_lo", shape, F32R))

    def ps(self, name, shape):
        return self.ctx.enter_context(self.nc.psum_tensor(name, shape, F32))

    def sem(self, name):
        return self.ctx.enter_context(self.nc.semaphore(name))


def in_order(eng, sem):
    count = [0]

    def step(ins):
        count[0] += 1
        ins.then_inc(sem, 1)
        eng.wait_ge(sem, count[0])

    return step


def norm_buffers(c, tag):
    return {
        "stats": c.sb(f"{tag}_stats", [TT, NT, 6]), "mv": c.sb(f"{tag}_mv", [TT, NT, 2]),
        "var": c.sb(f"{tag}_var", [TT, NT]), "rstd": c.sb(f"{tag}_rstd", [TT, NT]),
        "half": c.sb(f"{tag}_half", [TT, NT]),
        "stats_done": c.sem(f"{tag}_stats_done"), "mv_done": c.sem(f"{tag}_mv_done"),
        "var_done": c.sem(f"{tag}_var_done"), "half_set": c.sem(f"{tag}_half_set"),
        "rstd_done": c.sem(f"{tag}_rstd_done"), "xn_done": c.sem(f"{tag}_xn_done"),
    }


def norm_vector(dve, n, x, xn):
    for t in range(NT):
        dve.bn_stats(out=n["stats"][:, t, :], in_=x[:, t, :]).then_inc(n["stats_done"], 1)
    for t in range(NT):
        dve.wait_ge(n["stats_done"], t + 1)
        dve.bn_aggr(out=n["mv"][:, t, :], in_=n["stats"][:, t, :]).then_inc(n["mv_done"], 1)
    dve.wait_ge(n["mv_done"], NT)
    dve.tensor_scalar(n["var"][:, :], n["mv"][:, :, 1], 1e-5, None, ALU.add).then_inc(n["var_done"], 1)
    dve.wait_ge(n["rstd_done"], 1)
    for t in range(NT):
        dve.tensor_scalar(xn[:, t, :], x[:, t, :], n["mv"][:, t, 0:1], n["rstd"][:, t:t + 1],
                          ALU.subtract, ALU.mult).then_inc(n["xn_done"], 1)


def norm_pool(pool, n):
    pool.memset(n["half"][:, :], -0.5).then_inc(n["half_set"], 1)
    pool.wait_ge(n["half_set"], 1)
    pool.wait_ge(n["var_done"], 1)
    pool.tensor_tensor(n["rstd"][:, :], n["var"][:, :], n["half"][:, :], ALU.pow).then_inc(n["rstd_done"], 1)


def fake_quant(dve, step, src, out, absmax, scale, inverse, n):
    step(dve.tensor_reduce(absmax, src, AX.X, ALU.max, apply_absolute_value=True))
    step(dve.tensor_scalar(scale, absmax, 1.0 / 127.0, 1e-8, ALU.mult, ALU.max))
    step(dve.reciprocal(inverse, scale))
    for k in range(n):
        step(dve.tensor_scalar(out[:, k, :], src[:, k, :], inverse[:, k:k + 1], MAGIC, ALU.mult, ALU.add))
        step(dve.tensor_scalar(out[:, k, :], out[:, k, :], MAGIC, 127.0, ALU.subtract, ALU.min))
        step(dve.tensor_scalar(out[:, k, :], out[:, k, :], -127.0, scale[:, k:k + 1], ALU.max, ALU.mult))


def transpose_tiles(pe, bank, src, g, ident):
    for k in range(KC):
        for h in range(2):
            at = k * 2 * TT + h * TT
            mm = pe.transpose(bank[:, at:at + TT], src[:, 2 * g + h, k * P:(k + 1) * P], ident[0:TT, 0:TT])
    return mm


def setup(nc, a, K):
    with ExitStack() as ctx:
        c = Core(nc, ctx)
        names = ["Wq", "Wg", "Wk", "Wv", "Wo", "wq", "wk", "wv", "wp"]
        raw = {n: c.sb(f"raw_{n}", [P, KC, D]) for n in names}
        xn = c.sb("s_xn", [TT, NT, D])
        xnT = c.sb("s_xnT", [P, KC, T])
        expq = c.sb("s_expq", [P, 8, TG])
        am, sc, iv = (c.sb(f"s_{n}", [P, 2, KC]) for n in ("am", "sc", "iv"))
        banks = [c.ps(f"s_bank{i}", [P, 512]) for i in range(8)]
        n = norm_buffers(c, "n0")
        x_in, w_in, v_in = c.sem("x_in"), [c.sem(f"w_in_{m}") for m in names], c.sem("v_in")
        zeroed, ones_set, masks_set = c.sem("zeroed"), c.sem("ones_set"), c.sem("masks_set")
        full, emptied, quant = c.sem("s_full"), c.sem("s_emptied"), c.sem("s_quant")
        exp_done, min_done, phi_done = c.sem("s_exp"), c.sem("s_min"), c.sem("s_phi")
        gate_done, quant_done, tanh_done = c.sem("s_gate"), c.sem("s_quantised"), c.sem("s_tanh")
        src = {
            "Wq": a["L0_xattn_Wq"], "Wg": a["L0_xattn_Wg"], "Wk": a["L0_xattn_Wkv"][0:D, :],
            "Wv": a["L0_xattn_Wkv"][D:2 * D, :], "Wo": a["L0_xattn_Wo"], "wq": a["L1_xattn_wq"],
            "wk": a["L1_xattn_wkv"][0:D, :], "wv": a["L1_xattn_wkv"][D:2 * D, :], "wp": a["L1_xattn_wp"],
        }
        NW, NX = len(names), NT // 2
        order = ["Wq", "Wg", "Wk", "Wv", "Wo", "wk", "wv", "wq", "wp"]
        block = ctx.enter_context(nc.Block())

        @block.sync
        def _(sp):
            sp.dma_start(K["x"][:, :, :], a["x"].rearrange("b l d -> (b l) d").rearrange("(t p) d -> p t d", p=TT)).then_inc(x_in, 16)
            for m, s in zip(names, w_in):
                sp.dma_start(raw[m][:, :, :], src[m].rearrange("(o p) i -> p o i", p=P)).then_inc(s, 16)
            sp.wait_ge(v_in, 16 * 8)

        @block.scalar
        def _(act):
            with nc.allow_non_contiguous_dma(reason="biases, one value to a partition"):
                for t, v in (("bg", a["L0_xattn_bg"]), ("bq", a["L1_xattn_bq"]),
                             ("bk", a["L1_xattn_bkv"][0:D]), ("bv", a["L1_xattn_bkv"][D:2 * D])):
                    act.dma_start(K[t][:, :], v.rearrange("(o p) -> p o", p=P)).then_inc(v_in, 16)
                act.dma_start(K["bp"][:, :], a["L1_xattn_bp"].partition_broadcast(TT)).then_inc(v_in, 16)
                act.dma_start(K["gates"][:, 0:2], a["g_xattn"].partition_broadcast(TT)).then_inc(v_in, 16)
                act.dma_start(K["gates"][:, 2:4], a["g_ffn"].partition_broadcast(TT)).then_inc(v_in, 16)
                act.dma_start(K["gates"][:, 4:5], a["g_ffn"][0:1].partition_broadcast(TT)).then_inc(v_in, 16)
            act.wait_ge(v_in, 16 * 8)
            act.activation(K["gate_tanh"][:, :], K["gates"][:, 0:4], ACT.Tanh).then_inc(tanh_done, 1)
            for q in range(8):
                act.wait_ge(full, NW + NX + q + 1)
                act.activation(expq[:, q, :], banks[(NW + NX + q) % 8][:, 0:TG], ACT.Exp).then_inc(exp_done, 1)
            for q in range(8):
                k, g = divmod(q, NG)
                act.wait_ge(full, NW + NX + 8 + q + 1)
                act.activation(K["gateT"][:, k, g * TG:(g + 1) * TG], banks[(NW + NX + 8 + q) % 8][:, 0:TG],
                               ACT.Sigmoid, bias=K["bg"][:, k:k + 1]).then_inc(gate_done, 1)

        @block.gpsimd
        def _(pool):
            pool.memset(K["ident"][:, :], 0.0).then_inc(zeroed, 1)
            pool.memset(K["headmask"][:, :], 1.0).then_inc(ones_set, 1)
            pool.memset(K["pairmask"][:, :], 1.0).then_inc(ones_set, 1)
            pool.memset(K["fold"][:, :], 0.0).then_inc(zeroed, 1)
            pool.wait_ge(zeroed, 2)
            pool.affine_select(out=K["ident"][:, :], in_=K["ident"][:, :], compare_op=ALU.not_equal, fill=1.0,
                               base=0, pattern=[[-1, P]], channel_multiplier=1).then_inc(masks_set, 1)
            pool.wait_ge(ones_set, 2)
            hm = K["headmask"][:, :].rearrange("p (h n) -> p h n", h=HC)
            pool.affine_select(out=hm, in_=hm, compare_op=ALU.is_ge, fill=0.0, base=0,
                               pattern=[[-HD, HC], [0, L]], channel_multiplier=1).then_inc(masks_set, 1)
            pool.wait_ge(masks_set, 2)
            pool.affine_select(out=hm, in_=hm, compare_op=ALU.is_ge, fill=0.0, base=HD - 1,
                               pattern=[[HD, HC], [0, L]], channel_multiplier=-1).then_inc(masks_set, 1)
            pool.wait_ge(masks_set, 3)
            pool.tensor_copy(K["blockmask"][:, :].rearrange("p (h e) -> p h e", h=HC), hm[:, :, 0:HD]).then_inc(masks_set, 1)
            pm = K["pairmask"][:, :].rearrange("p (j h e) -> p j h e", j=4, h=2)
            pool.affine_select(out=pm[:, :, 0, :], in_=pm[:, :, 0, :], compare_op=ALU.is_ge, fill=0.0, base=L - 1,
                               pattern=[[0, 4], [0, HD]], channel_multiplier=-1).then_inc(masks_set, 1)
            pool.affine_select(out=pm[:, :, 1, :], in_=pm[:, :, 1, :], compare_op=ALU.is_ge, fill=0.0, base=-L,
                               pattern=[[0, 4], [0, HD]], channel_multiplier=1).then_inc(masks_set, 1)
            pool.affine_select(out=K["fold"][:, :], in_=K["fold"][:, :], compare_op=ALU.not_equal, fill=1.0,
                               base=0, pattern=[[-1, L]], channel_multiplier=1).then_inc(masks_set, 1)
            pool.wait_ge(masks_set, 7)
            pool.affine_select(out=K["fold"][:, :], in_=K["fold"][:, :], compare_op=ALU.not_equal, fill=1.0,
                               base=-L, pattern=[[-1, L]], channel_multiplier=1).then_inc(masks_set, 1)
            norm_pool(pool, n)
            for q in range(8):
                pool.wait_ge(exp_done, q + 1)
                pool.tensor_scalar(expq[:, q, :], expq[:, q, :], 1.0, 0.0, ALU.min, ALU.max).then_inc(min_done, 1)

        @block.vector
        def _(dve):
            step = in_order(dve, quant)
            dve.wait_ge(x_in, 16)
            norm_vector(dve, n, K["x"], xn)
            for i, m in enumerate(("wq", "wp")):
                dve.wait_ge(w_in[names.index(m)], 16)
                fake_quant(dve, step, raw[m][:, :, :], raw[m], am[:, i, :], sc[:, i, :], iv[:, i, :], KC)
            for i, m in enumerate(order):
                dve.wait_ge(full, i + 1)
                dve.tensor_copy(K["T_" + m][:, :, :].rearrange("p k o -> p (k o)"), banks[i % 8][:, :]).then_inc(emptied, 1)
            for g in range(NX):
                dve.wait_ge(full, NW + g + 1)
                dve.tensor_copy(xnT[:, :, g * 2 * TT:(g + 1) * 2 * TT],
                                banks[(NW + g) % 8][:, 0:TG].rearrange("p (k n) -> p k n", k=KC)).then_inc(emptied, 1)
            for q in range(8):
                k, g = divmod(q, NG)
                dve.wait_ge(min_done, q + 1)
                dve.scalar_tensor_tensor(out=K["phiqT"][:, k, g * TG:(g + 1) * TG], in0=banks[(NW + NX + q) % 8][:, 0:TG],
                                         scalar=0.0, in1=expq[:, q, :], op0=ALU.max, op1=ALU.add).then_inc(phi_done, 1)

        @block.tensor
        def _(pe):
            pe.wait_ge(masks_set, 1)
            for i, m in enumerate(order):
                pe.wait_ge(w_in[names.index(m)], 16)
                if m in ("wq", "wp"):
                    pe.wait_ge(quant, (3 + 3 * KC) * (1 + ("wq", "wp").index(m)))
                if i >= 8:
                    pe.wait_ge(emptied, i - 7)
                for k in range(KC):
                    for o in range(KC):
                        mm = pe.transpose(banks[i % 8][:, (k * KC + o) * P:(k * KC + o + 1) * P],
                                          raw[m][:, o, k * P:(k + 1) * P], K["ident"][:, :])
                mm.then_inc(full, 1)
            for g in range(NX):
                pe.wait_ge(n["xn_done"], 2 * g + 2)
                pe.wait_ge(emptied, NW + g - 7)
                transpose_tiles(pe, banks[(NW + g) % 8], xn, g, K["ident"]).then_inc(full, 1)
            pe.wait_ge(emptied, NW + NX)
            for which, w in enumerate(("T_Wq", "T_Wg")):
                for q in range(8):
                    k, g = divmod(q, NG)
                    if which:
                        pe.wait_ge(phi_done, q + 1)
                    for i in range(KC):
                        mm = pe.matmul(banks[(NW + NX + 8 * which + q) % 8][:, 0:TG], K[w][:, i, k * P:(k + 1) * P],
                                       xnT[:, i, g * TG:(g + 1) * TG], start=(i == 0), stop=(i == KC - 1))
                    mm.then_inc(full, 1)


def linear_attention(nc, a, K):
    with ExitStack() as ctx:
        c = Core(nc, ctx)
        raw = [c.sb(f"l_raw{u}", [CH, NC, D]) for u in range(2)]
        rows = c.parts("l_rows", [CH, NC, CW])
        ctxT = c.parts("l_ctxT", [P, KC, S])
        phik = c.parts("l_phik", [CH, NC, D])
        wk = c.parts("l_wk", [P, KC, D])
        phif = c.sb("l_phif", [CH, 2, CP * D])
        expk = c.sb("l_expk", [CH, 2, CP * D])
        G = c.sb("l_G", [P, KC, D + 1])
        GT = c.sb("l_GT", [P, KC, D])
        KV = c.sb("l_KV", [P, KC, P])
        KS = c.sb("l_KS", [P, KC, P])
        den = c.sb("l_den", [P, KC, L])
        rden = c.sb("l_rden", [P, KC, L])
        t_bank = [c.ps(f"l_t{i}", [P, 512]) for i in range(2)]
        k_bank = [c.ps(f"l_k{i}", [P, 512]) for i in range(2)]
        g_bank = [c.ps(f"l_g{i}", [P, 512]) for i in range(KC)]
        gt_bank, s_bank = c.ps("l_gt", [P, 512]), c.ps("l_s", [P, 512])
        nd = s_bank[:, 256:256 + 4 * L].rearrange("p (k w n) -> p k w n", k=KC, w=2)
        ones_set, wk_hi, wk_done = c.sem("l_ones"), c.sem("l_wk_hi"), c.sem("l_wk_done")
        raw_in = [c.sem(f"l_raw_in{u}") for u in range(2)]
        rows_hi, rows_lo = c.sem("l_rows_hi"), c.sem("l_rows_lo")
        t_full, t_hi, t_lo = c.sem("l_t_full"), c.sem("l_t_hi"), c.sem("l_t_lo")
        k_full, min_done, exp_done, phi_done = c.sem("l_k_full"), c.sem("l_min"), c.sem("l_exp"), c.sem("l_phi")
        phi_hi, phi_lo = c.sem("l_phi_hi"), c.sem("l_phi_lo")
        g_part, g_read = c.sem("l_g_part"), c.sem("l_g_read")
        gt_full, gt_read = c.sem("l_gt_full"), c.sem("l_gt_read")
        kv_full, kv_read = c.sem("l_kv_full"), c.sem("l_kv_read")
        nd_full, den_eps, den_inv, nd_read = c.sem("l_nd_full"), c.sem("l_den_eps"), c.sem("l_den_inv"), c.sem("l_nd_read")
        block = ctx.enter_context(nc.Block())
        flat = lambda t: t.rearrange("p c d -> p (c d)")

        def load(sp, b, u):
            v = a["ctx_2048"][bass.ds(b, 1), :, :].rearrange("b (p c) d -> p (b c) d", p=CH)
            sp.dma_start(raw[u][0:112, :, :], v[0:112, :, :]).then_inc(raw_in[u], 16)
            sp.dma_start(raw[u][112:CH, :, :], v[112:CH, :, :]).then_inc(raw_in[u], 16)

        @block.sync
        def _(sp):
            load(sp, 0, 0)
            load(sp, 1, 1)
            with sp.Fori(0, B // 2 - 1) as i:
                for u in range(2):
                    sp.wait_ge(t_full, NP * (2 * i + u + 1))
                    sp.wait_ge(rows_lo, NP * (2 * i + u + 1))
                    load(sp, 2 * i + 2 + u, u)

        @block.gpsimd
        def _(pool):
            pool.memset(rows.hi[:, :, D:CW].bitcast(F32), 1.0).then_inc(ones_set, 1)
            pool.memset(rows.lo[:, :, D:CW].bitcast(F32), 0.0).then_inc(ones_set, 1)
            pool.wait_ge(wk_hi, 1)
            pool.tensor_tensor(wk.lo[:, :, :], K["T_Wk"][:, :, :], wk.hi[:, :, :].bitcast(F32), ALU.subtract).then_inc(wk_done, 1)

            def batch(b, u):
                for g in range(NP):
                    sl = slice(g * CP, (g + 1) * CP)
                    pool.wait_ge(rows_hi, NP * b + g + 1)
                    pool.tensor_tensor(rows.lo[:, sl, 0:D], raw[u][:, sl, :], rows.hi[:, sl, 0:D].bitcast(F32),
                                       ALU.subtract).then_inc(rows_lo, 1)
                    pool.wait_ge(phi_hi, NP * b + g + 1)
                    pool.tensor_tensor(flat(phik.lo[:, sl, :]), phif[:, g % 2, :], flat(phik.hi[:, sl, :]).bitcast(F32),
                                       ALU.subtract).then_inc(phi_lo, 1)

            with pool.Fori(0, B // 2) as i:
                batch(2 * i, 0)
                batch(2 * i + 1, 1)

        @block.scalar
        def _(act):
            act.copy(wk.hi[:, :, :], K["T_Wk"][:, :, :]).then_inc(wk_hi, 1)

            def t_copy(b, g):
                act.wait_ge(t_full, NP * b + g + 1)
                act.copy(ctxT.hi[:, :, g * CP * CH:(g + 1) * CP * CH],
                         t_bank[g % 2][:, 0:KC * CP * CH].rearrange("p (k n) -> p k n", k=KC)).then_inc(t_hi, 1)

            def batch(b, n, u, first=False, last=False):
                for g in range(NP):
                    if g + 2 < NP:
                        t_copy(b, g + 2)
                    elif not last:
                        t_copy(b + 1, g + 2 - NP)
                    if g == 4 and not first:
                        act.wait_ge(gt_full, b)
                        act.copy(flat(GT[:, :, :]), gt_bank[:, :]).then_inc(gt_read, 1)
                    act.wait_ge(min_done, NP * b + g + 1)
                    act.activation(expk[:, g % 2, :], expk[:, g % 2, :], ACT.Exp).then_inc(exp_done, 1)
                    if g == 0:
                        act.wait_ge(raw_in[u], 32 * (n + 1))
                    if not first:
                        act.wait_ge(g_part, NP * b - NP + g + 1)
                    act.copy(rows.hi[:, g * CP:(g + 1) * CP, 0:D], raw[u][:, g * CP:(g + 1) * CP, :]).then_inc(rows_hi, 1)
                    act.wait_ge(phi_done, NP * b + g + 1)
                    act.copy(flat(phik.hi[:, g * CP:(g + 1) * CP, :]), phif[:, g % 2, :]).then_inc(phi_hi, 1)

            t_copy(0, 0)
            t_copy(0, 1)
            batch(0, 0, 0, first=True)
            with act.Fori(0, B // 2 - 1) as i:
                batch(2 * i + 1, i, 1)
                batch(2 * i + 2, i + 1, 0)
            batch(B - 1, B // 2 - 1, 1, last=True)
            act.wait_ge(gt_full, B)
            act.copy(flat(GT[:, :, :]), gt_bank[:, :]).then_inc(gt_read, 1)

        @block.vector
        def _(dve):
            def g_copy(b):
                dve.wait_ge(g_part, NP * (b + 1))
                for k in range(KC):
                    dve.tensor_copy(G[:, k, :], g_bank[k][:, 0:D + 1]).then_inc(g_read, 1)

            def kv_copy(b):
                dve.wait_ge(kv_full, b + 1)
                dve.tensor_tensor(KV[:, :, :], s_bank[:, 0:D].rearrange("p (k e) -> p k e", k=KC),
                                  K["blockmask"][:, :].unsqueeze(1).to_broadcast([P, KC, P]), ALU.mult).then_inc(kv_read, 1)
                for k in range(KC):
                    dve.tensor_scalar(KS[:, k, :], K["blockmask"][:, :], G[:, k, D:D + 1], None, ALU.mult).then_inc(kv_read, 1)

            def nd_use(b):
                dve.wait_ge(nd_full, b + 1)
                dve.tensor_scalar(den[:, :, :], nd[:, :, 1, :], 1e-6, None, ALU.add).then_inc(den_eps, 1)
                dve.wait_ge(den_eps, b + 1)
                dve.reciprocal(rden[:, :, :], den[:, :, :]).then_inc(den_inv, 1)
                dve.wait_ge(den_inv, b + 1)
                dve.tensor_tensor(K["attT"][:, :, bass.ds(b * L, L)], nd[:, :, 0, :], rden[:, :, :], ALU.mult).then_inc(nd_read, 1)

            def t_low(b, g):
                dve.wait_ge(t_hi, NP * b + g + 1)
                cols = slice(g * CP * CH, (g + 1) * CP * CH)
                dve.tensor_tensor(ctxT.lo[:, :, cols], t_bank[g % 2][:, 0:KC * CP * CH].rearrange("p (k n) -> p k n", k=KC),
                                  ctxT.hi[:, :, cols].bitcast(F32), ALU.subtract).then_inc(t_lo, 1)

            def batch(b, first=False, last=False):
                for g in range(NP):
                    if g == 3 and not first:
                        g_copy(b - 1)
                    if g == 5 and not first:
                        kv_copy(b - 1)
                    dve.wait_ge(k_full, NP * b + g + 1)
                    if g >= 2 or not first:
                        dve.wait_ge(phi_done, NP * b + g - 1)
                    dve.tensor_scalar(expk[:, g % 2, :], k_bank[g % 2][0:CH, :], 0.0, None, ALU.min).then_inc(min_done, 1)
                    if g + 2 < NP:
                        t_low(b, g + 2)
                    elif not last:
                        t_low(b + 1, g + 2 - NP)
                    dve.wait_ge(exp_done, NP * b + g + 1)
                    if g >= 2 or not first:
                        dve.wait_ge(phi_lo, NP * b + g - 1)
                    dve.scalar_tensor_tensor(out=phif[:, g % 2, :], in0=k_bank[g % 2][0:CH, :], scalar=0.0,
                                             in1=expk[:, g % 2, :], op0=ALU.max, op1=ALU.add).then_inc(phi_done, 1)
                if not first:
                    nd_use(b - 1)

            t_low(0, 0)
            t_low(0, 1)
            batch(0, first=True)
            with dve.Fori(1, B - 1) as b:
                batch(b)
            batch(B - 1, last=True)
            g_copy(B - 1)
            kv_copy(B - 1)
            nd_use(B - 1)
            dve.wait_ge(nd_read, B)
            dve.tensor_tensor(K["attT"][:, :, :], K["attT"][:, :, :], K["gateT"][:, :, :], ALU.mult)

        @block.tensor
        def _(pe):
            pe.wait_ge(wk_done, 1)

            def t_group(b, n, u, g, first=False):
                if g == 0:
                    pe.wait_ge(raw_in[u], 32 * (n + 1))
                if not first:
                    pe.wait_ge(t_lo, NP * b + g - 1)
                for k in range(KC):
                    for h in range(CP):
                        at = (k * CP + h) * CH
                        mm = pe.transpose(t_bank[g % 2][:, at:at + CH], raw[u][:, g * CP + h, k * P:(k + 1) * P],
                                          K["ident"][0:CH, 0:CH])
                mm.then_inc(t_full, 1)

            def k_group(b, g, first):
                pe.wait_ge(t_lo, NP * b + g + 1)
                if g >= 2 or not first:
                    pe.wait_ge(phi_done, NP * b + g - 1)
                for h in range(CP):
                    at = (g * CP + h) * CH
                    mm = matmul_parts(pe, k_bank[g % 2][0:CH, h * D:(h + 1) * D],
                                      [(ctxT.at(slice(None), i, slice(at, at + CH)), wk.at(slice(None), i, slice(None)))
                                       for i in range(KC)])
                mm.then_inc(k_full, 1)

            def g_group(b, g, first):
                pe.wait_ge(phi_lo, NP * b + g + 1)
                pe.wait_ge(rows_lo, NP * b + g + 1)
                if g == 0 and first:
                    pe.wait_ge(ones_set, 2)
                elif g == 0:
                    pe.wait_ge(g_read, KC * b)
                for ch in range(g * CP, (g + 1) * CP):
                    for k in range(KC):
                        mm = matmul_parts(pe, g_bank[k][:, 0:D + 2],
                                          [(phik.at(slice(None), ch, slice(k * P, (k + 1) * P)), rows.at(slice(None), ch, slice(0, D + 2)))],
                                          start=(ch == 0), stop=(ch == NC - 1))
                mm.then_inc(g_part, 1)

            def gt(b):
                pe.wait_ge(g_read, KC * (b + 1))
                for i in range(KC):
                    for k in range(KC):
                        at = (i * KC + k) * P
                        mm = pe.transpose(gt_bank[:, at:at + P], G[:, k, i * P:(i + 1) * P], K["ident"][:, :])
                mm.then_inc(gt_full, 1)

            def kv(b, again):
                pe.wait_ge(gt_read, b + 1)
                if again:
                    pe.wait_ge(nd_read, b)
                for k in range(KC):
                    for i in range(KC):
                        mm = pe.matmul(s_bank[:, k * P:(k + 1) * P], GT[:, i, k * P:(k + 1) * P],
                                       K["T_Wv"][:, i, k * P:(k + 1) * P], start=(i == 0), stop=(i == KC - 1))
                mm.then_inc(kv_full, 1)

            def numden(b):
                pe.wait_ge(kv_read, (1 + KC) * (b + 1))
                for k in range(KC):
                    for w, lhs in enumerate((KV, KS)):
                        mm = pe.matmul(nd[:, k, w, :], lhs[:, k, :], K["phiqT"][:, k, bass.ds(b * L, L)],
                                       start=True, stop=True)
                mm.then_inc(nd_full, 1)

            def batch(b, n, u, first=False, last=False, known=False):
                for g in range(NP):
                    k_group(b, g, first)
                    if g + 2 < NP:
                        t_group(b, 0, u, g + 2)
                    elif not last:
                        t_group(b + 1, n, 1 - u, g + 2 - NP)
                    if g == 5 and not first:
                        numden(b - 1)
                    if g >= 3:
                        g_group(b, g - 3, first)
                    elif not first:
                        g_group(b - 1, g + 3, False)
                    if g == 3 and not first:
                        gt(b - 1)
                    if g == 4 and not first:
                        kv(b - 1, not known)

            t_group(0, 0, 0, 0, first=True)
            t_group(0, 0, 0, 1, first=True)
            batch(0, 0, 0, first=True)
            batch(1, 1, 1, known=True)
            batch(2, 1, 0)
            with pe.Fori(1, B // 2 - 1) as i:
                batch(2 * i + 1, i + 1, 1)
                batch(2 * i + 2, i + 1, 0)
            batch(B - 1, 0, 1, last=True)
            for g in range(3, NP):
                g_group(B - 1, g, False)
            gt(B - 1)
            kv(B - 1, True)
            numden(B - 1)


def experts(nc, a, K):
    with ExitStack() as ctx:
        c = Core(nc, ctx)
        xn = c.sb("e_xn", [TT, NT, D])
        acc = c.sb("e_acc", [TT, NT, D])
        xnT = c.sb("e_xnT", [P, KC, T])
        wr = c.sb("e_wr", [P, KC, E])
        wgu = [c.sb(f"e_wgu{u}", [P, KC, 2 * I]) for u in range(2)]
        wd = [c.sb(f"e_wd{u}", [P, IC, D]) for u in range(2)]
        hT = [c.sb(f"e_hT{u}", [P, IC, TG]) for u in range(2)]
        sil = c.sb("e_sil", [P, 2, TG])
        comb = c.sb("e_comb", [TT, NT, 1 + E])
        pr, key, pick, rest, ranks = (c.sb(f"e_{m}", [TT, NT, E]) for m in ("pr", "key", "pick", "rest", "ranks"))
        irank = c.sb("e_irank", [TT, E], I32)
        mx, tot = c.sb("e_mx", [TT, NT]), c.sb("e_tot", [TT, NT])
        g_bank = [c.ps(f"e_g{i}", [P, 512]) for i in range(2)]
        u_bank = [c.ps(f"e_u{i}", [P, 512]) for i in range(2)]
        d_bank = [c.ps(f"e_d{i}", [P, 512]) for i in range(4)]
        n = norm_buffers(c, "n1")
        w_in, wr_in = [c.sem(f"e_w_in{u}") for u in range(2)], c.sem("e_wr_in")
        o_full, o_read, small = c.sem("e_o_full"), c.sem("e_o_read"), c.sem("e_small")
        t_full, t_read, r_full = c.sem("e_t_full"), c.sem("e_t_read"), c.sem("e_r_full")
        exp_go, exp_done, iota_done, rank_done = c.sem("e_exp_go"), c.sem("e_exp"), c.sem("e_iota"), c.sem("e_rank")
        g_full, u_full, sil_done, h_done = c.sem("e_g_full"), c.sem("e_u_full"), c.sem("e_sil_done"), c.sem("e_h")
        d_full, d_read, comb_done, zeroed = c.sem("e_d_full"), c.sem("e_d_read"), c.sem("e_comb_done"), c.sem("e_zero")
        block = ctx.enter_context(nc.Block())
        STEPS = NG
        gu_of = lambda e: a["L0_ffn_w_gate_up"][bass.ds(e, 1), :, :].rearrange("e (k p) n -> p (e k) n", p=P)
        wd_of = lambda e: a["L0_ffn_w_down"][bass.ds(e, 1), :, :].rearrange("e (k p) n -> p (e k) n", p=P)

        @block.sync
        def _(sp):
            def load(u, gu, down):
                sp.dma_start(wgu[u][:, :, :], gu).then_inc(w_in[u], 16)
                sp.dma_start(wd[u][:, :, :], down).then_inc(w_in[u], 16)

            with nc.allow_non_contiguous_dma(reason="router weights, 8 to a row"):
                sp.dma_start(wr[:, :, :], a["L0_ffn_gate_w"].rearrange("(k p) e -> p k e", p=P)).then_inc(wr_in, 16)
            load(0, a["L0_ffn_shared_gate_up"].rearrange("(k p) n -> p k n", p=P),
                 a["L0_ffn_shared_down"].rearrange("(k p) n -> p k n", p=P))
            load(1, gu_of(0), wd_of(0))
            with sp.Fori(1, E // 2) as i:
                sp.wait_ge(d_full, NG * (2 * i - 1))
                load(0, gu_of(2 * i - 1), wd_of(2 * i - 1))
                sp.wait_ge(d_full, NG * 2 * i)
                load(1, gu_of(2 * i), wd_of(2 * i))
            sp.wait_ge(d_full, NG * (E - 1))
            load(0, gu_of(E - 1), wd_of(E - 1))

        @block.gpsimd
        def _(pool):
            pool.memset(comb[:, :, 0:1], 1.0).then_inc(zeroed, 1)
            pool.memset(acc[:, :, :], 0.0).then_inc(zeroed, 1)
            pool.iota(irank[:, :], [[-1, E]], base=E, channel_multiplier=0).then_inc(iota_done, 1)
            pool.wait_ge(iota_done, 1)
            pool.tensor_copy(ranks[:, :, :], irank[:, :].unsqueeze(1).to_broadcast([TT, NT, E])).then_inc(rank_done, 1)
            norm_pool(pool, n)

        @block.scalar
        def _(act):
            act.wait_ge(exp_go, 1)
            act.activation(pr[:, :, :], key[:, :, :], ACT.Exp).then_inc(exp_done, 1)

            def expert(m):
                for g in range(STEPS):
                    for j in range(IC):
                        k = (m * STEPS + g) * IC + j
                        act.wait_ge(g_full, k + 1)
                        if not isinstance(m, int) or m or g or j >= 2:
                            act.wait_ge(h_done, k - 1)
                        act.activation(sil[:, j % 2, :], g_bank[j % 2][:, 0:TG], ACT.Silu).then_inc(sil_done, 1)

            expert(0)
            with act.Fori(1, 1 + E) as m:
                expert(m)

        @block.vector
        def _(dve):
            step = in_order(dve, small)
            for t in range(NT):
                dve.wait_ge(o_full, t + 1)
                dve.scalar_tensor_tensor(out=K["x"][:, t, :], in0=d_bank[t % 4][0:TT, 0:D], scalar=K["gate_tanh"][:, 0:1],
                                         in1=K["x"][:, t, :], op0=ALU.mult, op1=ALU.add).then_inc(o_read, 1)
            dve.wait_ge(o_read, NT)
            norm_vector(dve, n, K["x"], xn)
            for g in range(NT // 2):
                dve.wait_ge(t_full, g + 1)
                dve.tensor_copy(xnT[:, :, g * 2 * TT:(g + 1) * 2 * TT],
                                g_bank[g % 2][:, 0:TG].rearrange("p (k n) -> p k n", k=KC)).then_inc(t_read, 1)
            dve.wait_ge(r_full, 1)
            logits = d_bank[0][0:TT, 0:NT * E].rearrange("p (t e) -> p t e", e=E)
            wide = lambda v: v.unsqueeze(2).to_broadcast([TT, NT, E])
            step(dve.tensor_reduce(mx[:, :], logits, AX.X, ALU.max))
            dve.tensor_tensor(key[:, :, :], logits, wide(mx[:, :]), ALU.subtract).then_inc(exp_go, 1)
            dve.wait_ge(exp_done, 1)
            step(dve.tensor_reduce(tot[:, :], pr[:, :, :], AX.X, ALU.add))
            step(dve.reciprocal(tot[:, :], tot[:, :]))
            step(dve.tensor_tensor(pr[:, :, :], pr[:, :, :], wide(tot[:, :]), ALU.mult))
            step(dve.tensor_copy(rest[:, :, :], pr[:, :, :]))
            dve.wait_ge(rank_done, 1)
            dve.wait_ge(zeroed, 2)
            chosen = comb[:, :, 1:1 + E]
            for r in range(2):
                step(dve.tensor_reduce(mx[:, :], rest[:, :, :], AX.X, ALU.max))
                step(dve.tensor_tensor(key[:, :, :], rest[:, :, :], wide(mx[:, :]), ALU.is_equal))
                step(dve.tensor_tensor(key[:, :, :], key[:, :, :], ranks[:, :, :], ALU.mult))
                step(dve.tensor_reduce(mx[:, :], key[:, :, :], AX.X, ALU.max))
                step(dve.tensor_tensor(pick[:, :, :], key[:, :, :], wide(mx[:, :]), ALU.is_equal))
                if r == 0:
                    step(dve.tensor_copy(chosen, pick[:, :, :]))
                    step(dve.scalar_tensor_tensor(out=rest[:, :, :].rearrange("p t e -> p (t e)"),
                                                  in0=pick[:, :, :].rearrange("p t e -> p (t e)"), scalar=-2.0,
                                                  in1=rest[:, :, :].rearrange("p t e -> p (t e)"), op0=ALU.mult, op1=ALU.add))
                else:
                    step(dve.tensor_tensor(chosen, chosen, pick[:, :, :], ALU.add))
            step(dve.tensor_tensor(pr[:, :, :], pr[:, :, :], chosen, ALU.mult))
            step(dve.tensor_reduce(tot[:, :], pr[:, :, :], AX.X, ALU.add))
            step(dve.reciprocal(tot[:, :], tot[:, :]))
            step(dve.tensor_tensor(chosen, pr[:, :, :], wide(tot[:, :]), ALU.mult))

            def up(m, g, known):
                for j in range(IC):
                    k = (m * STEPS + g) * IC + j
                    dve.wait_ge(sil_done, k + 1)
                    dve.wait_ge(u_full, k + 1)
                    if not known or m * STEPS + g >= 2:
                        dve.wait_ge(d_full, m * STEPS + g - 1)
                    dve.tensor_tensor(hT[g % 2][:, j, :], sil[:, j % 2, :], u_bank[j % 2][:, 0:TG], ALU.mult).then_inc(h_done, 1)

            def down(m, g, known):
                dve.wait_ge(d_full, m * STEPS + g + 1)
                if not known or m * STEPS + g:
                    dve.wait_ge(d_read, 4 * (m * STEPS + g))
                for q in range(4):
                    t = 4 * g + q
                    dve.scalar_tensor_tensor(out=acc[:, t, :], in0=d_bank[q][0:TT, 0:D], scalar=comb[:, t, bass.ds(m, 1)],
                                             in1=acc[:, t, :], op0=ALU.mult, op1=ALU.add).then_inc(d_read, 1)

            def expert(m, known):
                for g in range(STEPS):
                    up(m, g, known)
                    if g:
                        down(m, g - 1, known)
                    elif not known:
                        down(m - 1, STEPS - 1, False)

            expert(0, True)
            with dve.Fori(1, 1 + E) as m:
                expert(m, False)
            down(E, STEPS - 1, True)
            dve.wait_ge(d_read, 4 * STEPS * (1 + E))
            dve.scalar_tensor_tensor(out=K["x"][:, :, :].rearrange("p t d -> p (t d)"), in0=acc[:, :, :].rearrange("p t d -> p (t d)"),
                                     scalar=K["gate_tanh"][:, 2:3], in1=K["x"][:, :, :].rearrange("p t d -> p (t d)"),
                                     op0=ALU.mult, op1=ALU.add)

        @block.tensor
        def _(pe):
            for t in range(NT):
                if t >= 4:
                    pe.wait_ge(o_read, t - 3)
                for i in range(KC):
                    mm = pe.matmul(d_bank[t % 4][0:TT, 0:D], K["attT"][:, i, t * TT:(t + 1) * TT], K["T_Wo"][:, i, :],
                                   start=(i == 0), stop=(i == KC - 1))
                mm.then_inc(o_full, 1)
            for g in range(NT // 2):
                pe.wait_ge(n["xn_done"], 2 * g + 2)
                if g >= 2:
                    pe.wait_ge(t_read, g - 1)
                transpose_tiles(pe, g_bank[g % 2], xn, g, K["ident"]).then_inc(t_full, 1)
            pe.wait_ge(t_read, NT // 2)
            pe.wait_ge(wr_in, 16)
            for t in range(NT):
                for i in range(KC):
                    mm = pe.matmul(d_bank[0][0:TT, t * E:(t + 1) * E], xnT[:, i, t * TT:(t + 1) * TT], wr[:, i, :],
                                   start=(i == 0), stop=(i == KC - 1))
            mm.then_inc(r_full, 1)
            pe.wait_ge(exp_go, 1)

            def up(m, g, u, known):
                for j in range(IC):
                    k = (m * STEPS + g) * IC + j
                    if not known or k >= 2:
                        pe.wait_ge(h_done, k - 1)
                    for bank, col, done in ((g_bank, j, g_full), (u_bank, IC + j, u_full)):
                        for i in range(KC):
                            mm = pe.matmul(bank[j % 2][:, 0:TG], wgu[u][:, i, col * P:(col + 1) * P],
                                           xnT[:, i, g * TG:(g + 1) * TG], start=(i == 0), stop=(i == KC - 1))
                        mm.then_inc(done, 1)

            def down(m, g, u, known):
                pe.wait_ge(h_done, IC * (m * STEPS + g + 1))
                if not known or m * STEPS + g:
                    pe.wait_ge(d_read, 4 * (m * STEPS + g))
                for q in range(4):
                    for j in range(IC):
                        mm = pe.matmul(d_bank[q][0:TT, 0:D], hT[g % 2][:, j, q * TT:(q + 1) * TT], wd[u][:, j, :],
                                       start=(j == 0), stop=(j == IC - 1))
                mm.then_inc(d_full, 1)

            def expert(m, n, u, known):
                pe.wait_ge(w_in[u], 32 * (n + 1))
                for g in range(STEPS):
                    up(m, g, u, known)
                    if g:
                        down(m, g - 1, u, known)
                    elif not known:
                        down(m - 1, STEPS - 1, 1 - u, False)

            expert(0, 0, 0, True)
            with pe.Fori(0, E // 2) as i:
                expert(2 * i + 1, i, 1, False)
                expert(2 * i + 2, i + 1, 0, False)
            down(E, STEPS - 1, 0, True)


A_PLAN = [[("K10", 0)], [("K11", 0), ("V0", 0), ("V1", 0)], [("K12", 0), ("V2", 0), ("V3", 0)], [("V4", 0), ("V5", 0)],
          [("T0", 1), ("T1", 1)], [("K00", 1), ("T2", 1), ("T3", 1)], [("K01", 1), ("T4", 1), ("T5", 1)], [("K02", 1)]]
A_AHEAD = [w for slot in A_PLAN for w, ahead in slot if ahead]
A_ORDER = A_AHEAD + [w for slot in A_PLAN for w, ahead in slot if not ahead]
HI_OF = [[w for w in A_ORDER[i::2] if w[0] != "V"] for i in range(2)]
HI_N = [len(of) for of in HI_OF]
HI_NTH = {w: n + 1 for of in HI_OF for n, w in enumerate(of)}
KG = 3
GW = S // KG


def queries(nc, a, K):
    with ExitStack() as ctx:
        c = Core(nc, ctx)
        xn = c.sb("q_xn", [TT, NT, D])
        xnT = c.sb("q_xnT", [P, KC, T])
        am, sc, iv = (c.sb(f"q_{m}", [TT, NT]) for m in ("am", "sc", "iv"))
        t_bank = [c.ps(f"q_t{i}", [P, 512]) for i in range(4)]
        q_bank = [c.ps(f"q_q{i}", [P, 512]) for i in range(4)]
        n = norm_buffers(c, "n2")
        small, t_full, t_read, q_full, q_read = (c.sem(f"q_{m}") for m in ("small", "t_full", "t_read", "q_full", "q_read"))
        STEPS_ALL = 3 + 3 * NT
        block = ctx.enter_context(nc.Block())

        @block.gpsimd
        def _(pool):
            norm_pool(pool, n)

        @block.vector
        def _(dve):
            step = in_order(dve, small)
            norm_vector(dve, n, K["x"], xn)
            dve.wait_ge(n["xn_done"], NT)
            fake_quant(dve, step, xn[:, :, :], xn, am[:, :], sc[:, :], iv[:, :], NT)
            for g in range(NT // 2):
                dve.wait_ge(t_full, g + 1)
                dve.tensor_copy(xnT[:, :, g * 2 * TT:(g + 1) * 2 * TT],
                                t_bank[g % 4][:, 0:TG].rearrange("p (k n) -> p k n", k=KC)).then_inc(t_read, 1)

        @block.scalar
        def _(act):
            for q in range(KC * NG):
                k, g = divmod(q, NG)
                act.wait_ge(q_full, q + 1)
                act.activation(K["phiqT"][:, k, g * TG:(g + 1) * TG], q_bank[q % 4][:, 0:TG], ACT.Identity,
                               bias=K["bq"][:, k:k + 1]).then_inc(q_read, 1)

        @block.tensor
        def _(pe):
            for g in range(NT // 2):
                pe.wait_ge(small, 3 + 3 * (2 * g + 2))
                if g >= 4:
                    pe.wait_ge(t_read, g - 3)
                transpose_tiles(pe, t_bank[g % 4], xn, g, K["ident"]).then_inc(t_full, 1)
            pe.wait_ge(t_read, NT // 2)
            for q in range(KC * NG):
                k, g = divmod(q, NG)
                if q >= 4:
                    pe.wait_ge(q_read, q - 3)
                for i in range(KC):
                    mm = pe.matmul(q_bank[q % 4][:, 0:TG], K["T_wq"][:, i, k * P:(k + 1) * P], xnT[:, i, g * TG:(g + 1) * TG],
                                   start=(i == 0), stop=(i == KC - 1))
                mm.then_inc(q_full, 1)


def softmax_attention(nc, a, K):
    with ExitStack() as ctx:
        c = Core(nc, ctx)
        ctx_sb = c.sb("a_ctx", [CH, NC, D])
        ctxT = c.parts("a_ctxT", [P, KC, S])
        keyT = c.parts("a_keyT", [P, KC, S])
        val = c.sb("a_val", [CH, NC, D])
        wk, wv = c.parts("a_wk", [P, KC, D]), c.parts("a_wv", [P, KC, D])
        qfull = c.sb("a_qfull", [P, KC, HC, L])
        qbd = c.parts("a_qbd", [P, KC, HC, L])
        prob = [c.sb(f"a_prob{u}", [TT, S]) for u in range(2)]
        probT = c.sb("a_probT", [CH, NC, TG])
        mxs = c.sb("a_mxs", [TT, PAIRS])
        lsum = c.sb("a_lsum", [TT, PAIRS])
        linv = c.sb("a_linv", [TT, PAIRS])
        lsel = c.sb("a_lsel", [TT, 4, 2, HD])
        lT = c.sb("a_lT", [P, L])
        picked = c.sb("a_picked", [P, HC, L])
        osum = c.sb("a_osum", [P, L])
        mraw = c.sb("a_mraw", [TT, PAIRS])
        s_bank = c.ps("a_s", [P, 3, 512])
        a_bank = [c.ps(f"a_a{i}", [P, 512]) for i in range(2)]
        p_bank = [c.ps(f"a_p{i}", [P, 512]) for i in range(2)]
        o_bank = c.ps("a_o", [P, 512])
        ctx_in = c.sem("a_ctx_in")
        w_hi, w_done = c.sem("a_w_hi"), c.sem("a_w_done")
        q_masked, q_hi, q_made = c.sem("a_q_masked"), c.sem("a_q_hi"), c.sem("a_q_made")
        a_full = [c.sem(f"a_a_full{i}") for i in range(2)]
        a_hi = [c.sem(f"a_a_hi{i}") for i in range(2)]
        a_read = [c.sem(f"a_a_read{i}") for i in range(2)]
        s_full, max_done, exp_done = c.sem("a_s_full"), c.sem("a_max"), c.sem("a_exp")
        p_full = [c.sem(f"a_p_full{i}") for i in range(2)]
        p_read = [c.sem(f"a_p_read{i}") for i in range(2)]
        linv_done, lsel_done = c.sem("a_linv_done"), c.sem("a_lsel_done")
        mraw_done = c.sem("a_mraw_done")
        o_full, lt_done, pick_done, sum_done, o_done = (c.sem(f"a_o_{m}") for m in ("full", "lt", "pick", "sum", "done"))
        block = ctx.enter_context(nc.Block())
        AN = len(A_ORDER) // 2
        flat = lambda t: t.rearrange("p c d -> p (c d)")

        def load(sp, b):
            v = a["ctx_2048"][bass.ds(b, 1), :, :].rearrange("b (p c) d -> p (b c) d", p=CH)
            sp.dma_start(ctx_sb[0:112, :, :], v[0:112, :, :]).then_inc(ctx_in, 16)
            sp.dma_start(ctx_sb[112:CH, :, :], v[112:CH, :, :]).then_inc(ctx_in, 16)

        @block.sync
        def _(sp):
            load(sp, 0)
            last_t = A_ORDER.index("T5")
            with sp.Fori(0, B - 1) as b:
                sp.wait_ge(a_full[last_t % 2], AN * b + last_t // 2 + 1)
                load(sp, b + 1)

        @block.gpsimd
        def _(pool):
            for n, (w, name) in enumerate(((wk, "T_wk"), (wv, "T_wv"))):
                pool.wait_ge(w_hi, n + 1)
                pool.tensor_tensor(w.lo[:, :, :], K[name][:, :, :], w.hi[:, :, :].bitcast(F32), ALU.subtract).then_inc(w_done, 1)

            def spread(b, known):
                mask = K["headmask"][:, :].rearrange("p (h n) -> p h n", h=HC)
                for k in range(KC):
                    nth = KC * b + k + 1
                    q = K["phiqT"][:, k, bass.ds(b * L, L)]
                    pool.tensor_tensor(qfull[:, k, :, :], mask, q.unsqueeze(1).to_broadcast([P, HC, L]), ALU.mult).then_inc(q_masked, 1)
                    pool.wait_ge(q_masked, nth)
                    if not known:
                        pool.wait_ge(s_full, PAIRS * b - PAIRS + 4 * k + 4)
                    pool.tensor_tensor(qbd.hi[:, k, :, :], qfull[:, k, :, :], mask, ALU.mult).then_inc(q_hi, 1)
                    pool.wait_ge(q_hi, nth)
                    pool.tensor_tensor(qbd.lo[:, k, :, :], qfull[:, k, :, :], qbd.hi[:, k, :, :].bitcast(F32),
                                       ALU.subtract).then_inc(q_made, 1)
                    pool.wait_ge(q_made, nth)

            spread(0, True)
            with pool.Fori(1, B) as b:
                spread(b, False)

        def slot_order(j, turns, last):
            banks = [("turn", f, 0) for f in range(3)] if turns else []
            pieces = [(w, 0, ahead) for w, ahead in A_PLAN[j] if not (last and ahead)]
            if j in (0, 4):
                return banks + pieces
            order = []
            for n in range(3):
                order += banks[n:n + 1] + pieces[n:n + 1]
            return order

        def place(w):
            at = A_ORDER.index(w)
            return at % 2, at // 2 + 1

        def target(t, w):
            g = int(w[-1])
            if w[0] == "T":
                return t[:, :, g * CP * CH:(g + 1) * CP * CH]
            return t[:, int(w[1]), g * GW:(g + 1) * GW]

        def source(w):
            bank = a_bank[place(w)[0]]
            if w[0] == "T":
                return bank[:, 0:KC * CP * CH].rearrange("p (k n) -> p k n", k=KC)
            return bank[:, 0:GW]

        @block.scalar
        def _(act):
            act.copy(wk.hi[:, :, :], K["T_wk"][:, :, :]).then_inc(w_hi, 1)
            act.copy(wv.hi[:, :, :], K["T_wv"][:, :, :]).then_inc(w_hi, 1)

            def piece(b, w):
                i, nth = place(w)
                act.wait_ge(a_full[i], AN * b + nth)
                if w[0] == "T":
                    act.copy(target(ctxT.hi, w), source(w)).then_inc(a_hi[i], 1)
                elif w[0] == "K":
                    k = int(w[1])
                    act.activation(target(keyT.hi, w), source(w), ACT.Identity, bias=K["bk"][:, k:k + 1]).then_inc(a_hi[i], 1)
                else:
                    g = int(w[1])
                    act.copy(flat(val[:, g * CP:(g + 1) * CP, :]), a_bank[i][0:CH, :]).then_inc(a_read[i], 1)

            def exp(b, j):
                act.wait_ge(max_done, PAIRS * b + j + 1)
                act.activation(prob[j % 2][:, :].rearrange("p (g n) -> p g n", g=KG), s_bank[0:TT, :, 0:GW], ACT.Exp,
                               bias=mxs[:, j:j + 1], scale=HD ** -0.5, accum_out=lsum[:, j:j + 1]).then_inc(exp_done, 1)

            def p_copy(b, j):
                at = 3 * j
                act.wait_ge(p_full[at % 2], 12 * b + at // 2 + 1)
                act.copy(probT[:, 0:4, (j % 4) * TT:(j % 4 + 1) * TT],
                         p_bank[at % 2][0:CH, 0:TG].rearrange("p (c n) -> p c n", c=4)).then_inc(p_read[at % 2], 1)

            def batch(b, first=False, last=False):
                for j in range(PAIRS):
                    pieces = [(w, ahead) for w, ahead in A_PLAN[j] if not (last and ahead)]
                    early = 0 if j in (0, 4) else 1
                    if j or not first:
                        p_copy(b if j else b - 1, (j - 1) % PAIRS)
                    for w, ahead in pieces[:early]:
                        piece(b + ahead, w)
                    exp(b, j)
                    for w, ahead in pieces[early:]:
                        piece(b + ahead, w)

            for w in A_AHEAD:
                piece(0, w)
            batch(0, first=True)
            with act.Fori(1, B - 1) as b:
                batch(b)
            batch(B - 1, last=True)
            p_copy(B - 1, PAIRS - 1)

        @block.vector
        def _(dve):
            def piece(b, w):
                i, nth = place(w)
                if w[0] == "T":
                    dve.wait_ge(a_hi[i], HI_N[i] * b + HI_NTH[w])
                    dve.tensor_tensor(target(ctxT.lo, w), source(w), target(ctxT.hi, w).bitcast(F32), ALU.subtract).then_inc(a_read[i], 1)
                elif w[0] == "K":
                    k = int(w[1])
                    dve.wait_ge(a_hi[i], HI_N[i] * b + HI_NTH[w])
                    dve.scalar_tensor_tensor(out=target(keyT.lo, w), in0=source(w), scalar=K["bk"][:, k:k + 1],
                                             in1=target(keyT.hi, w).bitcast(F32), op0=ALU.add, op1=ALU.subtract).then_inc(a_read[i], 1)

            def maximum(b, j):
                dve.wait_ge(s_full, PAIRS * b + j + 1)
                dve.tensor_reduce(mraw[:, j:j + 1], s_bank[0:TT, :, 0:GW], AX.XY, ALU.max, negate=True).then_inc(mraw_done, 1)
                dve.wait_ge(mraw_done, PAIRS * b + j + 1)
                dve.tensor_scalar(mxs[:, j:j + 1], mraw[:, j:j + 1], HD ** -0.5, None, ALU.mult).then_inc(max_done, 1)

            def p_copy(b, j, f):
                at = 3 * j + f
                dve.wait_ge(p_full[at % 2], 12 * b + at // 2 + 1)
                dve.tensor_copy(probT[:, 4 * f:4 * f + 4, (j % 4) * TT:(j % 4 + 1) * TT],
                                p_bank[at % 2][0:CH, 0:TG].rearrange("p (c n) -> p c n", c=4)).then_inc(p_read[at % 2], 1)

            def select(b, g):
                dve.wait_ge(exp_done, PAIRS * b + 4 * g + 4)
                dve.reciprocal(linv[:, 4 * g:4 * g + 4], lsum[:, 4 * g:4 * g + 4]).then_inc(linv_done, 1)
                dve.wait_ge(linv_done, 2 * b + g + 1)
                dve.tensor_tensor(lsel[:, :, :, :], K["pairmask"][:, :].rearrange("p (j h e) -> p j h e", j=4, h=2),
                                  linv[:, 4 * g:4 * g + 4].unsqueeze(2).unsqueeze(3).to_broadcast([TT, 4, 2, HD]),
                                  ALU.mult).then_inc(lsel_done, 1)

            def outputs(b, g):
                nth = 2 * b + g + 1
                dve.wait_ge(o_full, nth)
                dve.tensor_copy(lT[:, :], o_bank[:, TG:TG + L]).then_inc(lt_done, 1)
                dve.tensor_tensor(picked[:, :, :].rearrange("p h n -> p (h n)"), o_bank[:, 0:TG], K["headmask"][:, :],
                                  ALU.mult).then_inc(pick_done, 1)
                dve.wait_ge(pick_done, nth)
                dve.tensor_reduce(osum[:, :], picked[:, :, :].rearrange("p h n -> p n h"), AX.X, ALU.add).then_inc(sum_done, 1)
                dve.wait_ge(sum_done, nth)
                dve.wait_ge(lt_done, nth)
                dve.tensor_tensor(K["attT"][:, g, bass.ds(b * L, L)], osum[:, :], lT[:, :], ALU.mult).then_inc(o_done, 1)

            def batch(b, first=False, last=False):
                for j in range(PAIRS):
                    if j == 4:
                        select(b, 0)
                    if j == 0 and not first:
                        select(b - 1, 1)
                    maximum(b, j)
                    if j == 5:
                        outputs(b, 0)
                    if j == 1 and not first:
                        outputs(b - 1, 1)
                    for what, f, ahead in slot_order(j, not first or j, last):
                        if what == "turn":
                            if f:
                                p_copy(b if j else b - 1, (j - 1) % PAIRS, f)
                        else:
                            piece(b + ahead, what)

            for w in A_AHEAD:
                piece(0, w)
            batch(0, first=True)
            with dve.Fori(1, B - 1) as b:
                batch(b)
            batch(B - 1, last=True)
            select(B - 1, 1)
            for f in (1, 2):
                p_copy(B - 1, PAIRS - 1, f)
            outputs(B - 1, 1)
            dve.wait_ge(o_done, 2 * B)
            for k in range(KC):
                dve.tensor_scalar(K["attT"][:, k, :], K["attT"][:, k, :], K["bv"][:, k:k + 1], None, ALU.add)

        @block.tensor
        def _(pe):
            pe.wait_ge(w_done, 2)

            def wait_pieces(b, pieces):
                for i in range(2):
                    nth = [place(w)[1] for w in pieces if place(w)[0] == i]
                    if nth:
                        pe.wait_ge(a_read[i], AN * b + max(nth))

            def piece(b, w, known=False):
                i, nth = place(w)
                bank = a_bank[i]
                if not known or nth > 1:
                    pe.wait_ge(a_read[i], AN * b + nth - 1)
                g = int(w[-1])
                if w[0] == "T":
                    if g == 0:
                        pe.wait_ge(ctx_in, 32 * (b + 1))
                    for k in range(KC):
                        for h in range(CP):
                            o = (k * CP + h) * CH
                            mm = pe.transpose(bank[:, o:o + CH], ctx_sb[:, g * CP + h, k * P:(k + 1) * P], K["ident"][0:CH, 0:CH])
                elif w[0] == "K":
                    k = int(w[1])
                    if k == 0:
                        wait_pieces(b, (f"T{2 * g}", f"T{2 * g + 1}"))
                    mm = matmul_parts(pe, bank[:, 0:GW],
                                      [(wk.at(slice(None), i, slice(k * P, (k + 1) * P)),
                                        ctxT.at(slice(None), i, slice(g * GW, (g + 1) * GW))) for i in range(KC)])
                else:
                    for h in range(CP):
                        o = (g * CP + h) * CH
                        mm = matmul_parts(pe, bank[0:CH, h * D:(h + 1) * D],
                                          [(ctxT.at(slice(None), i, slice(o, o + CH)), wv.at(slice(None), i, slice(None)))
                                           for i in range(KC)])
                mm.then_inc(a_full[i], 1)

            def scores(b, j, known):
                k, q = divmod(j, 4)
                if q == 0:
                    pe.wait_ge(q_made, KC * b + k + 1)
                    wait_pieces(b, [f"K{k}{g}" for g in range(KG)])
                if not known or PAIRS * b + j:
                    pe.wait_ge(exp_done, PAIRS * b + j)
                pair = qbd.at(slice(None), k, slice(2 * q, 2 * q + 2), slice(None))
                pair = Parts(pair.hi.rearrange("p h n -> p (h n)"), pair.lo.rearrange("p h n -> p (h n)"))
                for g in range(KG):
                    mm = matmul_parts(pe, s_bank[0:TT, g, 0:GW], [(pair, keyT.at(slice(None), k, slice(g * GW, (g + 1) * GW)))])
                mm.then_inc(s_full, 1)

            def turn(b, j, f, known):
                if f == 0:
                    pe.wait_ge(exp_done, PAIRS * b + j + 1)
                at = 3 * j + f
                if not known or 12 * b + at // 2:
                    pe.wait_ge(p_read[at % 2], 12 * b + at // 2)
                for q in range(4):
                    ch = 4 * f + q
                    mm = pe.transpose(p_bank[at % 2][0:CH, q * TT:(q + 1) * TT], prob[j % 2][:, ch * CH:(ch + 1) * CH],
                                      K["ident"][0:TT, 0:TT])
                mm.then_inc(p_full[at % 2], 1)

            def values(b, g, known):
                last = 12 * (g + 1) - 1
                pe.wait_ge(p_read[(last - 1) % 2], 12 * b + (last - 1) // 2 + 1)
                pe.wait_ge(p_read[last % 2], 12 * b + last // 2)
                if g == 0:
                    wait_pieces(b, [f"V{n}" for n in range(NP)])
                if not known or 2 * b + g:
                    pe.wait_ge(o_done, 2 * b + g)
                for ch in range(NC):
                    if ch == 8:
                        pe.wait_ge(p_read[last % 2], 12 * b + last // 2 + 1)
                    pe.matmul(o_bank[:, 0:TG], val[:, ch, g * P:(g + 1) * P], probT[:, ch, :],
                              start=(ch == 0), stop=(ch == NC - 1))
                pe.wait_ge(lsel_done, 2 * b + g + 1)
                pe.matmul(o_bank[:, TG:TG + L], lsel[:, :, :, :].rearrange("p j h e -> p (j h e)"), K["fold"][:, :],
                          start=True, stop=True).then_inc(o_full, 1)

            def batch(b, first=False, last=False):
                for j in range(PAIRS):
                    scores(b, j, first)
                    for what, f, ahead in slot_order(j, not first or j, last):
                        if what == "turn":
                            turn(b if j else b - 1, (j - 1) % PAIRS, f, first)
                        else:
                            piece(b + ahead, what)
                    if j == 4:
                        values(b, 0, first)
                    if j == 0 and not first:
                        values(b - 1, 1, False)

            for w in A_AHEAD:
                piece(0, w, True)
            batch(0, first=True)
            with pe.Fori(1, B - 1) as b:
                batch(b)
            batch(B - 1, last=True)
            for f in range(3):
                turn(B - 1, PAIRS - 1, f, False)
            values(B - 1, 1, False)


def attention_output(nc, a, K):
    with ExitStack() as ctx:
        c = Core(nc, ctx)
        o = c.sb("p_o", [TT, NT, D])
        oT = c.sb("p_oT", [P, KC, T])
        am, sc, iv = (c.sb(f"p_{m}", [TT, NT]) for m in ("am", "sc", "iv"))
        t_bank = [c.ps(f"p_t{i}", [P, 512]) for i in range(4)]
        q_bank = [c.ps(f"p_q{i}", [P, 512]) for i in range(4)]
        small, r_full, r_read, t_full, t_read, q_full, q_read = (
            c.sem(f"p_{m}") for m in ("small", "r_full", "r_read", "t_full", "t_read", "q_full", "q_read"))
        block = ctx.enter_context(nc.Block())

        @block.vector
        def _(dve):
            step = in_order(dve, small)
            for t in range(NT):
                dve.wait_ge(r_full, t + 1)
                dve.tensor_copy(o[:, t, :], q_bank[t % 4][0:TT, 0:D]).then_inc(r_read, 1)
            dve.wait_ge(r_read, NT)
            fake_quant(dve, step, o[:, :, :], o, am[:, :], sc[:, :], iv[:, :], NT)
            for g in range(NT // 2):
                dve.wait_ge(t_full, g + 1)
                dve.tensor_copy(oT[:, :, g * 2 * TT:(g + 1) * 2 * TT],
                                t_bank[g % 4][:, 0:TG].rearrange("p (k n) -> p k n", k=KC)).then_inc(t_read, 1)
            for t in range(NT):
                dve.wait_ge(q_full, t + 1)
                step(dve.tensor_tensor(o[:, t, :], q_bank[t % 4][0:TT, 0:D], K["bp"][:, :], ALU.add))
                dve.scalar_tensor_tensor(out=K["x"][:, t, :], in0=o[:, t, :], scalar=K["gate_tanh"][:, 1:2],
                                         in1=K["x"][:, t, :], op0=ALU.mult, op1=ALU.add).then_inc(q_read, 1)

        @block.tensor
        def _(pe):
            for t in range(NT):
                if t >= 4:
                    pe.wait_ge(r_read, t - 3)
                for k in range(KC):
                    mm = pe.transpose(q_bank[t % 4][0:TT, k * P:(k + 1) * P], K["attT"][:, k, t * TT:(t + 1) * TT], K["ident"][:, :])
                mm.then_inc(r_full, 1)
            for g in range(NT // 2):
                pe.wait_ge(small, 3 + 3 * (2 * g + 2))
                if g >= 4:
                    pe.wait_ge(t_read, g - 3)
                transpose_tiles(pe, t_bank[g % 4], o, g, K["ident"]).then_inc(t_full, 1)
            for t in range(NT):
                pe.wait_ge(t_read, t // 2 + 1)
                if t < 4:
                    pe.wait_ge(r_read, NT)
                else:
                    pe.wait_ge(q_read, t - 3)
                for i in range(KC):
                    mm = pe.matmul(q_bank[t % 4][0:TT, 0:D], oT[:, i, t * TT:(t + 1) * TT], K["T_wp"][:, i, :],
                                   start=(i == 0), stop=(i == KC - 1))
                mm.then_inc(q_full, 1)


def dequantise(nc, a, K):
    with ExitStack() as ctx:
        c = Core(nc, ctx)
        pk = [c.sb(f"w_pk{u}", [P, 8 * P], I32) for u in range(2)]
        scl = [c.sb(f"w_scl{u}", [P, 64]) for u in range(2)]
        nib = c.sb("w_nib", [P, 8 * P, 2], I32)
        mag = c.sb("w_mag", [P, 8 * P, 2], I32)
        v0, v1 = c.sb("w_v0", [P, 8 * P, 2]), c.sb("w_v1", [P, 8 * P, 2])
        W = [c.sb(f"w_W{u}", [P, 2 * 8 * P]) for u in range(2)]
        banks = [c.ps(f"w_b{i}", [P, 512]) for i in range(8)]
        w_in = [c.sem(f"w_in{u}") for u in range(2)]
        small, turned, full, emptied = c.sem("w_small"), c.sem("w_turned"), c.sem("w_full"), c.sem("w_emptied")
        jobs = []
        for name, dst in (("gate", "WgT"), ("up", "WuT")):
            for h in range(2):
                wv = a[f"L1_ffn_{name}_W_packed"].rearrange("(m p) k -> p m k", p=P)[:, 8 * h:8 * h + 8, :]
                sv = a[f"L1_ffn_{name}_scales"].rearrange("(m p) k -> p m k", p=P)[:, 8 * h:8 * h + 8, :]
                jobs.append((dst, h, wv, sv, 8))
        for h in range(2):
            wv = a["L1_ffn_down_W_packed"][h * P:(h + 1) * P, :].unsqueeze(1)
            sv = a["L1_ffn_down_scales"][h * P:(h + 1) * P, :].unsqueeze(1)
            jobs.append(("WdT", h, wv, sv, 1))
        NS = 11
        block = ctx.enter_context(nc.Block())

        @block.sync
        def _(sp):
            for n, (_, _, wv, sv, m) in enumerate(jobs):
                if n >= 2:
                    sp.wait_ge(small, NS * (n - 1))
                with nc.allow_non_contiguous_dma(reason="block scales, 8 to a row"):
                    sp.dma_start(pk[n % 2][:, :].rearrange("p (m k) -> p m k", m=m), wv).then_inc(w_in[n % 2], 16)
                    sp.dma_start(scl[n % 2][:, :].rearrange("p (m k) -> p m k", m=m), sv).then_inc(w_in[n % 2], 16)

        @block.vector
        def _(dve):
            step = in_order(dve, small)
            flat = lambda t: t[:, :, :].rearrange("p k e -> p (k e)")
            for n in range(len(jobs)):
                u = n % 2
                dve.wait_ge(w_in[u], 32 * (n // 2 + 1))
                step(dve.tensor_scalar(nib[:, :, 0], pk[u][:, :], 15, None, ALU.bitwise_and))
                step(dve.tensor_scalar(nib[:, :, 1], pk[u][:, :], 4, 15, ALU.logical_shift_right, ALU.bitwise_and))
                step(dve.tensor_scalar(flat(mag), flat(nib), 7, None, ALU.bitwise_and))
                step(dve.tensor_scalar(flat(v0), flat(mag), 2.0, -8.0, ALU.mult, ALU.add))
                step(dve.scalar_tensor_tensor(out=flat(v0), in0=flat(mag), scalar=-2.0, in1=flat(v0), op0=ALU.add, op1=ALU.max))
                step(dve.scalar_tensor_tensor(out=flat(v0), in0=flat(mag), scalar=0.5, in1=flat(v0), op0=ALU.mult, op1=ALU.max))
                step(dve.tensor_scalar(flat(v1), flat(nib), 8.0, -2.0, ALU.is_ge, ALU.mult))
                step(dve.tensor_scalar(flat(v1), flat(v1), 1.0, None, ALU.add))
                step(dve.tensor_tensor(flat(v0), flat(v0), flat(v1), ALU.mult))
                if n >= 2:
                    dve.wait_ge(full, 4 * (n - 1))
                step(dve.tensor_tensor(W[u][:, :].rearrange("p (s k) -> p s k", k=BLK),
                                       v0[:, :, :].rearrange("p k e -> p (k e)").rearrange("p (s k) -> p s k", k=BLK),
                                       scl[u][:, :].unsqueeze(2).to_broadcast([P, 64, BLK]), ALU.mult))
                step(dve.tensor_copy(v1[:, 0:1, 0:1], v0[:, 0:1, 0:1]))

        @block.scalar
        def _(act):
            for n, (dst, h, _, _, m) in enumerate(jobs):
                for f in range(4):
                    act.wait_ge(full, 4 * n + f + 1)
                    bank = banks[(4 * n + f) % 8]
                    if m == 8:
                        out = K[dst][:, :, (8 * h + 2 * f) * P:(8 * h + 2 * f + 2) * P]
                        act.copy(out, bank[:, :].rearrange("p (k n) -> p k n", k=KC)).then_inc(emptied, 1)
                    else:
                        out = K[dst][:, 4 * f:4 * f + 4, h * P:(h + 1) * P]
                        act.copy(out, bank[:, :].rearrange("p (m n) -> p m n", m=4)).then_inc(emptied, 1)

        @block.tensor
        def _(pe):
            for n, (dst, h, _, _, m) in enumerate(jobs):
                pe.wait_ge(small, NS * (n + 1))
                for f in range(4):
                    if 4 * n + f >= 8:
                        pe.wait_ge(emptied, 4 * n + f - 7)
                    bank = banks[(4 * n + f) % 8]
                    for q in range(4):
                        if m == 8:
                            k, r = divmod(q, 2)
                            src = W[n % 2][:, (2 * f + r) * D + k * P:(2 * f + r) * D + (k + 1) * P]
                        else:
                            src = W[n % 2][:, (4 * f + q) * P:(4 * f + q + 1) * P]
                        mm = pe.transpose(bank[:, q * P:(q + 1) * P], src, K["ident"][:, :])
                    mm.then_inc(full, 1)


def feed_forward(nc, a, out, K):
    with ExitStack() as ctx:
        c = Core(nc, ctx)
        xn = c.sb("f_xn", [TT, NT, D])
        xnT = c.sb("f_xnT", [P, KC, T])
        sq, tn, h1 = (c.sb(f"f_{m}", [P, 2, TG]) for m in ("sq", "tn", "h1"))
        hT = c.sb("f_hT", [P, 2, TG])
        g_bank = [c.ps(f"f_g{i}", [P, 512]) for i in range(2)]
        u_bank = [c.ps(f"f_u{i}", [P, 512]) for i in range(2)]
        d_bank = [c.ps(f"f_d{i}", [P, 512]) for i in range(4)]
        n = norm_buffers(c, "n3")
        t_full, t_read, g_full, u_full = (c.sem(f"f_{m}") for m in ("t_full", "t_read", "g_full", "u_full"))
        sq_done, cube_done, inner_done, tanh_done, half_done, gelu_done, h_done = (
            c.sem(f"f_{m}") for m in ("sq_done", "cube_done", "inner_done", "tanh_done", "half_done", "gelu_done", "h_done"))
        d_full, x_done, stored = c.sem("f_d_full"), c.sem("f_x_done"), c.sem("f_stored")
        block = ctx.enter_context(nc.Block())
        NS = NG * MC

        @block.gpsimd
        def _(pool):
            norm_pool(pool, n)
            for s in range(NS):
                pool.wait_ge(sq_done, s + 1)
                pool.tensor_scalar(sq[:, s % 2, :], sq[:, s % 2, :], 0.044715, 1.0, ALU.mult, ALU.add).then_inc(cube_done, 1)
                if s:
                    pool.wait_ge(tanh_done, s)
                    pool.tensor_scalar(tn[:, (s - 1) % 2, :], tn[:, (s - 1) % 2, :], 1.0, 0.5, ALU.add, ALU.mult).then_inc(half_done, 1)
            pool.wait_ge(tanh_done, NS)
            pool.tensor_scalar(tn[:, (NS - 1) % 2, :], tn[:, (NS - 1) % 2, :], 1.0, 0.5, ALU.add, ALU.mult).then_inc(half_done, 1)

        @block.scalar
        def _(act):
            def square(s):
                act.wait_ge(g_full, s + 1)
                if s >= 2:
                    act.wait_ge(inner_done, s - 1)
                act.activation(sq[:, s % 2, :], g_bank[s % 2][:, 0:TG], ACT.Square).then_inc(sq_done, 1)

            def tanh(s):
                act.wait_ge(inner_done, s + 1)
                if s >= 2:
                    act.wait_ge(gelu_done, s - 1)
                act.activation(tn[:, s % 2, :], sq[:, s % 2, :], ACT.Tanh, scale=0.7978845608028654).then_inc(tanh_done, 1)

            square(0)
            for s in range(NS):
                tanh(s)
                if s + 1 < NS:
                    square(s + 1)

        @block.vector
        def _(dve):
            norm_vector(dve, n, K["x"], xn)
            for g in range(NT // 2):
                dve.wait_ge(t_full, g + 1)
                dve.tensor_copy(xnT[:, :, g * 2 * TT:(g + 1) * 2 * TT],
                                g_bank[g % 2][:, 0:TG].rearrange("p (k n) -> p k n", k=KC)).then_inc(t_read, 1)

            def inner(s):
                dve.wait_ge(cube_done, s + 1)
                dve.tensor_tensor(sq[:, s % 2, :], sq[:, s % 2, :], g_bank[s % 2][:, 0:TG], ALU.mult).then_inc(inner_done, 1)

            def product(s):
                dve.wait_ge(half_done, s + 1)
                dve.tensor_tensor(h1[:, s % 2, :], tn[:, s % 2, :], g_bank[s % 2][:, 0:TG], ALU.mult).then_inc(gelu_done, 1)
                dve.wait_ge(gelu_done, s + 1)
                dve.wait_ge(u_full, s + 1)
                if s >= 2:
                    dve.wait_ge(d_full, s - 1)
                dve.tensor_tensor(hT[:, s % 2, :], h1[:, s % 2, :], u_bank[s % 2][:, 0:TG], ALU.mult).then_inc(h_done, 1)

            def result(g):
                dve.wait_ge(d_full, MC * (g + 1))
                for q in range(4):
                    t = 4 * g + q
                    dve.scalar_tensor_tensor(out=K["x"][:, t, :], in0=d_bank[q][0:TT, 0:D], scalar=K["gate_tanh"][:, 3:4],
                                             in1=K["x"][:, t, :], op0=ALU.mult, op1=ALU.add).then_inc(x_done, 1)

            for s in range(NS):
                inner(s)
                product(s)
                if s and s % MC == 0:
                    result(s // MC - 1)
            result(NG - 1)

        @block.tensor
        def _(pe):
            for g in range(NT // 2):
                pe.wait_ge(n["xn_done"], 2 * g + 2)
                if g >= 2:
                    pe.wait_ge(t_read, g - 1)
                transpose_tiles(pe, g_bank[g % 2], xn, g, K["ident"]).then_inc(t_full, 1)
            pe.wait_ge(t_read, NT // 2)

            def up(s):
                g, m = divmod(s, MC)
                if s >= 2:
                    pe.wait_ge(h_done, s - 1)
                for bank, w, done in ((g_bank, "WgT", g_full), (u_bank, "WuT", u_full)):
                    for i in range(KC):
                        mm = pe.matmul(bank[s % 2][:, 0:TG], K[w][:, i, m * P:(m + 1) * P], xnT[:, i, g * TG:(g + 1) * TG],
                                       start=(i == 0), stop=(i == KC - 1))
                    mm.then_inc(done, 1)

            def down(s):
                g, m = divmod(s, MC)
                pe.wait_ge(h_done, s + 1)
                if m == 0 and g:
                    pe.wait_ge(x_done, 4 * g)
                for q in range(4):
                    mm = pe.matmul(d_bank[q][0:TT, 0:D], hT[:, s % 2, q * TT:(q + 1) * TT], K["WdT"][:, m, :],
                                   start=(m == 0), stop=(m == MC - 1))
                mm.then_inc(d_full, 1)

            up(0)
            for s in range(NS):
                if s + 1 < NS:
                    up(s + 1)
                down(s)

        @block.sync
        def _(sp):
            y = out.rearrange("b l d -> (b l) d").rearrange("(t p) d -> p t d", p=TT)
            for g in range(NG):
                sp.wait_ge(x_done, 4 * (g + 1))
                sp.dma_start(y[:, 4 * g:4 * g + 4, :], K["x"][:, 4 * g:4 * g + 4, :]).then_inc(stored, 16)
            sp.wait_ge(stored, 16 * NG)


def build(nc, a, out):
    with ExitStack() as ctx:
        c = Core(nc, ctx)
        K = {
            "x": c.sb("x", [TT, NT, D]), "attT": c.sb("attT", [P, KC, T]),
            "ident": c.sb("ident", [P, P]), "headmask": c.sb("headmask", [P, TG]), "blockmask": c.sb("blockmask", [P, P]),
            "pairmask": c.sb("pairmask", [TT, P]), "fold": c.sb("fold", [TT, L]),
            "gates": c.sb("gates", [TT, 5]), "gate_tanh": c.sb("gate_tanh", [TT, 4]), "bp": c.sb("bp", [TT, D]),
        }
        for m in ("bg", "bq", "bk", "bv"):
            K[m] = c.sb(m, [P, KC])
        for m in ("Wq", "Wg", "Wk", "Wv", "Wo", "wq", "wk", "wv", "wp"):
            K["T_" + m] = c.sb("T_" + m, [P, KC, D])
        with ExitStack() as scope:
            K["phiqT"] = scope.enter_context(nc.sbuf_tensor("phiqT", [P, KC, T], F32))
            with ExitStack() as inner:
                K["gateT"] = inner.enter_context(nc.sbuf_tensor("gateT", [P, KC, T], F32))
                setup(nc, a, K)
                linear_attention(nc, a, K)
            experts(nc, a, K)
            queries(nc, a, K)
            softmax_attention(nc, a, K)
        attention_output(nc, a, K)
        with ExitStack() as scope:
            K["WgT"] = scope.enter_context(nc.sbuf_tensor("WgT", [P, KC, M], F32))
            K["WuT"] = scope.enter_context(nc.sbuf_tensor("WuT", [P, KC, M], F32))
            K["WdT"] = scope.enter_context(nc.sbuf_tensor("WdT", [P, MC, D], F32))
            dequantise(nc, a, K)
            feed_forward(nc, a, out, K)


_INS = ["x", "ctx_2048", "g_xattn", "g_ffn", "L0_xattn_Wq", "L0_xattn_Wg", "L0_xattn_bg", "L0_xattn_Wkv", "L0_xattn_Wo",
        "L0_ffn_gate_w", "L0_ffn_w_gate_up", "L0_ffn_w_down", "L0_ffn_shared_gate_up", "L0_ffn_shared_down",
        "L1_xattn_wq", "L1_xattn_bq", "L1_xattn_wkv", "L1_xattn_bkv", "L1_xattn_wp", "L1_xattn_bp",
        "L1_ffn_gate_W_packed", "L1_ffn_gate_scales", "L1_ffn_up_W_packed", "L1_ffn_up_scales",
        "L1_ffn_down_W_packed", "L1_ffn_down_scales"]


def kernel(**inputs):
    import concourse.bacc as bacc
    from concourse.bass_utils import run_bass_kernel_spmd

    nc = bacc.Bacc("TRN2", target_bir_lowering=False, num_devices=1)
    arrays, a = {}, {}
    for name in _INS:
        v = np.ascontiguousarray(inputs[name])
        arrays[f"in_{name}"] = v
        a[name] = nc.dram_tensor(f"in_{name}", v.shape, mybir.dt.from_np(v.dtype), kind="ExternalInput").ap()
    out = nc.dram_tensor("out", (B, L, D), F32, kind="ExternalOutput").ap()
    build(nc, a, out)
    r = run_bass_kernel_spmd(nc, [arrays], core_ids=[0])
    return r.results[0]["out"]
```

```python
from contextlib import ExitStack

import numpy as np

import concourse.bass as bass
from concourse import mybir

F32 = mybir.dt.float32
F32R = mybir.dt.float32r
I32 = mybir.dt.int32
ALU = mybir.AluOpType
ACT = mybir.ActivationFunctionType
AX = mybir.AxisListType

B, L, D, S = 32, 56, 256, 1500
H, HD = 16, 16
P = 128
KC = D // P
HC = P // HD
T = B * L
TT = 2 * L
NT = T // TT
TG = 4 * TT
NG = T // TG
CH = 125
NC = S // CH
CP = 2
NP = NC // CP
CW = D + 4
E, I = 8, 512
IC = I // P
M, MC = 2048, 2048 // P
BLK = 32
MAGIC = 12582912.0
PAIRS = H // 2
SCALE = HD ** -0.5
QG = 4


def full(t):
    return t[tuple(slice(None) for _ in t.shape)]


class Parts:

    def __init__(self, hi, lo):
        self.hi, self.lo = hi, lo

    def at(self, *index):
        return Parts(self.hi[index], self.lo[index])


def matmul_parts(pe, out, pairs, start=True, stop=True):
    for n, (a, b) in enumerate(pairs):
        passes = ((a.hi, b.lo), (a.hi, b.hi), (a.lo, b.hi))
        for m, (lhs, rhs) in enumerate(passes):
            mm = pe.matmul(out, lhs, rhs, start=(start and n == 0 and m == 0),
                           stop=(stop and n == len(pairs) - 1 and m == 2))
    return mm


class Core:

    def __init__(self, nc, ctx):
        self.nc, self.ctx, self.sems = nc, ctx, []
        ctx.callback(self.close)

    def close(self):
        if self.sems:
            self.nc.clear_and_free_semaphores(self.sems)
            self.nc.all_engine_barrier()

    def sb(self, name, shape, dt=F32):
        return self.ctx.enter_context(self.nc.sbuf_tensor(name, shape, dt))

    def parts(self, name, shape):
        return Parts(self.sb(name + "_hi", shape, F32R), self.sb(name + "_lo", shape, F32R))

    def ps(self, name, shape):
        return self.ctx.enter_context(self.nc.psum_tensor(name, shape, F32))

    def sem(self, name):
        self.sems.append(self.nc.alloc_semaphore(name=name))
        return self.sems[-1]


def in_order(eng, sem):
    count = [0]

    def step(ins):
        count[0] += 1
        ins.then_inc(sem, 1)
        eng.wait_ge(sem, count[0])

    return step


def norm_buffers(c, tag):
    return {
        "stats": c.sb(f"{tag}_stats", [TT, NT, 6]), "mv": c.sb(f"{tag}_mv", [TT, NT, 2]),
        "var": c.sb(f"{tag}_var", [TT, NT]), "rstd": c.sb(f"{tag}_rstd", [TT, NT]),
        "half": c.sb(f"{tag}_half", [TT, NT]),
        "stats_done": c.sem(f"{tag}_stats_done"), "mv_done": c.sem(f"{tag}_mv_done"),
        "var_done": c.sem(f"{tag}_var_done"), "half_set": c.sem(f"{tag}_half_set"),
        "rstd_done": c.sem(f"{tag}_rstd_done"), "xn_done": c.sem(f"{tag}_xn_done"),
    }


def norm_vector(dve, n, x, xn):
    for t in range(NT):
        dve.bn_stats(out=n["stats"][:, t, :], in_=x[:, t, :]).then_inc(n["stats_done"], 1)
    for t in range(NT):
        dve.wait_ge(n["stats_done"], t + 1)
        dve.bn_aggr(out=n["mv"][:, t, :], in_=n["stats"][:, t, :]).then_inc(n["mv_done"], 1)
    dve.wait_ge(n["mv_done"], NT)
    dve.tensor_scalar(n["var"][:, :], n["mv"][:, :, 1], 1e-5, None, ALU.add).then_inc(n["var_done"], 1)
    dve.wait_ge(n["rstd_done"], 1)
    for t in range(NT):
        dve.tensor_scalar(xn[:, t, :], x[:, t, :], n["mv"][:, t, 0:1], n["rstd"][:, t:t + 1],
                          ALU.subtract, ALU.mult).then_inc(n["xn_done"], 1)


def norm_pool(pool, n):
    pool.memset(n["half"][:, :], -0.5).then_inc(n["half_set"], 1)
    pool.wait_ge(n["half_set"], 1)
    pool.wait_ge(n["var_done"], 1)
    pool.tensor_tensor(n["rstd"][:, :], n["var"][:, :], n["half"][:, :], ALU.pow).then_inc(n["rstd_done"], 1)


def fake_quant(dve, sem, base, src, out, absmax, scale, inverse, n):
    count = [base]

    def step(ins):
        count[0] += 1
        ins.then_inc(sem, 1)

    step(dve.tensor_reduce(absmax, src, AX.X, ALU.max, apply_absolute_value=True))
    dve.wait_ge(sem, count[0])
    step(dve.tensor_scalar(scale, absmax, 1.0 / 127.0, 1e-8, ALU.mult, ALU.max))
    dve.wait_ge(sem, count[0])
    step(dve.reciprocal(inverse, scale))
    for first in range(0, n, QG):
        groups = range(first, min(first + QG, n))
        dve.wait_ge(sem, count[0])
        for k in groups:
            step(dve.tensor_scalar(out[:, k, :], src[:, k, :], inverse[:, k:k + 1], MAGIC, ALU.mult, ALU.add))
        dve.wait_ge(sem, count[0])
        for k in groups:
            step(dve.tensor_scalar(out[:, k, :], out[:, k, :], MAGIC, 127.0, ALU.subtract, ALU.min))
        dve.wait_ge(sem, count[0])
        for k in groups:
            step(dve.tensor_scalar(out[:, k, :], out[:, k, :], -127.0, scale[:, k:k + 1], ALU.max, ALU.mult))


def quantised(k):
    return 3 + 3 * QG * (k // QG + 1)


def transpose_tiles(pe, bank, src, g, ident):
    for k in range(KC):
        for h in range(2):
            at = k * 2 * TT + h * TT
            mm = pe.transpose(bank[:, at:at + TT], src[:, 2 * g + h, k * P:(k + 1) * P], ident[0:TT, 0:TT])
    return mm


def setup(nc, a, K):
    with ExitStack() as ctx:
        c = Core(nc, ctx)
        names = ["Wq", "Wg", "Wk", "Wv", "Wo", "wq", "wk", "wv", "wp"]
        raw = {n: c.sb(f"raw_{n}", [P, KC, D]) for n in names}
        xn = c.sb("s_xn", [TT, NT, D])
        xnT = c.sb("s_xnT", [P, KC, T])
        expq = c.sb("s_expq", [P, 8, TG])
        am, sc, iv = (c.sb(f"s_{n}", [P, 2, KC]) for n in ("am", "sc", "iv"))
        banks = [c.ps(f"s_bank{i}", [P, 512]) for i in range(8)]
        n = norm_buffers(c, "n0")
        x_in, w_in, v_in = c.sem("x_in"), [c.sem(f"w_in_{m}") for m in names], c.sem("v_in")
        zeroed, ones_set, masks_set = c.sem("zeroed"), c.sem("ones_set"), c.sem("masks_set")
        full, emptied, quant = c.sem("s_full"), c.sem("s_emptied"), c.sem("s_quant")
        exp_done, min_done, phi_done = c.sem("s_exp"), c.sem("s_min"), c.sem("s_phi")
        w_hi = c.sem("s_w_hi")
        src = {
            "Wq": a["L0_xattn_Wq"], "Wg": a["L0_xattn_Wg"], "Wk": a["L0_xattn_Wkv"][0:D, :],
            "Wv": a["L0_xattn_Wkv"][D:2 * D, :], "Wo": a["L0_xattn_Wo"], "wq": a["L1_xattn_wq"],
            "wk": a["L1_xattn_wkv"][0:D, :], "wv": a["L1_xattn_wkv"][D:2 * D, :], "wp": a["L1_xattn_wp"],
        }
        NW, NX = len(names), NT // 2
        order = ["Wq", "Wg", "Wk", "Wv", "Wo", "wk", "wv", "wq", "wp"]
        split = [m for m in order if isinstance(K["T_" + m], Parts)]
        block = ctx.enter_context(nc.Block())

        @block.sync
        def _(sp):
            sp.dma_start(K["x"][:, :, :], a["x"].rearrange("b l d -> (b l) d").rearrange("(t p) d -> p t d", p=TT)).then_inc(x_in, 16)
            for m, s in zip(names, w_in):
                sp.dma_start(raw[m][:, :, :], src[m].rearrange("(o p) i -> p o i", p=P)).then_inc(s, 16)
            sp.wait_ge(v_in, 16 * 8)

        @block.scalar
        def _(act):
            with nc.allow_non_contiguous_dma(reason="biases, one value to a partition"):
                for t, v in (("bg", a["L0_xattn_bg"]), ("bq", a["L1_xattn_bq"]),
                             ("bk", a["L1_xattn_bkv"][0:D]), ("bv", a["L1_xattn_bkv"][D:2 * D])):
                    act.dma_start(K[t][:, :], v.rearrange("(o p) -> p o", p=P)).then_inc(v_in, 16)
                act.dma_start(K["bp"][:, :], a["L1_xattn_bp"].partition_broadcast(TT)).then_inc(v_in, 16)
                act.dma_start(K["gates"][:, 0:2], a["g_xattn"].partition_broadcast(TT)).then_inc(v_in, 16)
                act.dma_start(K["gates"][:, 2:4], a["g_ffn"].partition_broadcast(TT)).then_inc(v_in, 16)
                act.dma_start(K["gates"][:, 4:5], a["g_ffn"][0:1].partition_broadcast(TT)).then_inc(v_in, 16)
            act.wait_ge(v_in, 16 * 8)
            act.activation(K["gate_tanh"][:, :], K["gates"][:, 0:4], ACT.Tanh)
            for q in range(8):
                act.wait_ge(full, NW + NX + q + 1)
                act.activation(expq[:, q, :], banks[(NW + NX + q) % 8][:, 0:TG], ACT.Exp).then_inc(exp_done, 1)
            for q in range(8):
                k, g = divmod(q, NG)
                act.wait_ge(full, NW + NX + 8 + q + 1)
                act.activation(K["gateT"][:, k, g * TG:(g + 1) * TG], banks[(NW + NX + 8 + q) % 8][:, 0:TG],
                               ACT.Sigmoid, bias=K["bg"][:, k:k + 1])

        @block.gpsimd
        def _(pool):
            pool.memset(K["ident"][:, :], 0.0).then_inc(zeroed, 1)
            pool.memset(K["headmask"][:, :], 1.0).then_inc(ones_set, 1)
            pool.memset(K["pairmask"][:, :], 1.0).then_inc(ones_set, 1)
            pool.memset(K["fold"][:, :], 0.0).then_inc(zeroed, 1)
            pool.wait_ge(zeroed, 2)
            pool.affine_select(out=K["ident"][:, :], in_=K["ident"][:, :], compare_op=ALU.not_equal, fill=1.0,
                               base=0, pattern=[[-1, P]], channel_multiplier=1).then_inc(masks_set, 1)
            pool.wait_ge(ones_set, 2)
            hm = K["headmask"][:, :].rearrange("p (h n) -> p h n", h=HC)
            pool.affine_select(out=hm, in_=hm, compare_op=ALU.is_ge, fill=0.0, base=0,
                               pattern=[[-HD, HC], [0, L]], channel_multiplier=1).then_inc(masks_set, 1)
            pool.wait_ge(masks_set, 2)
            pool.affine_select(out=hm, in_=hm, compare_op=ALU.is_ge, fill=0.0, base=HD - 1,
                               pattern=[[HD, HC], [0, L]], channel_multiplier=-1).then_inc(masks_set, 1)
            pool.wait_ge(masks_set, 3)
            pool.tensor_copy(K["blockmask"][:, :].rearrange("p (h e) -> p h e", h=HC), hm[:, :, 0:HD]).then_inc(masks_set, 1)
            pm = K["pairmask"][:, :].rearrange("p (j h e) -> p j h e", j=4, h=2)
            pool.affine_select(out=pm[:, :, 0, :], in_=pm[:, :, 0, :], compare_op=ALU.is_ge, fill=0.0, base=L - 1,
                               pattern=[[0, 4], [0, HD]], channel_multiplier=-1).then_inc(masks_set, 1)
            pool.affine_select(out=pm[:, :, 1, :], in_=pm[:, :, 1, :], compare_op=ALU.is_ge, fill=0.0, base=-L,
                               pattern=[[0, 4], [0, HD]], channel_multiplier=1).then_inc(masks_set, 1)
            pool.affine_select(out=K["fold"][:, :], in_=K["fold"][:, :], compare_op=ALU.not_equal, fill=1.0,
                               base=0, pattern=[[-1, L]], channel_multiplier=1).then_inc(masks_set, 1)
            pool.wait_ge(masks_set, 7)
            pool.affine_select(out=K["fold"][:, :], in_=K["fold"][:, :], compare_op=ALU.not_equal, fill=1.0,
                               base=-L, pattern=[[-1, L]], channel_multiplier=1).then_inc(masks_set, 1)
            norm_pool(pool, n)
            for q in range(8):
                pool.wait_ge(exp_done, q + 1)
                pool.tensor_scalar(expq[:, q, :], expq[:, q, :], 1.0, 0.0, ALU.min, ALU.max).then_inc(min_done, 1)

        @block.vector
        def _(dve):
            dve.wait_ge(x_in, 16)
            norm_vector(dve, n, K["x"], xn)
            for i, m in enumerate(("wq", "wp")):
                dve.wait_ge(w_in[names.index(m)], 16)
                fake_quant(dve, quant, (3 + 3 * KC) * i, raw[m][:, :, :], raw[m], am[:, i, :], sc[:, i, :], iv[:, i, :], KC)
            for i, m in enumerate(order):
                dve.wait_ge(full, i + 1)
                to = K["T_" + m]
                if isinstance(to, Parts):
                    hi, lo = (part[:, :, :].rearrange("p k o -> p (k o)") for part in (to.hi, to.lo))
                    dve.tensor_copy(hi, banks[i % 8][:, :]).then_inc(w_hi, 1)
                    dve.wait_ge(w_hi, split.index(m) + 1)
                    dve.tensor_tensor(lo, banks[i % 8][:, :], hi.bitcast(F32), ALU.subtract).then_inc(emptied, 1)
                else:
                    dve.tensor_copy(to[:, :, :].rearrange("p k o -> p (k o)"), banks[i % 8][:, :]).then_inc(emptied, 1)
            for g in range(NX):
                dve.wait_ge(full, NW + g + 1)
                dve.tensor_copy(xnT[:, :, g * 2 * TT:(g + 1) * 2 * TT],
                                banks[(NW + g) % 8][:, 0:TG].rearrange("p (k n) -> p k n", k=KC)).then_inc(emptied, 1)
            for q in range(8):
                k, g = divmod(q, NG)
                dve.wait_ge(min_done, q + 1)
                dve.scalar_tensor_tensor(out=K["phiqT"][:, k, g * TG:(g + 1) * TG], in0=banks[(NW + NX + q) % 8][:, 0:TG],
                                         scalar=0.0, in1=expq[:, q, :], op0=ALU.max, op1=ALU.add).then_inc(phi_done, 1)

        @block.tensor
        def _(pe):
            pe.wait_ge(masks_set, 1)
            for i, m in enumerate(order):
                pe.wait_ge(w_in[names.index(m)], 16)
                if m in ("wq", "wp"):
                    pe.wait_ge(quant, (3 + 3 * KC) * (1 + ("wq", "wp").index(m)))
                if i >= 8:
                    pe.wait_ge(emptied, i - 7)
                for k in range(KC):
                    for o in range(KC):
                        mm = pe.transpose(banks[i % 8][:, (k * KC + o) * P:(k * KC + o + 1) * P],
                                          raw[m][:, o, k * P:(k + 1) * P], K["ident"][:, :])
                mm.then_inc(full, 1)
            for g in range(NX):
                pe.wait_ge(n["xn_done"], 2 * g + 2)
                pe.wait_ge(emptied, NW + g - 7)
                transpose_tiles(pe, banks[(NW + g) % 8], xn, g, K["ident"]).then_inc(full, 1)
            pe.wait_ge(emptied, NW + NX)
            for which, w in enumerate(("T_Wq", "T_Wg")):
                for q in range(8):
                    k, g = divmod(q, NG)
                    if which:
                        pe.wait_ge(phi_done, q + 1)
                    for i in range(KC):
                        mm = pe.matmul(banks[(NW + NX + 8 * which + q) % 8][:, 0:TG], K[w][:, i, k * P:(k + 1) * P],
                                       xnT[:, i, g * TG:(g + 1) * TG], start=(i == 0), stop=(i == KC - 1))
                    mm.then_inc(full, 1)


def linear_attention(nc, a, K):
    with ExitStack() as ctx:
        c = Core(nc, ctx)
        raw = [c.sb(f"l_raw{u}", [CH, NC, D]) for u in range(2)]
        rows = c.parts("l_rows", [CH, NC, CW])
        ctxT = c.parts("l_ctxT", [P, KC, S])
        phik = c.parts("l_phik", [CH, NC, D])
        wk = K["T_Wk"]
        phif = c.sb("l_phif", [CH, 2, CP * D])
        expk = c.sb("l_expk", [CH, 2, CP * D])
        G = c.sb("l_G", [P, KC, D + 1])
        GT = c.sb("l_GT", [P, KC, D])
        KV = c.sb("l_KV", [P, KC, P])
        KS = c.sb("l_KS", [P, KC, P])
        den = c.sb("l_den", [P, KC, L])
        rden, gden = c.sb("l_rden", [P, KC, L]), c.sb("l_gden", [P, KC, L])
        den_gated = c.sem("l_den_gated")
        t_bank = [c.ps(f"l_t{i}", [P, 512]) for i in range(2)]
        k_bank = [c.ps(f"l_k{i}", [P, 512]) for i in range(2)]
        g_bank = [c.ps(f"l_g{i}", [P, 512]) for i in range(KC)]
        gt_bank, s_bank = c.ps("l_gt", [P, 512]), c.ps("l_s", [P, 512])
        nd = s_bank[:, 256:256 + 4 * L].rearrange("p (k w n) -> p k w n", k=KC, w=2)
        ones_set = c.sem("l_ones")
        raw_in = [c.sem(f"l_raw_in{u}") for u in range(2)]
        rows_hi, rows_lo = c.sem("l_rows_hi"), c.sem("l_rows_lo")
        t_full, t_hi, t_lo = c.sem("l_t_full"), c.sem("l_t_hi"), c.sem("l_t_lo")
        k_full, min_done, exp_done, phi_done = c.sem("l_k_full"), c.sem("l_min"), c.sem("l_exp"), c.sem("l_phi")
        phi_hi, phi_lo = c.sem("l_phi_hi"), c.sem("l_phi_lo")
        g_part, g_read = c.sem("l_g_part"), c.sem("l_g_read")
        gt_full, gt_read = c.sem("l_gt_full"), c.sem("l_gt_read")
        kv_full, kv_read = c.sem("l_kv_full"), c.sem("l_kv_read")
        nd_full, den_eps, den_inv, nd_read = c.sem("l_nd_full"), c.sem("l_den_eps"), c.sem("l_den_inv"), c.sem("l_nd_read")
        block = ctx.enter_context(nc.Block())
        flat = lambda t: t.rearrange("p c d -> p (c d)")

        def load(sp, b, u):
            v = a["ctx_2048"][bass.ds(b, 1), :, :].rearrange("b (p c) d -> p (b c) d", p=CH)
            sp.dma_start(raw[u][0:112, :, :], v[0:112, :, :]).then_inc(raw_in[u], 16)
            sp.dma_start(raw[u][112:CH, :, :], v[112:CH, :, :]).then_inc(raw_in[u], 16)

        @block.sync
        def _(sp):
            load(sp, 0, 0)
            load(sp, 1, 1)
            with sp.Fori(0, B // 2 - 1) as i:
                for u in range(2):
                    sp.wait_ge(t_full, NP * (2 * i + u + 1))
                    sp.wait_ge(rows_lo, NP * (2 * i + u + 1))
                    load(sp, 2 * i + 2 + u, u)

        @block.gpsimd
        def _(pool):
            pool.memset(rows.hi[:, :, D:CW].bitcast(F32), 1.0).then_inc(ones_set, 1)
            pool.memset(rows.lo[:, :, D:CW].bitcast(F32), 0.0).then_inc(ones_set, 1)

            def batch(b, u):
                for g in range(NP):
                    sl = slice(g * CP, (g + 1) * CP)
                    pool.wait_ge(rows_hi, NP * b + g + 1)
                    pool.tensor_tensor(rows.lo[:, sl, 0:D], raw[u][:, sl, :], rows.hi[:, sl, 0:D].bitcast(F32),
                                       ALU.subtract).then_inc(rows_lo, 1)
                    pool.wait_ge(phi_hi, NP * b + g + 1)
                    pool.tensor_tensor(flat(phik.lo[:, sl, :]), phif[:, g % 2, :], flat(phik.hi[:, sl, :]).bitcast(F32),
                                       ALU.subtract).then_inc(phi_lo, 1)

            with pool.Fori(0, B // 2) as i:
                batch(2 * i, 0)
                batch(2 * i + 1, 1)

        @block.scalar
        def _(act):

            def t_copy(b, g):
                act.wait_ge(t_full, NP * b + g + 1)
                act.copy(ctxT.hi[:, :, g * CP * CH:(g + 1) * CP * CH],
                         t_bank[g % 2][:, 0:KC * CP * CH].rearrange("p (k n) -> p k n", k=KC)).then_inc(t_hi, 1)

            def batch(b, n, u, first=False, last=False):
                for g in range(NP):
                    if g + 2 < NP:
                        t_copy(b, g + 2)
                    elif not last:
                        t_copy(b + 1, g + 2 - NP)
                    if g == 4 and not first:
                        act.wait_ge(gt_full, b)
                        act.copy(flat(GT[:, :, :]), gt_bank[:, :]).then_inc(gt_read, 1)
                    act.wait_ge(min_done, NP * b + g + 1)
                    act.activation(expk[:, g % 2, :], expk[:, g % 2, :], ACT.Exp).then_inc(exp_done, 1)
                    if g == 0:
                        act.wait_ge(raw_in[u], 32 * (n + 1))
                    if not first:
                        act.wait_ge(g_part, NP * b - NP + g + 1)
                    act.copy(rows.hi[:, g * CP:(g + 1) * CP, 0:D], raw[u][:, g * CP:(g + 1) * CP, :]).then_inc(rows_hi, 1)
                    act.wait_ge(phi_done, NP * b + g + 1)
                    act.copy(flat(phik.hi[:, g * CP:(g + 1) * CP, :]), phif[:, g % 2, :]).then_inc(phi_hi, 1)

            t_copy(0, 0)
            t_copy(0, 1)
            batch(0, 0, 0, first=True)
            with act.Fori(0, B // 2 - 1) as i:
                batch(2 * i + 1, i, 1)
                batch(2 * i + 2, i + 1, 0)
            batch(B - 1, B // 2 - 1, 1, last=True)
            act.wait_ge(gt_full, B)
            act.copy(flat(GT[:, :, :]), gt_bank[:, :]).then_inc(gt_read, 1)

        @block.vector
        def _(dve):
            def g_copy(b):
                dve.wait_ge(g_part, NP * (b + 1))
                for k in range(KC):
                    dve.tensor_copy(G[:, k, :], g_bank[k][:, 0:D + 1]).then_inc(g_read, 1)

            def kv_copy(b):
                dve.wait_ge(kv_full, b + 1)
                dve.tensor_tensor(KV[:, :, :], s_bank[:, 0:D].rearrange("p (k e) -> p k e", k=KC),
                                  K["blockmask"][:, :].unsqueeze(1).to_broadcast([P, KC, P]), ALU.mult).then_inc(kv_read, 1)
                for k in range(KC):
                    dve.tensor_scalar(KS[:, k, :], K["blockmask"][:, :], G[:, k, D:D + 1], None, ALU.mult).then_inc(kv_read, 1)

            def nd_use(b):
                dve.wait_ge(nd_full, b + 1)
                dve.tensor_scalar(den[:, :, :], nd[:, :, 1, :], 1e-6, None, ALU.add).then_inc(den_eps, 1)
                dve.wait_ge(den_eps, b + 1)
                dve.reciprocal(rden[:, :, :], den[:, :, :]).then_inc(den_inv, 1)
                dve.wait_ge(den_inv, b + 1)
                dve.tensor_tensor(gden[:, :, :], rden[:, :, :], K["gateT"][:, :, bass.ds(b * L, L)], ALU.mult).then_inc(den_gated, 1)
                dve.wait_ge(den_gated, b + 1)
                dve.tensor_tensor(K["attT"][:, :, bass.ds(b * L, L)], nd[:, :, 0, :], gden[:, :, :], ALU.mult).then_inc(nd_read, 1)

            def t_low(b, g):
                dve.wait_ge(t_hi, NP * b + g + 1)
                cols = slice(g * CP * CH, (g + 1) * CP * CH)
                dve.tensor_tensor(ctxT.lo[:, :, cols], t_bank[g % 2][:, 0:KC * CP * CH].rearrange("p (k n) -> p k n", k=KC),
                                  ctxT.hi[:, :, cols].bitcast(F32), ALU.subtract).then_inc(t_lo, 1)

            def batch(b, first=False, last=False):
                for g in range(NP):
                    if g == 3 and not first:
                        g_copy(b - 1)
                    if g == 5 and not first:
                        kv_copy(b - 1)
                    dve.wait_ge(k_full, NP * b + g + 1)
                    if g >= 2 or not first:
                        dve.wait_ge(phi_done, NP * b + g - 1)
                    dve.tensor_scalar(expk[:, g % 2, :], k_bank[g % 2][0:CH, :], 0.0, None, ALU.min).then_inc(min_done, 1)
                    if g + 2 < NP:
                        t_low(b, g + 2)
                    elif not last:
                        t_low(b + 1, g + 2 - NP)
                    dve.wait_ge(exp_done, NP * b + g + 1)
                    if g >= 2 or not first:
                        dve.wait_ge(phi_lo, NP * b + g - 1)
                    dve.scalar_tensor_tensor(out=phif[:, g % 2, :], in0=k_bank[g % 2][0:CH, :], scalar=0.0,
                                             in1=expk[:, g % 2, :], op0=ALU.max, op1=ALU.add).then_inc(phi_done, 1)
                if not first:
                    nd_use(b - 1)

            t_low(0, 0)
            t_low(0, 1)
            batch(0, first=True)
            with dve.Fori(1, B - 1) as b:
                batch(b)
            batch(B - 1, last=True)
            g_copy(B - 1)
            kv_copy(B - 1)
            nd_use(B - 1)

        @block.tensor
        def _(pe):

            def t_group(b, n, u, g, first=False):
                if g == 0:
                    pe.wait_ge(raw_in[u], 32 * (n + 1))
                if not first:
                    pe.wait_ge(t_lo, NP * b + g - 1)
                for k in range(KC):
                    for h in range(CP):
                        at = (k * CP + h) * CH
                        mm = pe.transpose(t_bank[g % 2][:, at:at + CH], raw[u][:, g * CP + h, k * P:(k + 1) * P],
                                          K["ident"][0:CH, 0:CH])
                mm.then_inc(t_full, 1)

            def k_group(b, g, first):
                pe.wait_ge(t_lo, NP * b + g + 1)
                if g >= 2 or not first:
                    pe.wait_ge(phi_done, NP * b + g - 1)
                for h in range(CP):
                    at = (g * CP + h) * CH
                    mm = matmul_parts(pe, k_bank[g % 2][0:CH, h * D:(h + 1) * D],
                                      [(ctxT.at(slice(None), i, slice(at, at + CH)), wk.at(slice(None), i, slice(None)))
                                       for i in range(KC)])
                mm.then_inc(k_full, 1)

            def g_group(b, g, first):
                pe.wait_ge(phi_lo, NP * b + g + 1)
                pe.wait_ge(rows_lo, NP * b + g + 1)
                if g == 0 and first:
                    pe.wait_ge(ones_set, 2)
                elif g == 0:
                    pe.wait_ge(g_read, KC * b)
                for ch in range(g * CP, (g + 1) * CP):
                    for k in range(KC):
                        mm = matmul_parts(pe, g_bank[k][:, 0:D + 2],
                                          [(phik.at(slice(None), ch, slice(k * P, (k + 1) * P)), rows.at(slice(None), ch, slice(0, D + 2)))],
                                          start=(ch == 0), stop=(ch == NC - 1))
                mm.then_inc(g_part, 1)

            def gt(b):
                pe.wait_ge(g_read, KC * (b + 1))
                for i in range(KC):
                    for k in range(KC):
                        at = (i * KC + k) * P
                        mm = pe.transpose(gt_bank[:, at:at + P], G[:, k, i * P:(i + 1) * P], K["ident"][:, :])
                mm.then_inc(gt_full, 1)

            def kv(b, again):
                pe.wait_ge(gt_read, b + 1)
                if again:
                    pe.wait_ge(nd_read, b)
                for k in range(KC):
                    for i in range(KC):
                        mm = pe.matmul(s_bank[:, k * P:(k + 1) * P], GT[:, i, k * P:(k + 1) * P],
                                       K["T_Wv"][:, i, k * P:(k + 1) * P], start=(i == 0), stop=(i == KC - 1))
                mm.then_inc(kv_full, 1)

            def numden(b):
                pe.wait_ge(kv_read, (1 + KC) * (b + 1))
                for k in range(KC):
                    for w, lhs in enumerate((KV, KS)):
                        mm = pe.matmul(nd[:, k, w, :], lhs[:, k, :], K["phiqT"][:, k, bass.ds(b * L, L)],
                                       start=True, stop=True)
                mm.then_inc(nd_full, 1)

            def batch(b, n, u, first=False, last=False, known=False):
                for g in range(NP):
                    k_group(b, g, first)
                    if g + 2 < NP:
                        t_group(b, 0, u, g + 2)
                    elif not last:
                        t_group(b + 1, n, 1 - u, g + 2 - NP)
                    if g == 5 and not first:
                        numden(b - 1)
                    if g >= 3:
                        g_group(b, g - 3, first)
                    elif not first:
                        g_group(b - 1, g + 3, False)
                    if g == 3 and not first:
                        gt(b - 1)
                    if g == 4 and not first:
                        kv(b - 1, not known)

            t_group(0, 0, 0, 0, first=True)
            t_group(0, 0, 0, 1, first=True)
            batch(0, 0, 0, first=True)
            batch(1, 1, 1, known=True)
            batch(2, 1, 0)
            with pe.Fori(1, B // 2 - 1) as i:
                batch(2 * i + 1, i + 1, 1)
                batch(2 * i + 2, i + 1, 0)
            batch(B - 1, 0, 1, last=True)
            for g in range(3, NP):
                g_group(B - 1, g, False)
            gt(B - 1)
            kv(B - 1, True)
            numden(B - 1)


def experts(nc, a, K):
    with ExitStack() as ctx:
        c = Core(nc, ctx)
        xn = c.sb("e_xn", [TT, NT, D])
        acc = c.sb("e_acc", [TT, NT, D])
        xnT = c.parts("e_xnT", [P, KC, T])
        wr_in_full, wr = c.sb("e_wr_full", [P, KC, E]), c.parts("e_wr", [P, KC, E])
        gu_in, down_in = c.sb("e_gu_in", [P, KC, 2 * I]), c.sb("e_down_in", [P, IC, D])
        wgu = [c.parts(f"e_wgu{u}", [P, KC, 2 * I]) for u in range(2)]
        wd = [c.parts(f"e_wd{u}", [P, IC, D]) for u in range(2)]
        h = c.sb("e_h", [P, 2, TG])
        hT = [c.parts(f"e_hT{u}", [P, IC, TG]) for u in range(2)]
        sil = c.sb("e_sil", [P, 2, TG])
        comb = c.sb("e_comb", [TT, NT, 1 + E])
        pr, key, pick, rest, ranks = (c.sb(f"e_{m}", [TT, NT, E]) for m in ("pr", "key", "pick", "rest", "ranks"))
        irank = c.sb("e_irank", [TT, E], I32)
        mx, tot = c.sb("e_mx", [TT, NT]), c.sb("e_tot", [TT, NT])
        g_bank = [c.ps(f"e_g{i}", [P, 512]) for i in range(2)]
        u_bank = [c.ps(f"e_u{i}", [P, 512]) for i in range(2)]
        d_bank = [c.ps(f"e_d{i}", [P, 512]) for i in range(4)]
        n = norm_buffers(c, "n1")
        w_in, wr_in = c.sem("e_w_in"), c.sem("e_wr_in")
        w_hi, w_done, wr_hi, wr_done = c.sem("e_w_hi"), c.sem("e_w_done"), c.sem("e_wr_hi"), c.sem("e_wr_done")
        h_full, h_hi, h_lo, t_hi = c.sem("e_h_full"), c.sem("e_h_hi"), c.sem("e_h_lo"), c.sem("e_t_hi")
        o_full, o_read, small = c.sem("e_o_full"), c.sem("e_o_read"), c.sem("e_small")
        t_full, t_read, r_full = c.sem("e_t_full"), c.sem("e_t_read"), c.sem("e_r_full")
        exp_go, exp_done, iota_done, rank_done = c.sem("e_exp_go"), c.sem("e_exp"), c.sem("e_iota"), c.sem("e_rank")
        g_full, u_full, sil_done = c.sem("e_g_full"), c.sem("e_u_full"), c.sem("e_sil_done")
        d_full, d_read, zeroed = c.sem("e_d_full"), c.sem("e_d_read"), c.sem("e_zero")
        block = ctx.enter_context(nc.Block())
        W_PARTS = 3
        w_source = lambda n: gu_in[:, n, :] if n < KC else down_in[:, :, :]
        w_target = lambda u, n: wgu[u].at(slice(None), n, slice(None)) if n < KC else wd[u]
        STEPS = NG
        gu_of = lambda e: a["L0_ffn_w_gate_up"][bass.ds(e, 1), :, :].rearrange("e (k p) n -> p (e k) n", p=P)
        wd_of = lambda e: a["L0_ffn_w_down"][bass.ds(e, 1), :, :].rearrange("e (k p) n -> p (e k) n", p=P)

        @block.sync
        def _(sp):
            def load(gu, down):
                sp.dma_start(gu_in[:, :, :], gu).then_inc(w_in, 16)
                sp.dma_start(down_in[:, :, :], down).then_inc(w_in, 16)

            with nc.allow_non_contiguous_dma(reason="router weights, 8 to a row"):
                sp.dma_start(wr_in_full[:, :, :], a["L0_ffn_gate_w"].rearrange("(k p) e -> p k e", p=P)).then_inc(wr_in, 16)
            load(a["L0_ffn_shared_gate_up"].rearrange("(k p) n -> p k n", p=P),
                 a["L0_ffn_shared_down"].rearrange("(k p) n -> p k n", p=P))
            with sp.Fori(1, 1 + E) as m:
                sp.wait_ge(w_done, W_PARTS * m)
                load(gu_of(m - 1), wd_of(m - 1))

        @block.gpsimd
        def _(pool):
            pool.memset(comb[:, :, 0:1], 1.0).then_inc(zeroed, 1)
            pool.memset(acc[:, :, :], 0.0).then_inc(zeroed, 1)
            pool.iota(irank[:, :], [[-1, E]], base=E, channel_multiplier=0).then_inc(iota_done, 1)
            pool.wait_ge(iota_done, 1)
            pool.tensor_copy(ranks[:, :, :], irank[:, :].unsqueeze(1).to_broadcast([TT, NT, E])).then_inc(rank_done, 1)
            norm_pool(pool, n)
            pool.wait_ge(wr_hi, 1)
            pool.tensor_tensor(wr.lo[:, :, :], wr_in_full[:, :, :], wr.hi[:, :, :].bitcast(F32), ALU.subtract).then_inc(wr_done, 1)

            def split(m, u, part):
                pool.wait_ge(w_hi, W_PARTS * m + part + 1)
                to = w_target(u, part)
                pool.tensor_tensor(full(to.lo), w_source(part), full(to.hi).bitcast(F32), ALU.subtract).then_inc(w_done, 1)

            def expert(m, u, last=False):
                for g in range(STEPS):
                    for j in range(IC):
                        k = (m * STEPS + g) * IC + j
                        pool.wait_ge(h_hi, k + 1)
                        pool.tensor_tensor(hT[g % 2].lo[:, j, :], h[:, j % 2, :], hT[g % 2].hi[:, j, :].bitcast(F32),
                                           ALU.subtract).then_inc(h_lo, 1)
                        if g == 1 and j < W_PARTS and not last:
                            split(m + 1, 1 - u, j)

            for part in range(W_PARTS):
                split(0, 0, part)
            expert(0, 0)
            with pool.Fori(0, E // 2 - 1) as i:
                expert(2 * i + 1, 1)
                expert(2 * i + 2, 0)
            expert(E - 1, 1)
            expert(E, 0, last=True)

        @block.scalar
        def _(act):
            def split(m, u, part, known):
                if part == 0:
                    act.wait_ge(w_in, 32 * (m + 1))
                    if not known:
                        act.wait_ge(d_full, NG * (m - 1))
                act.copy(full(w_target(u, part).hi), w_source(part)).then_inc(w_hi, 1)

            act.wait_ge(wr_in, 16)
            act.copy(wr.hi[:, :, :], wr_in_full[:, :, :]).then_inc(wr_hi, 1)
            for part in range(W_PARTS):
                split(0, 0, part, True)
            for g in range(NT // 2):
                act.wait_ge(t_full, g + 1)
                act.copy(xnT.hi[:, :, g * 2 * TT:(g + 1) * 2 * TT],
                         g_bank[g % 2][:, 0:TG].rearrange("p (k n) -> p k n", k=KC)).then_inc(t_hi, 1)
            act.wait_ge(exp_go, 1)
            act.activation(pr[:, :, :], key[:, :, :], ACT.Exp).then_inc(exp_done, 1)

            def silu(m, g, j, known):
                k = (m * STEPS + g) * IC + j
                act.wait_ge(g_full, k + 1)
                if not known or k >= 2:
                    act.wait_ge(h_full, k - 1)
                act.activation(sil[:, j % 2, :], g_bank[j % 2][:, 0:TG], ACT.Silu).then_inc(sil_done, 1)

            def high(m, g, j, known):
                act.wait_ge(h_full, (m * STEPS + g) * IC + j + 1)
                if j == 0 and (not known or m * STEPS + g >= 2):
                    act.wait_ge(d_full, m * STEPS + g - 1)
                act.copy(hT[g % 2].hi[:, j, :], h[:, j % 2, :]).then_inc(h_hi, 1)

            def expert(m, u, known=False, last=False):
                for g in range(STEPS):
                    for j in range(IC):
                        silu(m, g, j, known)
                        if j:
                            high(m, g, j - 1, known)
                        elif g:
                            high(m, g - 1, IC - 1, known)
                        elif not known:
                            high(m - 1, STEPS - 1, IC - 1, False)
                        if g == 1 and j < W_PARTS and not last:
                            split(m + 1, 1 - u, j, known)

            expert(0, 0, known=True)
            with act.Fori(0, E // 2 - 1) as i:
                expert(2 * i + 1, 1)
                expert(2 * i + 2, 0)
            expert(E - 1, 1)
            expert(E, 0, last=True)
            high(E, STEPS - 1, IC - 1, False)

        @block.vector
        def _(dve):
            step = in_order(dve, small)
            for t in range(NT):
                dve.wait_ge(o_full, t + 1)
                dve.scalar_tensor_tensor(out=K["x"][:, t, :], in0=d_bank[t % 4][0:TT, 0:D], scalar=K["gate_tanh"][:, 0:1],
                                         in1=K["x"][:, t, :], op0=ALU.mult, op1=ALU.add).then_inc(o_read, 1)
            dve.wait_ge(o_read, NT)
            norm_vector(dve, n, K["x"], xn)
            for g in range(NT // 2):
                dve.wait_ge(t_hi, g + 1)
                cols = slice(g * 2 * TT, (g + 1) * 2 * TT)
                dve.tensor_tensor(xnT.lo[:, :, cols], g_bank[g % 2][:, 0:TG].rearrange("p (k n) -> p k n", k=KC),
                                  xnT.hi[:, :, cols].bitcast(F32), ALU.subtract).then_inc(t_read, 1)
            dve.wait_ge(r_full, 1)
            logits = d_bank[0][0:TT, 0:NT * E].rearrange("p (t e) -> p t e", e=E)
            wide = lambda v: v.unsqueeze(2).to_broadcast([TT, NT, E])
            step(dve.tensor_reduce(mx[:, :], logits, AX.X, ALU.max))
            dve.tensor_tensor(key[:, :, :], logits, wide(mx[:, :]), ALU.subtract).then_inc(exp_go, 1)
            dve.wait_ge(exp_done, 1)
            step(dve.tensor_reduce(tot[:, :], pr[:, :, :], AX.X, ALU.add))
            step(dve.reciprocal(tot[:, :], tot[:, :]))
            step(dve.tensor_tensor(pr[:, :, :], pr[:, :, :], wide(tot[:, :]), ALU.mult))
            step(dve.tensor_copy(rest[:, :, :], pr[:, :, :]))
            dve.wait_ge(rank_done, 1)
            dve.wait_ge(zeroed, 2)
            chosen = comb[:, :, 1:1 + E]
            for r in range(2):
                step(dve.tensor_reduce(mx[:, :], rest[:, :, :], AX.X, ALU.max))
                step(dve.tensor_tensor(key[:, :, :], rest[:, :, :], wide(mx[:, :]), ALU.is_equal))
                step(dve.tensor_tensor(key[:, :, :], key[:, :, :], ranks[:, :, :], ALU.mult))
                step(dve.tensor_reduce(mx[:, :], key[:, :, :], AX.X, ALU.max))
                step(dve.tensor_tensor(pick[:, :, :], key[:, :, :], wide(mx[:, :]), ALU.is_equal))
                if r == 0:
                    step(dve.tensor_copy(chosen, pick[:, :, :]))
                    step(dve.scalar_tensor_tensor(out=rest[:, :, :].rearrange("p t e -> p (t e)"),
                                                  in0=pick[:, :, :].rearrange("p t e -> p (t e)"), scalar=-2.0,
                                                  in1=rest[:, :, :].rearrange("p t e -> p (t e)"), op0=ALU.mult, op1=ALU.add))
                else:
                    step(dve.tensor_tensor(chosen, chosen, pick[:, :, :], ALU.add))
            step(dve.tensor_tensor(pr[:, :, :], pr[:, :, :], chosen, ALU.mult))
            step(dve.tensor_reduce(tot[:, :], pr[:, :, :], AX.X, ALU.add))
            step(dve.reciprocal(tot[:, :], tot[:, :]))
            step(dve.tensor_tensor(chosen, pr[:, :, :], wide(tot[:, :]), ALU.mult))

            def up(m, g, known):
                for j in range(IC):
                    k = (m * STEPS + g) * IC + j
                    dve.wait_ge(sil_done, k + 1)
                    dve.wait_ge(u_full, k + 1)
                    if not known or k >= 2:
                        dve.wait_ge(h_lo, k - 1)
                    dve.tensor_tensor(h[:, j % 2, :], sil[:, j % 2, :], u_bank[j % 2][:, 0:TG], ALU.mult).then_inc(h_full, 1)

            def down(m, g, known):
                dve.wait_ge(d_full, m * STEPS + g + 1)
                if not known or m * STEPS + g:
                    dve.wait_ge(d_read, 4 * (m * STEPS + g))
                for q in range(4):
                    t = 4 * g + q
                    dve.scalar_tensor_tensor(out=acc[:, t, :], in0=d_bank[q][0:TT, 0:D], scalar=comb[:, t, bass.ds(m, 1)],
                                             in1=acc[:, t, :], op0=ALU.mult, op1=ALU.add).then_inc(d_read, 1)

            def expert(m, known):
                for g in range(STEPS):
                    up(m, g, known)
                    if g:
                        down(m, g - 1, known)
                    elif not known:
                        down(m - 1, STEPS - 1, False)

            def result(g):
                dve.wait_ge(d_read, 4 * (E * STEPS + g + 1))
                of = lambda t: t[:, 4 * g:4 * g + 4, :].rearrange("p t d -> p (t d)")
                dve.scalar_tensor_tensor(out=of(K["x"]), in0=of(acc), scalar=K["gate_tanh"][:, 2:3], in1=of(K["x"]),
                                         op0=ALU.mult, op1=ALU.add)

            expert(0, True)
            with dve.Fori(1, E) as m:
                expert(m, False)
            for g in range(STEPS):
                up(E, g, False)
                if g:
                    down(E, g - 1, False)
                    result(g - 1)
                else:
                    down(E - 1, STEPS - 1, False)
            down(E, STEPS - 1, False)
            result(STEPS - 1)

        @block.tensor
        def _(pe):
            for t in range(NT):
                if t >= 4:
                    pe.wait_ge(o_read, t - 3)
                for i in range(KC):
                    mm = pe.matmul(d_bank[t % 4][0:TT, 0:D], K["attT"][:, i, t * TT:(t + 1) * TT], K["T_Wo"][:, i, :],
                                   start=(i == 0), stop=(i == KC - 1))
                mm.then_inc(o_full, 1)
            for g in range(NT // 2):
                pe.wait_ge(n["xn_done"], 2 * g + 2)
                if g >= 2:
                    pe.wait_ge(t_read, g - 1)
                transpose_tiles(pe, g_bank[g % 2], xn, g, K["ident"]).then_inc(t_full, 1)
            pe.wait_ge(t_read, NT // 2)
            pe.wait_ge(wr_done, 1)
            for t in range(NT):
                mm = matmul_parts(pe, d_bank[0][0:TT, t * E:(t + 1) * E],
                                  [(xnT.at(slice(None), i, slice(t * TT, (t + 1) * TT)), wr.at(slice(None), i, slice(None)))
                                   for i in range(KC)])
            mm.then_inc(r_full, 1)
            pe.wait_ge(exp_go, 1)

            def up(m, g, u, known):
                for j in range(IC):
                    k = (m * STEPS + g) * IC + j
                    if not known or k >= 2:
                        pe.wait_ge(h_full, k - 1)
                    for bank, col, done in ((g_bank, j, g_full), (u_bank, IC + j, u_full)):
                        mm = matmul_parts(pe, bank[j % 2][:, 0:TG],
                                          [(wgu[u].at(slice(None), i, slice(col * P, (col + 1) * P)),
                                            xnT.at(slice(None), i, slice(g * TG, (g + 1) * TG))) for i in range(KC)])
                        mm.then_inc(done, 1)

            def down(m, g, u, known):
                pe.wait_ge(h_lo, IC * (m * STEPS + g + 1))
                if not known or m * STEPS + g:
                    pe.wait_ge(d_read, 4 * (m * STEPS + g))
                for q in range(4):
                    mm = matmul_parts(pe, d_bank[q][0:TT, 0:D],
                                      [(hT[g % 2].at(slice(None), j, slice(q * TT, (q + 1) * TT)), wd[u].at(slice(None), j, slice(None)))
                                       for j in range(IC)])
                mm.then_inc(d_full, 1)

            def expert(m, u, known=False):
                pe.wait_ge(w_done, W_PARTS * (m + 1))
                for g in range(STEPS):
                    up(m, g, u, known)
                    if g:
                        down(m, g - 1, u, known)
                    elif not known:
                        down(m - 1, STEPS - 1, 1 - u, False)

            expert(0, 0, known=True)
            with pe.Fori(0, E // 2) as i:
                expert(2 * i + 1, 1)
                expert(2 * i + 2, 0)
            down(E, STEPS - 1, 0, True)


A_PLAN = [line.split() for line in (
    "S P0 K10 E D P1 K11 P2 K12",
    "S X E P0 V0 P1 P2",
    "S P0 V1 E D P1 V2 P2 V3",
    "S V4 E V5 X P0 P1 +T0 F +T1 P2",
    "S P0 +K00 E D P1 +T2 P2 +T3",
    "S X E P0 +K01 P1 P2",
    "S P0 +T4 P1 +T5 E D P2",
    "S X E P0 +K02 P1 F P2")]
A_AHEAD = [w[1:] for slot in A_PLAN for w in slot if w[0] == "+"]
A_ORDER = A_AHEAD + [w for slot in A_PLAN for w in slot if w[0] in "TKV"]
Q4 = 4
KG = 3
GW = S // KG


def queries(nc, a, K):
    with ExitStack() as ctx:
        c = Core(nc, ctx)
        xn = c.sb("q_xn", [TT, NT, D])
        xnT = c.sb("q_xnT", [P, KC, T])
        am, sc, iv = (c.sb(f"q_{m}", [TT, NT]) for m in ("am", "sc", "iv"))
        t_bank = [c.ps(f"q_t{i}", [P, 512]) for i in range(4)]
        q_bank = [c.ps(f"q_q{i}", [P, 512]) for i in range(4)]
        n = norm_buffers(c, "n2")
        small, t_full, t_read, q_full, q_read = (c.sem(f"q_{m}") for m in ("small", "t_full", "t_read", "q_full", "q_read"))
        bq_scaled, bq_done = c.sb("q_bq_scaled", [P, KC]), c.sem("q_bq_done")
        block = ctx.enter_context(nc.Block())

        @block.gpsimd
        def _(pool):
            norm_pool(pool, n)

        @block.vector
        def _(dve):
            norm_vector(dve, n, K["x"], xn)
            dve.wait_ge(n["xn_done"], NT)
            fake_quant(dve, small, 0, xn[:, :, :], xn, am[:, :], sc[:, :], iv[:, :], NT)

        @block.scalar
        def _(act):
            act.mul(bq_scaled[:, :], K["bq"][:, :], SCALE).then_inc(bq_done, 1)
            act.wait_ge(bq_done, 1)
            for g in range(NT // 2):
                act.wait_ge(t_full, g + 1)
                act.copy(xnT[:, :, g * 2 * TT:(g + 1) * 2 * TT],
                         t_bank[g % 4][:, 0:TG].rearrange("p (k n) -> p k n", k=KC)).then_inc(t_read, 1)
            for q in range(KC * NG):
                k, g = divmod(q, NG)
                act.wait_ge(q_full, q + 1)
                act.activation(K["qT"][:, k, g * TG:(g + 1) * TG], q_bank[q % 4][:, 0:TG], ACT.Identity,
                               bias=bq_scaled[:, k:k + 1], scale=SCALE).then_inc(q_read, 1)

        @block.tensor
        def _(pe):
            for g in range(NT // 2):
                pe.wait_ge(small, quantised(2 * g + 1))
                if g >= 4:
                    pe.wait_ge(t_read, g - 3)
                transpose_tiles(pe, t_bank[g % 4], xn, g, K["ident"]).then_inc(t_full, 1)
            pe.wait_ge(t_read, NT // 2)
            for q in range(KC * NG):
                k, g = divmod(q, NG)
                if q >= 4:
                    pe.wait_ge(q_read, q - 3)
                for i in range(KC):
                    mm = pe.matmul(q_bank[q % 4][:, 0:TG], K["T_wq"][:, i, k * P:(k + 1) * P], xnT[:, i, g * TG:(g + 1) * TG],
                                   start=(i == 0), stop=(i == KC - 1))
                mm.then_inc(q_full, 1)


def softmax_attention(nc, a, K):
    with ExitStack() as ctx:
        c = Core(nc, ctx)
        ctx_sb = c.sb("a_ctx", [CH, NC, D])
        ctxT = c.parts("a_ctxT", [P, KC, S])
        keyT = c.parts("a_keyT", [P, KC, S])
        val = c.sb("a_val", [CH, NC, Q4, 2, 64], F32R)
        wk, wv = K["T_wk"], K["T_wv"]
        qfull = c.sb("a_qfull", [P, KC, HC, L])
        qbd = c.parts("a_qbd", [P, KC, HC, L])
        prob = [c.sb(f"a_prob{u}", [TT, S]) for u in range(2)]
        probT = c.parts("a_probT", [CH, NC, 2 * TT])
        mxs = c.sb("a_mxs", [TT, PAIRS])
        lsum = c.sb("a_lsum", [TT, PAIRS])
        linv = c.sb("a_linv", [TT, PAIRS])
        lsel = c.sb("a_lsel", [TT, 4, 2, HD])
        lT = c.sb("a_lT", [P, L])
        mask64 = c.sb("a_mask64", [P, 4, L])
        half = c.sb("a_half", [P, 3 * 64])
        picked = c.sb("a_picked", [P, 4, L])
        two = c.sb("a_two", [P, 2, L])
        osum = c.sb("a_osum", [P, 2, L])
        two_done = c.sem("a_two_done")
        s_bank = c.ps("a_s", [P, 3, 512])
        a_bank = [c.ps(f"a_a{i}", [P, 512]) for i in range(2)]
        p_bank = [c.ps(f"a_p{i}", [P, 512]) for i in range(2)]
        o_bank = c.ps("a_o", [P, 512])
        ctx_in = c.sem("a_ctx_in")
        q_masked, q_hi, q_made = c.sem("a_q_masked"), c.sem("a_q_hi"), c.sem("a_q_made")
        a_full = [c.sem(f"a_a_full{i}") for i in range(2)]
        a_hi = [c.sem(f"a_a_hi{i}") for i in range(2)]
        a_read = [c.sem(f"a_a_read{i}") for i in range(2)]
        s_full, max_done, exp_done = c.sem("a_s_full"), c.sem("a_max"), c.sem("a_exp")
        p_full = [c.sem(f"a_p_full{i}") for i in range(2)]
        p_hi = [c.sem(f"a_p_hi{i}") for i in range(2)]
        p_read = [c.sem(f"a_p_read{i}") for i in range(2)]
        linv_done, lsel_done = c.sem("a_linv_done"), c.sem("a_lsel_done")
        v_full, pick_done, sum_done = c.sem("a_v_full"), c.sem("a_pick_done"), c.sem("a_sum_done")
        o_full, lt_done, o_done = c.sem("a_o_full"), c.sem("a_lt_done"), c.sem("a_o_done")
        half_zero, masks_set = c.sem("a_half_zero"), c.sem("a_masks_set")
        o_at, l_at, f_at = slice(0, 4 * L), slice(256, 256 + L), slice(320, 320 + L)
        block = ctx.enter_context(nc.Block())
        AN = len(A_ORDER) // 2
        flat = lambda t: t.rearrange("p c d -> p (c d)")

        def load(sp, b):
            v = a["ctx_2048"][bass.ds(b, 1), :, :].rearrange("b (p c) d -> p (b c) d", p=CH)
            sp.dma_start(ctx_sb[0:112, :, :], v[0:112, :, :]).then_inc(ctx_in, 16)
            sp.dma_start(ctx_sb[112:CH, :, :], v[112:CH, :, :]).then_inc(ctx_in, 16)

        @block.sync
        def _(sp):
            load(sp, 0)
            last_t = A_ORDER.index("T5")
            with sp.Fori(0, B - 1) as b:
                sp.wait_ge(a_full[last_t % 2], AN * b + last_t // 2 + 1)
                load(sp, b + 1)

        @block.gpsimd
        def _(pool):
            pool.memset(half[:, :], 0.0).then_inc(half_zero, 1)
            hm = K["headmask"][:, :].rearrange("p (h n) -> p h n", h=HC)
            pool.tensor_tensor(mask64[:, :, :], hm[:, 0:4, :], hm[:, 4:8, :], ALU.add).then_inc(masks_set, 1)
            pool.wait_ge(half_zero, 1)
            pool.tensor_tensor(half[:, 64:128], K["ident"][:, 0:64], K["ident"][:, 64:128], ALU.add).then_inc(masks_set, 1)

            def spread(b, k, known=False):
                mask = K["headmask"][:, :].rearrange("p (h n) -> p h n", h=HC)
                nth = KC * b + k + 1
                q = K["qT"][:, k, bass.ds(b * L, L)]
                pool.tensor_tensor(qfull[:, k, :, :], mask, q.unsqueeze(1).to_broadcast([P, HC, L]), ALU.mult).then_inc(q_masked, 1)
                pool.wait_ge(q_masked, nth)
                if not known:
                    pool.wait_ge(s_full, PAIRS * b - PAIRS + 4 * k + 4)
                pool.tensor_tensor(qbd.hi[:, k, :, :], qfull[:, k, :, :], mask, ALU.mult).then_inc(q_hi, 1)
                pool.wait_ge(q_hi, nth)
                pool.tensor_tensor(qbd.lo[:, k, :, :], qfull[:, k, :, :], qbd.hi[:, k, :, :].bitcast(F32),
                                   ALU.subtract).then_inc(q_made, 1)
                pool.wait_ge(q_made, nth)

            def select(b, k, known=False):
                pool.wait_ge(linv_done, 2 * b + k + 1)
                if not known:
                    pool.wait_ge(o_full, 2 * b + k)
                pool.tensor_tensor(lsel[:, :, :, :], K["pairmask"][:, :].rearrange("p (j h e) -> p j h e", j=4, h=2),
                                   linv[:, 4 * k:4 * k + 4].unsqueeze(2).unsqueeze(3).to_broadcast([TT, 4, 2, HD]),
                                   ALU.mult).then_inc(lsel_done, 1)

            def head_sum(b, q, known):
                nth = 4 * b + q + 1
                pool.wait_ge(pick_done, nth)
                pool.tensor_tensor(two[:, :, :], picked[:, 0:2, :], picked[:, 2:4, :], ALU.add).then_inc(two_done, 1)
                pool.wait_ge(two_done, nth)
                if q % 2 == 0 and (not known or q):
                    pool.wait_ge(o_full, 2 * b + q // 2)
                pool.tensor_tensor(osum[:, q % 2, :], two[:, 0, :], two[:, 1, :], ALU.add).then_inc(sum_done, 1)

            def batch(b, first=False, last=False):
                if not first:
                    select(b - 1, 1)
                    head_sum(b - 1, 2, False)
                    head_sum(b - 1, 3, False)
                if not last:
                    spread(b + 1, 0)
                select(b, 0, first)
                head_sum(b, 0, first)
                head_sum(b, 1, first)
                if not last:
                    spread(b + 1, 1)

            spread(0, 0, known=True)
            spread(0, 1, known=True)
            batch(0, first=True)
            with pool.Fori(1, B - 1) as b:
                batch(b)
            batch(B - 1, last=True)
            select(B - 1, 1)
            head_sum(B - 1, 2, False)
            head_sum(B - 1, 3, False)

        def steps(b, j, first, last):
            out = []
            for w in A_PLAN[j]:
                if w[0] == "+":
                    if not last:
                        out.append((w[1], w[1:], b + 1))
                elif w[0] in "TKVESD":
                    out.append((w[0], w, b))
                elif w[0] == "P" and (j or not first):
                    out.append(("P", w, b if j else b - 1))
                elif w[0] == "X" and (j > 1 or not first):
                    out.append(("X", w, b if j > 1 else b - 1))
                elif w[0] == "F" and (j == 7 or not first):
                    out.append(("F", w, b if j == 7 else b - 1))
            return out

        def p_place(j, f):
            at = 3 * j + f
            return at % 2, at // 2 + 1

        def p_target(t, j, f):
            return t[:, 4 * f:4 * f + 4, (j % 2) * TT:(j % 2 + 1) * TT]

        def p_source(i):
            return p_bank[i][0:CH, 0:TG].rearrange("p (c n) -> p c n", c=4)

        def place(w):
            at = A_ORDER.index(w)
            return at % 2, at // 2 + 1

        def targets(w):
            g = int(w[-1])
            if w[0] == "T":
                return [t[:, :, g * CP * CH:(g + 1) * CP * CH] for t in (ctxT.hi, ctxT.lo)]
            if w[0] == "K":
                return [t[:, int(w[1]), g * GW:(g + 1) * GW] for t in (keyT.hi, keyT.lo)]
            return [val[:, g * CP:(g + 1) * CP, :, part, :] for part in range(2)]

        def source(w):
            bank = a_bank[place(w)[0]]
            if w[0] == "T":
                return bank[:, 0:KC * CP * CH].rearrange("p (k n) -> p k n", k=KC)
            if w[0] == "K":
                return bank[:, 0:GW]
            return bank[0:CH, :].rearrange("p (c q e) -> p c q e", c=CP, q=4)

        @block.scalar
        def _(act):
            def piece(b, w):
                i, nth = place(w)
                act.wait_ge(a_full[i], AN * b + nth)
                if w[0] == "K":
                    k = int(w[1])
                    act.activation(targets(w)[0], source(w), ACT.Identity, bias=K["bk"][:, k:k + 1]).then_inc(a_hi[i], 1)
                else:
                    act.copy(targets(w)[0], source(w)).then_inc(a_hi[i], 1)

            def exp(b, j):
                act.wait_ge(max_done, PAIRS * b + j + 1)
                act.activation(prob[j % 2][:, :].rearrange("p (g n) -> p g n", g=KG), s_bank[0:TT, :, 0:GW], ACT.Exp,
                               bias=mxs[:, j:j + 1], accum_out=lsum[:, j:j + 1]).then_inc(exp_done, 1)

            def p_high(b, j, f):
                i, nth = p_place(j, f)
                act.wait_ge(p_full[i], 12 * b + nth)
                act.copy(p_target(probT.hi, j, f), p_source(i)).then_inc(p_hi[i], 1)

            def sums(b, k):
                act.wait_ge(o_full, 2 * b + k + 1)
                act.copy(lT[:, :], o_bank[:, l_at]).then_inc(lt_done, 1)

            def slot(b, j, first=False, last=False):
                for kind, w, of in steps(b, j, first, last):
                    if kind == "E":
                        exp(b, j)
                        if j in (0, 4) and not first:
                            sums(b - 1, j // 4)
                    elif kind == "P":
                        p_high(of, (j - 1) % PAIRS, int(w[1]))
                    elif kind in "TKV":
                        piece(of, w)

            for w in A_AHEAD:
                piece(0, w)
            for j in range(PAIRS):
                slot(0, j, first=True)
            with act.Fori(1, B - 1) as b:
                for j in range(PAIRS):
                    slot(b, j)
            for j in range(PAIRS):
                slot(B - 1, j, last=True)
            sums(B - 1, 0)
            for f in range(3):
                p_high(B - 1, PAIRS - 1, f)
            sums(B - 1, 1)
            act.wait_ge(o_done, 2 * B)
            act.activation(K["attT"][:, 1, :], K["attT"][:, 1, :], ACT.Identity, bias=K["bv"][:, 1:2])

        @block.vector
        def _(dve):
            def piece(b, w):
                i, nth = place(w)
                hi, lo = targets(w)
                dve.wait_ge(a_hi[i], AN * b + nth)
                if w[0] == "K":
                    k = int(w[1])
                    dve.scalar_tensor_tensor(out=lo, in0=source(w), scalar=K["bk"][:, k:k + 1], in1=hi.bitcast(F32),
                                             op0=ALU.add, op1=ALU.subtract).then_inc(a_read[i], 1)
                else:
                    dve.tensor_tensor(lo, source(w), hi.bitcast(F32), ALU.subtract).then_inc(a_read[i], 1)

            def maximum(b, j):
                dve.wait_ge(s_full, PAIRS * b + j + 1)
                dve.tensor_reduce(mxs[:, j:j + 1], s_bank[0:TT, :, 0:GW], AX.XY, ALU.max, negate=True).then_inc(max_done, 1)

            def p_low(b, j, f):
                i, nth = p_place(j, f)
                dve.wait_ge(p_hi[i], 12 * b + nth)
                dve.tensor_tensor(p_target(probT.lo, j, f), p_source(i), p_target(probT.hi, j, f).bitcast(F32),
                                  ALU.subtract).then_inc(p_read[i], 1)

            def select(b, k):
                dve.wait_ge(exp_done, PAIRS * b + 4 * k + 4)
                dve.reciprocal(linv[:, 4 * k:4 * k + 4], lsum[:, 4 * k:4 * k + 4]).then_inc(linv_done, 1)

            def pick(b, q):
                nth = 4 * b + q + 1
                dve.wait_ge(v_full, nth)
                if not isinstance(b, int) or nth > 1:
                    dve.wait_ge(sum_done, nth - 1)
                dve.tensor_tensor(picked[:, :, :].rearrange("p h n -> p (h n)"), o_bank[:, o_at],
                                  mask64[:, :, :].rearrange("p h n -> p (h n)"), ALU.mult).then_inc(pick_done, 1)

            def outputs(b, k):
                nth = 2 * b + k + 1
                dve.wait_ge(lt_done, nth)
                dve.tensor_tensor(K["attT"][:, k, bass.ds(b * L, L)], o_bank[:, f_at], lT[:, :], ALU.mult).then_inc(o_done, 1)

            def finish(b, j, first):
                if j == 0 and not first:
                    outputs(b - 1, 0)
                    select(b - 1, 1)
                if j == 4:
                    if not first:
                        outputs(b - 1, 1)
                    select(b, 0)
                if j >= 4:
                    pick(b, (j - 4) // 2)
                elif not first:
                    pick(b - 1, (j + 4) // 2)

            def slot(b, j, first=False, last=False):
                for kind, w, of in steps(b, j, first, last):
                    if kind == "S":
                        maximum(b, j)
                    elif kind == "D":
                        finish(b, j, first)
                    elif kind == "P":
                        p_low(of, (j - 1) % PAIRS, int(w[1]))
                    elif kind in "TKV":
                        piece(of, w)
            dve.wait_ge(masks_set, 2)
            for w in A_AHEAD:
                piece(0, w)
            for j in range(PAIRS):
                slot(0, j, first=True)
            with dve.Fori(1, B - 1) as b:
                for j in range(PAIRS):
                    slot(b, j)
            for j in range(PAIRS):
                slot(B - 1, j, last=True)
            outputs(B - 1, 0)
            select(B - 1, 1)
            pick(B - 1, 2)
            for f in range(3):
                p_low(B - 1, PAIRS - 1, f)
            pick(B - 1, 3)
            outputs(B - 1, 1)
            dve.wait_ge(o_done, 2 * B)
            dve.tensor_scalar(K["attT"][:, 0, :], K["attT"][:, 0, :], K["bv"][:, 0:1], None, ALU.add)

        @block.tensor
        def _(pe):
            pe.wait_ge(masks_set, 2)

            def wait_pieces(b, pieces):
                for i in range(2):
                    nth = [place(w)[1] for w in pieces if place(w)[0] == i]
                    if nth:
                        pe.wait_ge(a_read[i], AN * b + max(nth))

            def piece(b, w, known=False):
                i, nth = place(w)
                bank = a_bank[i]
                if not known or nth > 1:
                    pe.wait_ge(a_read[i], AN * b + nth - 1)
                g = int(w[-1])
                if w[0] == "T":
                    if g == 0:
                        pe.wait_ge(ctx_in, 32 * (b + 1))
                    for k in range(KC):
                        for h in range(CP):
                            o = (k * CP + h) * CH
                            mm = pe.transpose(bank[:, o:o + CH], ctx_sb[:, g * CP + h, k * P:(k + 1) * P], K["ident"][0:CH, 0:CH])
                elif w[0] == "K":
                    k = int(w[1])
                    if k == 0:
                        wait_pieces(b, (f"T{2 * g}", f"T{2 * g + 1}"))
                    mm = matmul_parts(pe, bank[:, 0:GW],
                                      [(wk.at(slice(None), i, slice(k * P, (k + 1) * P)),
                                        ctxT.at(slice(None), i, slice(g * GW, (g + 1) * GW))) for i in range(KC)])
                else:
                    for h in range(CP):
                        o = (g * CP + h) * CH
                        mm = matmul_parts(pe, bank[0:CH, h * D:(h + 1) * D],
                                          [(ctxT.at(slice(None), i, slice(o, o + CH)), wv.at(slice(None), i, slice(None)))
                                           for i in range(KC)])
                mm.then_inc(a_full[place(w)[0]], 1)

            def scores(b, j, known):
                k, q = divmod(j, 4)
                if q == 0:
                    pe.wait_ge(q_made, KC * b + k + 1)
                    wait_pieces(b, [f"K{k}{g}" for g in range(KG)])
                if not known or PAIRS * b + j:
                    pe.wait_ge(exp_done, PAIRS * b + j)
                pair = qbd.at(slice(None), k, slice(2 * q, 2 * q + 2), slice(None))
                pair = Parts(pair.hi.rearrange("p h n -> p (h n)"), pair.lo.rearrange("p h n -> p (h n)"))
                for g in range(KG):
                    mm = matmul_parts(pe, s_bank[0:TT, g, 0:GW], [(pair, keyT.at(slice(None), k, slice(g * GW, (g + 1) * GW)))])
                mm.then_inc(s_full, 1)

            def turn(b, j, f, known):
                if f == 0:
                    pe.wait_ge(exp_done, PAIRS * b + j + 1)
                i, nth = p_place(j, f)
                if not known or 12 * b + nth > 1:
                    pe.wait_ge(p_read[i], 12 * b + nth - 1)
                for q in range(4):
                    ch = 4 * f + q
                    mm = pe.transpose(p_bank[i][0:CH, q * TT:(q + 1) * TT], prob[j % 2][:, ch * CH:(ch + 1) * CH],
                                      K["ident"][0:TT, 0:TT])
                mm.then_inc(p_full[i], 1)

            def values(b, q, known):
                for i in range(2):
                    pe.wait_ge(p_read[i], 12 * b + 3 * (q + 1))
                if not known or 4 * b + q:
                    pe.wait_ge(pick_done, 4 * b + q)
                for ch in range(NC):
                    if q == 0 and ch == 0:
                        wait_pieces(b, [f"V{g}" for g in range(4)])
                    if q == 0 and ch in (8, 10):
                        wait_pieces(b, [f"V{ch // 2}"])
                    for p in (probT.lo, probT.hi):
                        mm = pe.matmul(o_bank[:, o_at], val[:, ch, q, :, :].rearrange("p s e -> p (s e)"), p[:, ch, :],
                                       start=(ch == 0 and p is probT.lo), stop=(ch == NC - 1 and p is probT.hi))
                mm.then_inc(v_full, 1)

            def fold(b, k, known):
                pe.wait_ge(sum_done, 4 * b + 2 * k + 2)
                pe.wait_ge(lsel_done, 2 * b + k + 1)
                if not known or 2 * b + k:
                    pe.wait_ge(o_done, 2 * b + k)
                for q in range(2):
                    pe.matmul(o_bank[:, f_at], half[:, 64 * (1 - q):64 * (1 - q) + P], osum[:, q, :], start=(q == 0), stop=(q == 1))
                pe.matmul(o_bank[:, l_at], lsel[:, :, :, :].rearrange("p j h e -> p (j h e)"), K["fold"][:, :],
                          start=True, stop=True).then_inc(o_full, 1)

            def slot(b, j, first=False, last=False):
                for kind, w, of in steps(b, j, first, last):
                    if kind == "S":
                        scores(b, j, first)
                    elif kind == "P":
                        turn(of, (j - 1) % PAIRS, int(w[1]), first)
                    elif kind == "X":
                        values(of, (j - 3) // 2 % 4, first)
                    elif kind == "F":
                        fold(of, 0 if j == 7 else 1, first)
                    elif kind in "TKV":
                        piece(of, w)

            for w in A_AHEAD:
                piece(0, w, True)
            for j in range(PAIRS):
                slot(0, j, first=True)
            with pe.Fori(1, B - 1) as b:
                for j in range(PAIRS):
                    slot(b, j)
            for j in range(PAIRS):
                slot(B - 1, j, last=True)
            for f in range(3):
                turn(B - 1, PAIRS - 1, f, False)
            values(B - 1, 3, False)
            fold(B - 1, 1, False)


def attention_output(nc, a, K):
    with ExitStack() as ctx:
        c = Core(nc, ctx)
        o = c.sb("p_o", [TT, NT, D])
        oT = c.sb("p_oT", [P, KC, T])
        am, sc, iv = (c.sb(f"p_{m}", [TT, NT]) for m in ("am", "sc", "iv"))
        t_bank = [c.ps(f"p_t{i}", [P, 512]) for i in range(4)]
        q_bank = [c.ps(f"p_q{i}", [P, 512]) for i in range(4)]
        gated_bias, bias_gated, bias_added = c.sb("p_gated_bias", [TT, D]), c.sem("p_bias_gated"), c.sem("p_bias_added")
        small, r_full, r_read, t_full, t_read, q_full, q_read = (
            c.sem(f"p_{m}") for m in ("small", "r_full", "r_read", "t_full", "t_read", "q_full", "q_read"))
        block = ctx.enter_context(nc.Block())

        @block.gpsimd
        def _(pool):
            pool.tensor_tensor(gated_bias[:, :], K["bp"][:, :], K["gate_tanh"][:, 1:2].to_broadcast([TT, D]), ALU.mult).then_inc(bias_gated, 1)
            pool.wait_ge(bias_gated, 1)
            pool.tensor_tensor(K["x"][:, :, :], K["x"][:, :, :], gated_bias[:, :].unsqueeze(1).to_broadcast([TT, NT, D]),
                               ALU.add).then_inc(bias_added, 1)

        @block.scalar
        def _(act):
            for t in range(NT):
                act.wait_ge(r_full, t + 1)
                act.copy(o[:, t, :], q_bank[t % 4][0:TT, 0:D]).then_inc(r_read, 1)
            for g in range(NT // 2):
                act.wait_ge(t_full, g + 1)
                act.copy(oT[:, :, g * 2 * TT:(g + 1) * 2 * TT],
                         t_bank[g % 4][:, 0:TG].rearrange("p (k n) -> p k n", k=KC)).then_inc(t_read, 1)

        @block.vector
        def _(dve):
            dve.wait_ge(r_read, NT)
            fake_quant(dve, small, 0, o[:, :, :], o, am[:, :], sc[:, :], iv[:, :], NT)
            dve.wait_ge(bias_added, 1)
            for t in range(NT):
                dve.wait_ge(q_full, t + 1)
                dve.scalar_tensor_tensor(out=K["x"][:, t, :], in0=q_bank[t % 4][0:TT, 0:D], scalar=K["gate_tanh"][:, 1:2],
                                         in1=K["x"][:, t, :], op0=ALU.mult, op1=ALU.add).then_inc(q_read, 1)

        @block.tensor
        def _(pe):
            for t in range(NT):
                if t >= 4:
                    pe.wait_ge(r_read, t - 3)
                for k in range(KC):
                    mm = pe.transpose(q_bank[t % 4][0:TT, k * P:(k + 1) * P], K["attT"][:, k, t * TT:(t + 1) * TT], K["ident"][:, :])
                mm.then_inc(r_full, 1)
            for g in range(NT // 2):
                pe.wait_ge(small, quantised(2 * g + 1))
                if g >= 4:
                    pe.wait_ge(t_read, g - 3)
                transpose_tiles(pe, t_bank[g % 4], o, g, K["ident"]).then_inc(t_full, 1)
            for t in range(NT):
                pe.wait_ge(t_read, t // 2 + 1)
                if t < 4:
                    pe.wait_ge(r_read, NT)
                else:
                    pe.wait_ge(q_read, t - 3)
                for i in range(KC):
                    mm = pe.matmul(q_bank[t % 4][0:TT, 0:D], oT[:, i, t * TT:(t + 1) * TT], K["T_wp"][:, i, :],
                                   start=(i == 0), stop=(i == KC - 1))
                mm.then_inc(q_full, 1)


def dequantise(nc, a, K):
    with ExitStack() as ctx:
        c = Core(nc, ctx)
        pk = [c.sb(f"w_pk{u}", [P, 8 * P], I32) for u in range(2)]
        scl = [c.sb(f"w_scl{u}", [P, 64]) for u in range(2)]
        nib = [c.sb(f"w_nib{u}", [P, 8 * P, 2], I32) for u in range(2)]
        mag = c.sb("w_mag", [P, 8 * P, 2], I32)
        v0, v1 = ([c.sb(f"w_{m}{u}", [P, 8 * P, 2]) for u in range(2)] for m in ("v0", "v1"))
        turning = c.sb("w_turning", [P, 1])
        banks = [c.ps(f"w_b{i}", [P, 512]) for i in range(8)]
        w_in = [c.sem(f"w_in{u}") for u in range(2)]
        turning_set, signed, factor, scaled = (c.sem(f"w_{m}") for m in ("turning_set", "signed", "factor", "scaled"))
        small, turned, hi_done, emptied = c.sem("w_small"), c.sem("w_turned"), c.sem("w_hi_done"), c.sem("w_emptied")
        jobs = []
        for name, dst in (("gate", "WgT"), ("up", "WuT")):
            for h in range(2):
                wv = a[f"L1_ffn_{name}_W_packed"].rearrange("(m p) k -> p m k", p=P)[:, 8 * h:8 * h + 8, :]
                sv = a[f"L1_ffn_{name}_scales"].rearrange("(m p) k -> p m k", p=P)[:, 8 * h:8 * h + 8, :]
                jobs.append((dst, h, wv, sv, 8))
        for h in range(2):
            wv = a["L1_ffn_down_W_packed"][h * P:(h + 1) * P, :].unsqueeze(1)
            sv = a["L1_ffn_down_scales"][h * P:(h + 1) * P, :].unsqueeze(1)
            jobs.append(("WdT", h, wv, sv, 1))
        NS = 6
        block = ctx.enter_context(nc.Block())

        def target(n, f):
            dst, h, _, _, m = jobs[n]
            bank, to = banks[(4 * n + f) % 8], K[dst]
            if m == 8:
                at = slice((8 * h + 2 * f) * P, (8 * h + 2 * f + 2) * P)
                return to.hi[:, :, at], to.lo[:, :, at], bank[:, :].rearrange("p (k n) -> p k n", k=KC)
            at = slice(h * P, (h + 1) * P)
            return to.hi[:, 4 * f:4 * f + 4, at], to.lo[:, 4 * f:4 * f + 4, at], bank[:, :].rearrange("p (m n) -> p m n", m=4)

        @block.sync
        def _(sp):
            for n, (_, _, wv, sv, m) in enumerate(jobs):
                if n >= 2:
                    sp.wait_ge(scaled, n - 1)
                with nc.allow_non_contiguous_dma(reason="block scales, 8 to a row"):
                    sp.dma_start(pk[n % 2][:, :].rearrange("p (m k) -> p m k", m=m), wv).then_inc(w_in[n % 2], 16)
                    sp.dma_start(scl[n % 2][:, :].rearrange("p (m k) -> p m k", m=m), sv).then_inc(w_in[n % 2], 16)

        @block.vector
        def _(dve):
            step = in_order(dve, small)
            flat = lambda t: t[:, :, :].rearrange("p k e -> p (k e)")

            def low(n):
                for f in range(4):
                    dve.wait_ge(hi_done, 4 * n + f + 1)
                    hi, lo, bank = target(n, f)
                    dve.tensor_tensor(lo, bank, hi.bitcast(F32), ALU.subtract).then_inc(emptied, 1)

            for n in range(len(jobs)):
                u = n % 2
                dve.wait_ge(w_in[u], 32 * (n // 2 + 1))
                if n >= 2:
                    dve.wait_ge(turned, 4 * (n - 1))
                step(dve.tensor_scalar(nib[u][:, :, 0], pk[u][:, :], 15, None, ALU.bitwise_and))
                step(dve.tensor_scalar(nib[u][:, :, 1], pk[u][:, :], 4, 15, ALU.logical_shift_right, ALU.bitwise_and))
                step(dve.tensor_scalar(flat(mag), flat(nib[u]), 7, None, ALU.bitwise_and))
                step(dve.tensor_scalar(flat(v0[u]), flat(mag), 2.0, -8.0, ALU.mult, ALU.add))
                step(dve.scalar_tensor_tensor(out=flat(v0[u]), in0=flat(mag), scalar=-2.0, in1=flat(v0[u]), op0=ALU.add, op1=ALU.max))
                step(dve.scalar_tensor_tensor(out=flat(v0[u]), in0=flat(mag), scalar=0.5, in1=flat(v0[u]), op0=ALU.mult, op1=ALU.max))
                if n:
                    low(n - 1)
            low(len(jobs) - 1)

        @block.gpsimd
        def _(pool):
            flat = lambda t: t[:, :, :].rearrange("p k e -> p (k e)")
            pool.memset(turning[:, :], 7.5).then_inc(turning_set, 1)
            for n in range(len(jobs)):
                u = n % 2
                pool.wait_ge(signed, n + 1)
                pool.tensor_tensor(flat(v1[u]).rearrange("p (s k) -> p s k", k=BLK), flat(v1[u]).rearrange("p (s k) -> p s k", k=BLK),
                                   scl[u][:, :].unsqueeze(2).to_broadcast([P, 64, BLK]), ALU.mult).then_inc(factor, 1)
                pool.wait_ge(factor, n + 1)
                pool.wait_ge(small, NS * (n + 1))
                pool.tensor_tensor(flat(v0[u]), flat(v0[u]), flat(v1[u]), ALU.mult).then_inc(scaled, 1)

        @block.scalar
        def _(act):
            def sign(n):
                u = n % 2
                act.wait_ge(small, NS * n + 2)
                if n >= 2:
                    act.wait_ge(scaled, n - 1)
                act.activation(v1[u][:, :, :], nib[u][:, :, :], ACT.Sign, scale=-1.0, bias=turning[:, :]).then_inc(signed, 1)

            act.wait_ge(turning_set, 1)
            sign(0)
            for n in range(len(jobs)):
                if n + 1 < len(jobs):
                    sign(n + 1)
                for f in range(4):
                    act.wait_ge(turned, 4 * n + f + 1)
                    hi, _, bank = target(n, f)
                    act.copy(hi, bank).then_inc(hi_done, 1)

        @block.tensor
        def _(pe):
            flat = lambda t: t[:, :, :].rearrange("p k e -> p (k e)")
            for n, (dst, h, _, _, m) in enumerate(jobs):
                pe.wait_ge(scaled, n + 1)
                for f in range(4):
                    if 4 * n + f >= 8:
                        pe.wait_ge(emptied, 4 * n + f - 7)
                    bank = banks[(4 * n + f) % 8]
                    for q in range(4):
                        if m == 8:
                            k, r = divmod(q, 2)
                            src = flat(v0[n % 2])[:, (2 * f + r) * D + k * P:(2 * f + r) * D + (k + 1) * P]
                        else:
                            src = flat(v0[n % 2])[:, (4 * f + q) * P:(4 * f + q + 1) * P]
                        mm = pe.transpose(bank[:, q * P:(q + 1) * P], src, K["ident"][:, :])
                    mm.then_inc(turned, 1)


def feed_forward(nc, a, out, K):
    with ExitStack() as ctx:
        c = Core(nc, ctx)
        xn = c.sb("f_xn", [TT, NT, D])
        xnT = c.parts("f_xnT", [P, KC, T])
        sq, tn, h1, h = (c.sb(f"f_{m}", [P, 2, TG]) for m in ("sq", "tn", "h1", "h"))
        hT = [c.parts(f"f_hT{u}", [P, TG]) for u in range(2)]
        g_bank = [c.ps(f"f_g{i}", [P, 512]) for i in range(2)]
        u_bank = [c.ps(f"f_u{i}", [P, 512]) for i in range(2)]
        d_bank = [c.ps(f"f_d{i}", [P, 512]) for i in range(4)]
        n = norm_buffers(c, "n3")
        t_full, t_hi, t_read, g_full, u_full = (c.sem(f"f_{m}") for m in ("t_full", "t_hi", "t_read", "g_full", "u_full"))
        sq_done, inner_done, tanh_done, gelu_done, h_full, h_hi, h_lo = (
            c.sem(f"f_{m}") for m in ("sq_done", "inner_done", "tanh_done", "gelu_done", "h_full", "h_hi", "h_lo"))
        d_full, x_done, stored = c.sem("f_d_full"), c.sem("f_x_done"), c.sem("f_stored")
        block = ctx.enter_context(nc.Block())

        @block.gpsimd
        def _(pool):
            norm_pool(pool, n)

            def low(s, u):
                pool.wait_ge(h_hi, s + 1)
                pool.tensor_tensor(hT[u].lo[:, :], h[:, u, :], hT[u].hi[:, :].bitcast(F32), ALU.subtract).then_inc(h_lo, 1)

            with pool.Fori(0, NG) as g:
                for m in range(MC):
                    low(MC * g + m, m % 2)

        @block.scalar
        def _(act):
            for g in range(NT // 2):
                act.wait_ge(t_full, g + 1)
                act.copy(xnT.hi[:, :, g * 2 * TT:(g + 1) * 2 * TT],
                         g_bank[g % 2][:, 0:TG].rearrange("p (k n) -> p k n", k=KC)).then_inc(t_hi, 1)

            def square(s, u, first):
                act.wait_ge(g_full, s + 1)
                if not first:
                    act.wait_ge(tanh_done, s - 1)
                act.activation(sq[:, u, :], g_bank[u][:, 0:TG], ACT.Square, scale=0.044715 ** 0.5).then_inc(sq_done, 1)

            def tanh(s, u, first):
                act.wait_ge(inner_done, s + 1)
                if not first:
                    act.wait_ge(gelu_done, s - 1)
                act.activation(tn[:, u, :], sq[:, u, :], ACT.Tanh, scale=0.7978845608028654).then_inc(tanh_done, 1)

            def high(s, u, first):
                act.wait_ge(h_full, s + 1)
                if not first:
                    act.wait_ge(d_full, s - 1)
                act.copy(hT[u].hi[:, :], h[:, u, :]).then_inc(h_hi, 1)

            def group(g, first):
                for m in range(MC):
                    s, early = MC * g + m, first and m < 2
                    square(s, m % 2, early)
                    if m or not first:
                        high(s - 1, 1 - m % 2, first and m < 3)
                    tanh(s, m % 2, early)

            group(0, True)
            with act.Fori(1, NG) as g:
                group(g, False)
            high(NG * MC - 1, 1, False)

        @block.vector
        def _(dve):
            norm_vector(dve, n, K["x"], xn)
            for g in range(NT // 2):
                dve.wait_ge(t_hi, g + 1)
                cols = slice(g * 2 * TT, (g + 1) * 2 * TT)
                dve.tensor_tensor(xnT.lo[:, :, cols], g_bank[g % 2][:, 0:TG].rearrange("p (k n) -> p k n", k=KC),
                                  xnT.hi[:, :, cols].bitcast(F32), ALU.subtract).then_inc(t_read, 1)

            def inner(s, u):
                dve.wait_ge(sq_done, s + 1)
                dve.scalar_tensor_tensor(out=sq[:, u, :], in0=sq[:, u, :], scalar=1.0, in1=g_bank[u][:, 0:TG],
                                         op0=ALU.add, op1=ALU.mult).then_inc(inner_done, 1)

            def product(s, u, first):
                dve.wait_ge(tanh_done, s + 1)
                dve.scalar_tensor_tensor(out=h1[:, u, :], in0=tn[:, u, :], scalar=1.0, in1=g_bank[u][:, 0:TG],
                                         op0=ALU.add, op1=ALU.mult).then_inc(gelu_done, 1)
                dve.wait_ge(gelu_done, s + 1)
                dve.wait_ge(u_full, s + 1)
                if not first:
                    dve.wait_ge(h_lo, s - 1)
                dve.scalar_tensor_tensor(out=h[:, u, :], in0=h1[:, u, :], scalar=0.5, in1=u_bank[u][:, 0:TG],
                                         op0=ALU.mult, op1=ALU.mult).then_inc(h_full, 1)

            def result(g):
                dve.wait_ge(d_full, MC * (g + 1))
                for q in range(4):
                    xq = K["x"][:, bass.ds(4 * g + q, 1), :].rearrange("p t d -> p (t d)")
                    dve.scalar_tensor_tensor(out=xq, in0=d_bank[q][0:TT, 0:D], scalar=K["gate_tanh"][:, 3:4],
                                             in1=xq, op0=ALU.mult, op1=ALU.add).then_inc(x_done, 1)

            def group(g, first):
                for m in range(MC):
                    s = MC * g + m
                    inner(s, m % 2)
                    product(s, m % 2, first and m < 2)
                    if m == 1 and not first:
                        result(g - 1)

            group(0, True)
            with dve.Fori(1, NG) as g:
                group(g, False)
            result(NG - 1)

        @block.tensor
        def _(pe):
            for g in range(NT // 2):
                pe.wait_ge(n["xn_done"], 2 * g + 2)
                if g >= 2:
                    pe.wait_ge(t_read, g - 1)
                transpose_tiles(pe, g_bank[g % 2], xn, g, K["ident"]).then_inc(t_full, 1)
            pe.wait_ge(t_read, NT // 2)

            def up(g, m, first):
                if not first or m >= 2:
                    pe.wait_ge(h_full, MC * g + m - 1)
                for bank, w, done in ((g_bank, "WgT", g_full), (u_bank, "WuT", u_full)):
                    mm = matmul_parts(pe, bank[m % 2][:, 0:TG],
                                      [(K[w].at(slice(None), i, slice(m * P, (m + 1) * P)),
                                        xnT.at(slice(None), i, bass.ds(g * TG, TG))) for i in range(KC)])
                    mm.then_inc(done, 1)

            def down(g, m, first):
                pe.wait_ge(h_lo, MC * g + m + 1)
                if m == 0 and not first:
                    pe.wait_ge(x_done, 4 * g)
                for q in range(4):
                    mm = matmul_parts(pe, d_bank[q][0:TT, 0:D],
                                      [(hT[m % 2].at(slice(None), slice(q * TT, (q + 1) * TT)), K["WdT"].at(slice(None), m, slice(None)))],
                                      start=(m == 0), stop=(m == MC - 1))
                mm.then_inc(d_full, 1)

            def group(g, first):
                for m in range(MC):
                    up(g, m, first)
                    if m > 1:
                        down(g, m - 2, first)
                    elif not first:
                        down(g - 1, MC + m - 2, False)

            group(0, True)
            with pe.Fori(1, NG) as g:
                group(g, False)
            down(NG - 1, MC - 2, False)
            down(NG - 1, MC - 1, False)

        @block.sync
        def _(sp):
            y = out.rearrange("b l d -> (b l) d").rearrange("(t p) d -> p t d", p=TT)
            for g in range(NG):
                sp.wait_ge(x_done, 4 * (g + 1))
                sp.dma_start(y[:, 4 * g:4 * g + 4, :], K["x"][:, 4 * g:4 * g + 4, :]).then_inc(stored, 16)
            sp.wait_ge(stored, 16 * NG)


def build(nc, a, out):
    with ExitStack() as ctx:
        c = Core(nc, ctx)
        K = {
            "x": c.sb("x", [TT, NT, D]), "attT": c.sb("attT", [P, KC, T]),
            "ident": c.sb("ident", [P, P]), "headmask": c.sb("headmask", [P, TG]), "blockmask": c.sb("blockmask", [P, P]),
            "pairmask": c.sb("pairmask", [TT, P]), "fold": c.sb("fold", [TT, L]),
            "gates": c.sb("gates", [TT, 5]), "gate_tanh": c.sb("gate_tanh", [TT, 4]), "bp": c.sb("bp", [TT, D]),
        }
        for m in ("bg", "bq", "bk", "bv"):
            K[m] = c.sb(m, [P, KC])
        def weights(scope, names, split=()):
            held = Core(nc, scope)
            for m in names:
                K["T_" + m] = held.parts("T_" + m, [P, KC, D]) if m in split else held.sb("T_" + m, [P, KC, D])

        weights(ctx, ("wp",))
        with ExitStack() as until_attention:
            weights(until_attention, ("wq", "wk", "wv"), split=("wk", "wv"))
            with ExitStack() as scope:
                weights(scope, ("Wo",))
                with ExitStack() as inner:
                    weights(inner, ("Wq", "Wg", "Wk", "Wv"), split=("Wk",))
                    K["phiqT"] = inner.enter_context(nc.sbuf_tensor("phiqT", [P, KC, T], F32))
                    K["gateT"] = inner.enter_context(nc.sbuf_tensor("gateT", [P, KC, T], F32))
                    setup(nc, a, K)
                    linear_attention(nc, a, K)
                experts(nc, a, K)
            K["qT"] = until_attention.enter_context(nc.sbuf_tensor("qT", [P, KC, T], F32))
            queries(nc, a, K)
            softmax_attention(nc, a, K)
        attention_output(nc, a, K)
        with ExitStack() as scope:
            weights = Core(nc, scope)
            K["WgT"], K["WuT"] = weights.parts("WgT", [P, KC, M]), weights.parts("WuT", [P, KC, M])
            K["WdT"] = weights.parts("WdT", [P, MC, D])
            dequantise(nc, a, K)
            feed_forward(nc, a, out, K)


_INS = ["x", "ctx_2048", "g_xattn", "g_ffn", "L0_xattn_Wq", "L0_xattn_Wg", "L0_xattn_bg", "L0_xattn_Wkv", "L0_xattn_Wo",
        "L0_ffn_gate_w", "L0_ffn_w_gate_up", "L0_ffn_w_down", "L0_ffn_shared_gate_up", "L0_ffn_shared_down",
        "L1_xattn_wq", "L1_xattn_bq", "L1_xattn_wkv", "L1_xattn_bkv", "L1_xattn_wp", "L1_xattn_bp",
        "L1_ffn_gate_W_packed", "L1_ffn_gate_scales", "L1_ffn_up_W_packed", "L1_ffn_up_scales",
        "L1_ffn_down_W_packed", "L1_ffn_down_scales"]


def kernel(**inputs):
    import concourse.bacc as bacc
    from concourse.bass_utils import run_bass_kernel_spmd

    nc = bacc.Bacc("TRN2", target_bir_lowering=False, num_devices=1)
    arrays, a = {}, {}
    for name in _INS:
        v = np.ascontiguousarray(inputs[name])
        arrays[f"in_{name}"] = v
        a[name] = nc.dram_tensor(f"in_{name}", v.shape, mybir.dt.from_np(v.dtype), kind="ExternalInput").ap()
    out = nc.dram_tensor("out", (B, L, D), F32, kind="ExternalOutput").ap()
    build(nc, a, out)
    r = run_bass_kernel_spmd(nc, [arrays], core_ids=[0])
    return r.results[0]["out"]
```
